# Optimizing a Trainium2 kernel written in Bass

```python
import numpy as np
import jax
import jax.numpy as jnp

def _softmax(x, axis=-1):
    return jax.nn.softmax(x, axis=axis)

def _gelu(x):
    return jax.nn.gelu(x, approximate=True)

def _silu(x):
    return jax.nn.silu(x)

def _sigmoid(x):
    return jax.nn.sigmoid(x)

def _layernorm(x, axis=-1, eps=1e-05):
    m = jnp.mean(x, axis=axis, keepdims=True)
    v = jnp.var(x, axis=axis, keepdims=True)
    return (x - m) / jnp.sqrt(v + eps)

def _scatter_add(tgt, idx, src, axis=0):
    return tgt.at[idx].add(src)

def _segment_sum(src, seg, n):
    return jax.ops.segment_sum(src, seg, n)
kernel_name = 'mk_decoder_preln_d2_seqx_r8_3f4345'

def setup_inputs(seed: int=0):
    np.random.seed(seed)
    _w = jnp.asarray

    def _rec_inputs():
        import jax
        import jax.numpy as jnp
        _rk = jax.random.key(seed)
        x = 7.22e-05 + 1 * jax.random.normal(jax.random.fold_in(_rk, 1), (8, 256, 128), jnp.float32)
        _lenS = 256 - jax.random.randint(jax.random.fold_in(_rk, 7), (8,), 0, max(1, 256 // 4) + 1, jnp.int32)
        _lenS2 = 256 - jax.random.randint(jax.random.fold_in(_rk, 8), (8,), 0, max(1, 256 // 4) + 1, jnp.int32)
        _ctx_1024P = jax.random.normal(jax.random.fold_in(_rk, 11), (8, 16, 128), jnp.float32)
        _ctx_1024c = jax.random.dirichlet(jax.random.fold_in(_rk, 511), 0.3 * jnp.ones((16,), jnp.float32), (8, 256))
        _ctx_1024t = jnp.einsum('bsk,bkd->bsd', _ctx_1024c, _ctx_1024P)
        _ctx_1024t = _ctx_1024t * jax.lax.rsqrt(jnp.mean(jnp.square(_ctx_1024t)) + 1e-12) * 0.953939
        ctx_1024 = 4.13588e-05 + 0.999923 * (_ctx_1024t + 0.3 * jax.random.normal(jax.random.fold_in(_rk, 611), (8, 256, 128), jnp.float32))
        fside_BxSxS2_0 = jax.random.uniform(jax.random.fold_in(_rk, 12), (8, 256, 256), jnp.float32, 0.0, 10)
        return (x, ctx_1024, fside_BxSxS2_0)
    x, ctx_1024, fside_BxSxS2_0 = _rec_inputs()

    def _L0_attn_setup():
        import jax, jax.numpy as jnp
        from jax import lax
        import numpy as np

        def log_g(x):
            return jnp.where(x >= 0, jnp.log(jnp.maximum(x, 0) + 0.5), -jax.nn.softplus(-x))
        key = jax.random.key(seed)
        k1, k2, k3, k4 = jax.random.split(key, 4)
        B, T, D, E = (8, 256, 128, 256)
        x = jax.random.normal(k1, (B, T, D), dtype=jnp.float32)
        W = jax.random.normal(k2, (3 * E, D), dtype=jnp.float32) * (1.0 / np.sqrt(D))
        b = jax.random.normal(k3, (3 * E,), dtype=jnp.float32) * 0.02
        Wd = jax.random.normal(k4, (D, E), dtype=jnp.float32) * (1.0 / np.sqrt(E))
        return {'x': x, 'W': W, 'b': b, 'Wd': Wd}
    _L0_attn_all = _L0_attn_setup()
    _L0_attn_in = {k: v for k, v in _L0_attn_all.items() if k in ('W', 'b', 'Wd')}
    del _L0_attn_all

    def _L0_xattn_setup():
        import jax, jax.numpy as jnp
        import numpy as np
        EMBED_DIM = 128
        NUM_HEADS = 16
        HEAD_DIM = EMBED_DIM // NUM_HEADS
        B, SQ, SK = (4, 256, 256)

        def _xavier(key, shape):
            fan_in, fan_out = (shape[1], shape[0])
            limit = float(np.sqrt(6.0 / (fan_in + fan_out)))
            return jax.random.uniform(key, shape, jnp.float32, -limit, limit)
        key = jax.random.key(seed)
        ks = jax.random.split(key, 9)
        return {'query': jax.random.normal(ks[0], (B, SQ, EMBED_DIM), jnp.float32), 'key_': jax.random.normal(ks[1], (B, SK, EMBED_DIM), jnp.float32), 'value': jax.random.normal(ks[2], (B, SK, EMBED_DIM), jnp.float32), 'distances': jax.random.uniform(ks[3], (B, SQ, SK), jnp.float32, 0.01, 10.0), 'Wq': _xavier(ks[4], (EMBED_DIM, EMBED_DIM)), 'bq': jnp.zeros((EMBED_DIM,), jnp.float32), 'Wk': _xavier(ks[5], (EMBED_DIM, EMBED_DIM)), 'bk': jnp.zeros((EMBED_DIM,), jnp.float32), 'Wv': _xavier(ks[6], (EMBED_DIM, EMBED_DIM)), 'bv': jnp.zeros((EMBED_DIM,), jnp.float32), 'Wo': _xavier(ks[7], (EMBED_DIM, EMBED_DIM)), 'bo': jnp.zeros((EMBED_DIM,), jnp.float32), 'distance_scaling': jnp.asarray(1.0, jnp.float32)}
    _L0_xattn_all = _L0_xattn_setup()
    _L0_xattn_in = {k: v for k, v in _L0_xattn_all.items() if k in ('Wq', 'bq', 'Wk', 'bk', 'Wv', 'bv', 'Wo', 'bo', 'distance_scaling')}
    del _L0_xattn_all

    def _L0_ffn_setup():
        import jax, jax.numpy as jnp
        import numpy as np
        NUM_EXPERTS = 8
        TOP_K = 2
        CAP_RATIO = 1.25
        INIT_STD = 0.02
        key = jax.random.key(seed)
        k1, k2, k3, k4 = jax.random.split(key, 4)
        B, T, H, F = (4, 256, 128, 512)
        x = jax.random.normal(k1, (B, T, H), jnp.float32)
        router_w = jax.random.normal(k2, (NUM_EXPERTS, H), jnp.float32) * INIT_STD
        w1 = jax.random.normal(k3, (NUM_EXPERTS, H, F), jnp.float32) * INIT_STD
        w2 = jax.random.normal(k4, (NUM_EXPERTS, F, H), jnp.float32) * INIT_STD
        return {'x': x, 'router_w': router_w, 'w1': w1, 'w2': w2}
    _L0_ffn_all = _L0_ffn_setup()
    _L0_ffn_in = {k: v for k, v in _L0_ffn_all.items() if k in ('router_w', 'w1', 'w2')}
    del _L0_ffn_all

    def _L1_attn_setup():
        import jax, jax.numpy as jnp
        import numpy as np
        D_MODEL = 128
        N_HEADS = 16
        D_HEAD = D_MODEL // N_HEADS
        SCALE = 1.0 / np.sqrt(D_HEAD).astype(np.float32)

        def _feature_map(x):
            return jax.nn.elu(x) + 1.0
        key = jax.random.key(seed)
        ks = jax.random.split(key, 7)
        b, s = (4, 256)
        w = 1.0 / np.sqrt(D_MODEL).astype(np.float32)
        return {'x': jax.random.normal(ks[0], (b, s, D_MODEL), dtype=jnp.float32), 'Wq': jax.random.normal(ks[1], (D_MODEL, D_MODEL), dtype=jnp.float32) * w, 'Wk': jax.random.normal(ks[2], (D_MODEL, D_MODEL), dtype=jnp.float32) * w, 'Wv': jax.random.normal(ks[3], (D_MODEL, D_MODEL), dtype=jnp.float32) * w, 'Wo': jax.random.normal(ks[4], (D_MODEL, D_MODEL), dtype=jnp.float32) * w, 'Wg': jax.random.normal(ks[5], (N_HEADS, D_MODEL), dtype=jnp.float32) * w, 'bg': jax.random.normal(ks[6], (N_HEADS,), dtype=jnp.float32) * 0.02}
    _L1_attn_all = _L1_attn_setup()
    _L1_attn_in = {k: v for k, v in _L1_attn_all.items() if k in ('Wq', 'Wk', 'Wv', 'Wo', 'Wg', 'bg')}
    del _L1_attn_all

    def _L1_xattn_setup():
        import jax, jax.numpy as jnp
        import numpy as np
        EPS_BACKEND = 1e-06
        NORM_EPS = 1e-06
        NUM_HEADS = 4

        def _mlstm_forward(q, k, v, ig_kernel, ig_bias, fg_kernel, fg_bias, outnorm_weight):
            B, S, E = q.shape
            NH = ig_bias.shape[0]
            DH = E // NH
            gate_input = jnp.concatenate([q, k, v], axis=-1)
            igate = gate_input @ ig_kernel + ig_bias
            fgate = gate_input @ fg_kernel + fg_bias
            qh = q.reshape(B, S, NH, DH).transpose(0, 2, 1, 3)
            kh = k.reshape(B, S, NH, DH).transpose(0, 2, 1, 3)
            vh = v.reshape(B, S, NH, DH).transpose(0, 2, 1, 3)
            ig = igate.transpose(0, 2, 1)
            fg = fgate.transpose(0, 2, 1)
            log_fg = jax.nn.log_sigmoid(fg)
            cums = jnp.concatenate([jnp.zeros((B, NH, 1), log_fg.dtype), jnp.cumsum(log_fg, axis=-1)], axis=-1)
            fg_mat = cums[..., :, None] - cums[..., None, :]
            mask = jnp.tril(jnp.ones((S + 1, S + 1), bool))
            fg_mat = jnp.where(mask, fg_mat, -jnp.inf)[..., 1:, 1:]
            log_D = fg_mat + ig[..., None, :]
            max_log_D = jnp.max(log_D, axis=-1, keepdims=True)
            D = jnp.exp(log_D - max_log_D)
            qk = jnp.einsum('bnsd,bntd->bnst', qh, kh) / jnp.sqrt(jnp.float32(DH))
            C = qk * D
            normalizer = jnp.maximum(jnp.abs(C.sum(-1, keepdims=True)), jnp.exp(-max_log_D))
            h = jnp.einsum('bnst,bntd->bnsd', C / (normalizer + EPS_BACKEND), vh)
            h = h.transpose(0, 2, 1, 3)
            mean = h.mean(-1, keepdims=True)
            var = h.var(-1, keepdims=True)
            hn = (h - mean) * jax.lax.rsqrt(var + NORM_EPS) * outnorm_weight
            return hn.reshape(B, S, E)
        key = jax.random.key(seed)
        ks = jax.random.split(key, 8)
        B, S, E, NH = (2, 256, 128, NUM_HEADS)
        DH = E // NH
        q = jax.random.normal(ks[0], (B, S, E), jnp.float32)
        k = jax.random.normal(ks[1], (B, S, E), jnp.float32)
        v = jax.random.normal(ks[2], (B, S, E), jnp.float32)
        ig_kernel = jax.random.normal(ks[3], (3 * E, NH), jnp.float32) * 0.02
        fg_kernel = jax.random.normal(ks[4], (3 * E, NH), jnp.float32) * 0.02
        ig_bias = jax.random.normal(ks[5], (NH,), jnp.float32) * 0.1
        fg_bias = jnp.linspace(3.0, 6.0, NH, dtype=jnp.float32)
        outnorm_weight = jnp.ones((NH, DH), jnp.float32)
        return {'q': q, 'k': k, 'v': v, 'ig_kernel': ig_kernel, 'ig_bias': ig_bias, 'fg_kernel': fg_kernel, 'fg_bias': fg_bias, 'outnorm_weight': outnorm_weight}
    _L1_xattn_all = _L1_xattn_setup()
    _L1_xattn_in = {k: v for k, v in _L1_xattn_all.items() if k in ('ig_kernel', 'ig_bias', 'fg_kernel', 'fg_bias', 'outnorm_weight')}
    del _L1_xattn_all

    def _L1_ffn_setup():
        import jax, jax.numpy as jnp
        import numpy as np
        HIDDEN = 128
        INTER = 512
        N_EXPERTS = 8
        TOP_K = 2
        INIT_STD = 0.02
        key = jax.random.key(seed)
        ks = jax.random.split(key, 6)
        x = jax.random.normal(ks[0], (2, 128, HIDDEN), dtype=jnp.float32)
        Wg = jax.random.normal(ks[1], (N_EXPERTS, HIDDEN), dtype=jnp.float32) * INIT_STD
        W1 = jax.random.normal(ks[2], (N_EXPERTS, HIDDEN, INTER), dtype=jnp.float32) * INIT_STD
        b1 = jnp.zeros((N_EXPERTS, INTER), dtype=jnp.float32)
        W2 = jax.random.normal(ks[3], (N_EXPERTS, INTER, HIDDEN), dtype=jnp.float32) * INIT_STD
        b2 = jnp.zeros((N_EXPERTS, HIDDEN), dtype=jnp.float32)
        return {'x': x, 'Wg': Wg, 'W1': W1, 'b1': b1, 'W2': W2, 'b2': b2}
    _L1_ffn_all = _L1_ffn_setup()
    _L1_ffn_in = {k: v for k, v in _L1_ffn_all.items() if k in ('Wg', 'W1', 'b1', 'W2', 'b2')}
    del _L1_ffn_all
    return {'x': x, 'ctx_1024': ctx_1024, 'fside_BxSxS2_0': fside_BxSxS2_0, 'L0_attn_W': _L0_attn_in['W'], 'L0_attn_b': _L0_attn_in['b'], 'L0_attn_Wd': _L0_attn_in['Wd'], 'L0_xattn_Wq': _L0_xattn_in['Wq'], 'L0_xattn_bq': _L0_xattn_in['bq'], 'L0_xattn_Wk': _L0_xattn_in['Wk'], 'L0_xattn_bk': _L0_xattn_in['bk'], 'L0_xattn_Wv': _L0_xattn_in['Wv'], 'L0_xattn_bv': _L0_xattn_in['bv'], 'L0_xattn_Wo': _L0_xattn_in['Wo'], 'L0_xattn_bo': _L0_xattn_in['bo'], 'L0_xattn_distance_scaling': _L0_xattn_in['distance_scaling'], 'L0_ffn_router_w': _L0_ffn_in['router_w'], 'L0_ffn_w1': _L0_ffn_in['w1'], 'L0_ffn_w2': _L0_ffn_in['w2'], 'L1_attn_Wq': _L1_attn_in['Wq'], 'L1_attn_Wk': _L1_attn_in['Wk'], 'L1_attn_Wv': _L1_attn_in['Wv'], 'L1_attn_Wo': _L1_attn_in['Wo'], 'L1_attn_Wg': _L1_attn_in['Wg'], 'L1_attn_bg': _L1_attn_in['bg'], 'L1_xattn_ig_kernel': _L1_xattn_in['ig_kernel'], 'L1_xattn_ig_bias': _L1_xattn_in['ig_bias'], 'L1_xattn_fg_kernel': _L1_xattn_in['fg_kernel'], 'L1_xattn_fg_bias': _L1_xattn_in['fg_bias'], 'L1_xattn_outnorm_weight': _L1_xattn_in['outnorm_weight'], 'L1_ffn_Wg': _L1_ffn_in['Wg'], 'L1_ffn_W1': _L1_ffn_in['W1'], 'L1_ffn_b1': _L1_ffn_in['b1'], 'L1_ffn_W2': _L1_ffn_in['W2'], 'L1_ffn_b2': _L1_ffn_in['b2']}

def reference(x, ctx_1024, fside_BxSxS2_0, L0_attn_W, L0_attn_b, L0_attn_Wd, L0_xattn_Wq, L0_xattn_bq, L0_xattn_Wk, L0_xattn_bk, L0_xattn_Wv, L0_xattn_bv, L0_xattn_Wo, L0_xattn_bo, L0_xattn_distance_scaling, L0_ffn_router_w, L0_ffn_w1, L0_ffn_w2, L1_attn_Wq, L1_attn_Wk, L1_attn_Wv, L1_attn_Wo, L1_attn_Wg, L1_attn_bg, L1_xattn_ig_kernel, L1_xattn_ig_bias, L1_xattn_fg_kernel, L1_xattn_fg_bias, L1_xattn_outnorm_weight, L1_ffn_Wg, L1_ffn_W1, L1_ffn_b1, L1_ffn_W2, L1_ffn_b2):
    import jax
    import jax.numpy as jnp

    def _L0_attn_ref(x, W, b, Wd):
        import jax, jax.numpy as jnp
        from jax import lax
        import numpy as np

        def log_g(x):
            return jnp.where(x >= 0, jnp.log(jnp.maximum(x, 0) + 0.5), -jax.nn.softplus(-x))
        k = jnp.einsum('btd,ed->bte', x, W) + b
        k_f, k_i, k_h = jnp.split(k, 3, axis=-1)
        log_f = -jax.nn.softplus(-k_f)
        log_i = -jax.nn.softplus(-k_i)
        log_tilde_h = log_g(k_h)
        B, T, E = log_f.shape
        log_h0 = jnp.full((B, 1, E), jnp.log(jnp.asarray(0.5, dtype=x.dtype)), dtype=x.dtype)
        a_star = jnp.pad(jnp.cumsum(log_f, axis=1), ((0, 0), (1, 0), (0, 0)))
        log_values = jnp.concatenate([log_h0, log_i + log_tilde_h], axis=1)
        log_h0_plus_b_star = lax.associative_scan(jnp.logaddexp, log_values - a_star, axis=1)
        h_t = jnp.exp(a_star + log_h0_plus_b_star)[:, 1:]
        return jnp.einsum('bte,de->btd', h_t, Wd)

    def _L0_xattn_ref(query, key_, value, distances, Wq, bq, Wk, bk, Wv, bv, Wo, bo, distance_scaling):
        import jax, jax.numpy as jnp
        import numpy as np
        EMBED_DIM = 128
        NUM_HEADS = 16
        HEAD_DIM = EMBED_DIM // NUM_HEADS
        B, SQ, SK = (4, 256, 256)

        def _xavier(key, shape):
            fan_in, fan_out = (shape[1], shape[0])
            limit = float(np.sqrt(6.0 / (fan_in + fan_out)))
            return jax.random.uniform(key, shape, jnp.float32, -limit, limit)
        b, sq, e = query.shape
        sk = key_.shape[1]
        h, d = (NUM_HEADS, HEAD_DIM)
        q = (query @ Wq.T + bq) * d ** (-0.5)
        k = key_ @ Wk.T + bk
        v = value @ Wv.T + bv
        q = q.reshape(b, sq, h, d).transpose(0, 2, 1, 3)
        k = k.reshape(b, sk, h, d).transpose(0, 2, 1, 3)
        v = v.reshape(b, sk, h, d).transpose(0, 2, 1, 3)
        scores = jnp.einsum('bhqd,bhkd->bhqk', q, k)
        distance_bias = -jnp.log(distances + 1e-09) * jnp.abs(distance_scaling)
        scores = scores + distance_bias[:, None, :, :]
        attn = jax.nn.softmax(scores, axis=-1)
        out = jnp.einsum('bhqk,bhkd->bhqd', attn, v)
        out = out.transpose(0, 2, 1, 3).reshape(b, sq, e)
        return out @ Wo.T + bo

    def _L0_ffn_ref(x, router_w, w1, w2):
        import jax, jax.numpy as jnp
        import numpy as np
        NUM_EXPERTS = 8
        TOP_K = 2
        CAP_RATIO = 1.25
        INIT_STD = 0.02
        B, T, H = x.shape
        E, K = (NUM_EXPERTS, TOP_K)
        xf = x.reshape(-1, H)
        N = xf.shape[0]
        P = N * K
        capacity = int(CAP_RATio * N * K / E) + 1 if False else int(CAP_RATIO * N * K / E) + 1
        logits = xf @ router_w.T
        probs = jax.nn.softmax(logits, axis=-1)
        k_probs, k_idx = jax.lax.top_k(probs, K)
        k_probs = k_probs / jnp.sum(k_probs, axis=-1, keepdims=True)
        flat_e = k_idx.reshape(-1)
        onehot = jax.nn.one_hot(flat_e, E, dtype=jnp.int32)
        rank = jnp.take_along_axis(jnp.cumsum(onehot, axis=0) - 1, flat_e[:, None], axis=1)[:, 0]
        keep = rank < capacity
        slot = jnp.minimum(rank, capacity - 1)
        token_id = jnp.arange(P) // K
        dispatched = jnp.where(keep[:, None], xf[token_id], 0.0)
        buf = jnp.zeros((E, capacity, H), x.dtype).at[flat_e, slot].add(dispatched)
        h = jax.nn.silu(jnp.einsum('ech,ehf->ecf', buf, w1))
        out_buf = jnp.einsum('ecf,efh->ech', h, w2)
        pair_out = out_buf[flat_e, slot] * keep[:, None].astype(x.dtype)
        combined = jnp.sum(pair_out.reshape(N, K, H) * k_probs[..., None], axis=1)
        return combined.reshape(B, T, H) + x

    def _L1_attn_ref(x, Wq, Wk, Wv, Wo, Wg, bg):
        import jax, jax.numpy as jnp
        import numpy as np
        D_MODEL = 128
        N_HEADS = 16
        D_HEAD = D_MODEL // N_HEADS
        SCALE = 1.0 / np.sqrt(D_HEAD).astype(np.float32)

        def _feature_map(x):
            return jax.nn.elu(x) + 1.0
        b, s, _ = x.shape
        q = (x @ Wq.T).reshape(b, s, N_HEADS, D_HEAD)
        k = (x @ Wk.T).reshape(b, s, N_HEADS, D_HEAD)
        v = (x @ Wv.T).reshape(b, s, N_HEADS, D_HEAD)
        q = _feature_map(q * SCALE)
        k = _feature_map(k)
        gate = jax.nn.sigmoid(x @ Wg.T + bg)
        qt = jnp.moveaxis(q, 1, 0)
        kt = jnp.moveaxis(k, 1, 0)
        vt = jnp.moveaxis(v, 1, 0)
        gt = jnp.moveaxis(gate, 1, 0)
        S0 = jnp.zeros((b, N_HEADS, D_HEAD, D_HEAD), dtype=x.dtype)

        def step(S, inp):
            q_t, k_t, v_t, g_t = inp
            S = g_t[:, :, None, None] * S + k_t[..., :, None] * v_t[..., None, :]
            y_t = jnp.einsum('bhi,bhij->bhj', q_t, S)
            return (S, y_t)
        _, ys = jax.lax.scan(step, S0, (qt, kt, vt, gt))
        y = jnp.moveaxis(ys, 0, 1).reshape(b, s, D_MODEL)
        return y @ Wo.T

    def _L1_xattn_ref(q, k, v, ig_kernel, ig_bias, fg_kernel, fg_bias, outnorm_weight):
        import jax, jax.numpy as jnp
        import numpy as np
        EPS_BACKEND = 1e-06
        NORM_EPS = 1e-06
        NUM_HEADS = 4

        def _mlstm_forward(q, k, v, ig_kernel, ig_bias, fg_kernel, fg_bias, outnorm_weight):
            B, S, E = q.shape
            NH = ig_bias.shape[0]
            DH = E // NH
            gate_input = jnp.concatenate([q, k, v], axis=-1)
            igate = gate_input @ ig_kernel + ig_bias
            fgate = gate_input @ fg_kernel + fg_bias
            qh = q.reshape(B, S, NH, DH).transpose(0, 2, 1, 3)
            kh = k.reshape(B, S, NH, DH).transpose(0, 2, 1, 3)
            vh = v.reshape(B, S, NH, DH).transpose(0, 2, 1, 3)
            ig = igate.transpose(0, 2, 1)
            fg = fgate.transpose(0, 2, 1)
            log_fg = jax.nn.log_sigmoid(fg)
            cums = jnp.concatenate([jnp.zeros((B, NH, 1), log_fg.dtype), jnp.cumsum(log_fg, axis=-1)], axis=-1)
            fg_mat = cums[..., :, None] - cums[..., None, :]
            mask = jnp.tril(jnp.ones((S + 1, S + 1), bool))
            fg_mat = jnp.where(mask, fg_mat, -jnp.inf)[..., 1:, 1:]
            log_D = fg_mat + ig[..., None, :]
            max_log_D = jnp.max(log_D, axis=-1, keepdims=True)
            D = jnp.exp(log_D - max_log_D)
            qk = jnp.einsum('bnsd,bntd->bnst', qh, kh) / jnp.sqrt(jnp.float32(DH))
            C = qk * D
            normalizer = jnp.maximum(jnp.abs(C.sum(-1, keepdims=True)), jnp.exp(-max_log_D))
            h = jnp.einsum('bnst,bntd->bnsd', C / (normalizer + EPS_BACKEND), vh)
            h = h.transpose(0, 2, 1, 3)
            mean = h.mean(-1, keepdims=True)
            var = h.var(-1, keepdims=True)
            hn = (h - mean) * jax.lax.rsqrt(var + NORM_EPS) * outnorm_weight
            return hn.reshape(B, S, E)
        return _mlstm_forward(q, k, v, ig_kernel, ig_bias, fg_kernel, fg_bias, outnorm_weight)

    def _L1_ffn_ref(x, Wg, W1, b1, W2, b2):
        import jax, jax.numpy as jnp
        import numpy as np
        HIDDEN = 128
        INTER = 512
        N_EXPERTS = 8
        TOP_K = 2
        INIT_STD = 0.02
        orig_shape = x.shape
        xt = x.reshape(-1, HIDDEN)
        T = xt.shape[0]
        logits = xt @ Wg.T
        topk_logits, topk_idx = jax.lax.top_k(logits, TOP_K)
        w = jax.nn.softmax(topk_logits, axis=-1)
        rows = jnp.arange(T)[:, None]
        gates = jnp.zeros((T, N_EXPERTS), xt.dtype).at[rows, topk_idx].add(w)
        h = jnp.einsum('th,ehi->tei', xt, W1) + b1
        h = jax.nn.gelu(h, approximate=False)
        o = jnp.einsum('tei,eih->teh', h, W2) + b2
        y = jnp.einsum('te,teh->th', gates, o)
        return y.reshape(orig_shape)
    x = x + _L0_attn_ref(_layernorm(x, axis=-1), L0_attn_W, L0_attn_b, L0_attn_Wd)
    x = x + _L0_xattn_ref(_layernorm(x, axis=-1), ctx_1024, ctx_1024, fside_BxSxS2_0, L0_xattn_Wq, L0_xattn_bq, L0_xattn_Wk, L0_xattn_bk, L0_xattn_Wv, L0_xattn_bv, L0_xattn_Wo, L0_xattn_bo, L0_xattn_distance_scaling)
    x = x + _L0_ffn_ref(_layernorm(x, axis=-1), L0_ffn_router_w, L0_ffn_w1, L0_ffn_w2)
    x = x + _L1_attn_ref(_layernorm(x, axis=-1), L1_attn_Wq, L1_attn_Wk, L1_attn_Wv, L1_attn_Wo, L1_attn_Wg, L1_attn_bg)
    x = x + _L1_xattn_ref(_layernorm(x, axis=-1), ctx_1024, ctx_1024, L1_xattn_ig_kernel, L1_xattn_ig_bias, L1_xattn_fg_kernel, L1_xattn_fg_bias, L1_xattn_outnorm_weight)
    x = x + _L1_ffn_ref(_layernorm(x, axis=-1), L1_ffn_Wg, L1_ffn_W1, L1_ffn_b1, L1_ffn_W2, L1_ffn_b2)
    return x

_drawn_inputs = setup_inputs


def setup_inputs(seed=0):
    import zlib

    import numpy as np

    out = dict(_drawn_inputs(seed))
    spreads = {'L0_xattn_bq': (0.0, 0.35),
     'L0_xattn_bk': (0.0, 2.0),
     'L0_xattn_bv': (0.0, 0.1),
     'L0_xattn_bo': (0.0, 0.1),
     'L1_xattn_outnorm_weight': (1.0, 0.6),
     'L1_ffn_b1': (0.0, 0.8),
     'L1_ffn_b2': (0.0, 0.8)}
    factors = {'L0_attn_b': 3.316,
     'L0_ffn_router_w': 5.447,
     'L0_ffn_w1': 4.543,
     'L0_ffn_w2': 4.372,
     'L1_attn_bg': 7.623,
     'L1_xattn_ig_kernel': 5.609,
     'L1_xattn_ig_bias': 64.0,
     'L1_xattn_fg_kernel': 64.0,
     'L1_xattn_fg_bias': 42.104,
     'L1_ffn_Wg': 8.0,
     'L1_ffn_W1': 8.0,
     'L1_ffn_W2': 8.0}
    for name, (base, spread) in spreads.items():
        noise = np.random.default_rng([zlib.crc32(name.encode()), seed]).standard_normal(out[name].shape)
        drawn = base * np.exp(spread * noise) if base else spread * noise
        out[name] = jnp.asarray(drawn.astype(out[name].dtype))
    for name, factor in factors.items():
        out[name] = (out[name] * factor).astype(out[name].dtype)
    return out
```

```python
from contextlib import ExitStack

import numpy as np

import concourse.bass as bass
from concourse import mybir

F32 = mybir.dt.float32
BF16 = mybir.dt.bfloat16
ALU = mybir.AluOpType
ACT = mybir.ActivationFunctionType
AX_X = mybir.AxisListType.X

P = 128
B, S, D = 8, 256, 128
PAIR = 2
T = PAIR * S
NT = T // P
STEPS = B // PAIR
E0 = 256
NC0 = 3 * E0 // P
H, HD = 16, 8
NE, FF = 8, 512
FC = FF // P
TOPK = 2
CAPACITY = int(1.25 * B * S * TOPK / NE) + 1
MH, MD = 4, 32
UNITS = PAIR * 2 * (H // 2)
BIG = 3.0e38


class Signal:

    def __init__(self, nc, ctx, name, per, base=0):
        self.sem = ctx.enter_context(nc.semaphore(name))
        self.per = per
        self.base = base

    def at(self, it, n):
        assert n > 0 or self.base > 0, "a wait must be against a value above zero"
        return it * self.per + (self.base + n)


def decoder(nc, a, out):
    with ExitStack() as ctx:
        def sb(name, shape, dt=F32):
            return ctx.enter_context(nc.sbuf_tensor(name, shape, dt))

        def sig(name, per, base=0):
            return Signal(nc, ctx, name, per, base)

        bank = [ctx.enter_context(nc.psum_tensor(f"bank{i}", [P, 512], F32)) for i in range(8)]

        ident = sb("ident", [P, P])
        earlier = sb("earlier", [P, P])
        ones = sb("ones", [P, P])
        lower = sb("lower", [P, NE, NE])
        pick = sb("pick", [P, HD, P])
        row = sb("row", [MH, MH, P])
        w_rnn = sb("w_rnn", [P, 3 * E0])
        b_rnn = sb("b_rnn", [P, NC0])
        b_rnn_half = sb("b_rnn_half", [P, NC0])
        wd_rnn = sb("wd_rnn", [P, E0 // P, D])
        w_x = sb("w_x", [P, 4, D])
        b_xqk = sb("b_xqk", [P, 2])
        bq_scaled = sb("bq_scaled", [P, 1])
        bv_row = sb("bv_row", [P, D])
        bo_row = sb("bo_row", [P, D])
        dscale = sb("dscale", [P, 1])
        dscale_abs = sb("dscale_abs", [P, 1])
        tiny = sb("tiny", [P, 1])
        w_l = sb("w_l", [P, 4, D])
        wg_l = sb("wg_l", [P, H, HD])
        wg_raw = sb("wg_raw", [P, H])
        bg_l = sb("bg_l", [P, 1])
        w_route = sb("w_route", [P, 2, NE])
        w_up = sb("w_up", [P, 2, NE, FF])
        w_down = sb("w_down", [P, 2, NE, FC, D])
        b_up = sb("b_up", [P, NE * FC])
        b_down = sb("b_down", [NE, D])
        gk_raw = sb("gk_raw", [P, 3, 2 * MH])
        gk = sb("gk", [P, 2, 36])
        gbias = sb("gbias", [36, 1])
        onw = sb("onw", [P, MH * MD])

        x_in = sb("x_in", [P, NT, D])
        dist = sb("dist", [P, NT, S])
        ctxT = sb("ctxT", [P, T])
        ctx_tok = sb("ctx_tok", [P, NT, MH, MD + 1])
        x = sb("x", [P, NT, D])
        xn = sb("xn", [P, NT, D])
        xnT = sb("xnT", [P, T])
        stats = sb("stats", [P, NT, 6])
        mv = sb("mv", [P, NT, 2])
        ve = sb("ve", [P, NT])
        rstd = sb("rstd", [P, NT])
        mhalf = sb("mhalf", [P, NT * MH])
        arena = sb("arena", [P, 2, 4096])
        flat = arena[:].rearrange("p a b -> p (a b)")

        def scratch(i, n=T):
            return flat[:, i * T:i * T + n]

        sgm = [scratch(c) for c in range(NC0)]
        g0 = [scratch(6 + e) for e in range(2)]
        bi = [scratch(8 + e) for e in range(2)]
        hT = [scratch(10 + e) for e in range(2)]
        qk_f = [scratch(0), scratch(1)]
        bounce = nc.dram_tensor("bounce", (2, P, T), F32, kind="Internal").ap()
        qr = sb("qr", [40, H, S])
        kr = sb("kr", [40, H, S])
        v_aug = sb("v_aug", [P, NT, H, HD + 1])
        nb = sb("nb", [P, NT, S])
        sc = sb("sc", [P, 3, 2, S])
        mneg = sb("mneg", [P, UNITS * 2])
        prob = sb("prob", [P, 3, 2, S])
        pT = sb("pT", [P, 2, T])
        rsum = sb("rsum", [P, H])
        attn = sb("attn", [P, NT, D])
        attnT = sb("attnT", [P, T])
        hid = arena[:].rearrange("p a (c t) -> p a c t", c=8)
        logit = sb("logit", [P, NT, NE])
        cmp_gt = sb("cmp_gt", [P, NT, NE, NE])
        cmp_eq = sb("cmp_eq", [P, NT, NE, NE])
        cnt = sb("cnt", [P, NT, NE])
        sel = sb("sel", [P, NT, NE])
        top = sb("top", [P, NT])
        ex = sb("ex", [P, NT, NE])
        gate = sb("gate", [P, NT, NE])
        taken = sb("taken", [P, NE])
        gateT = sb("gateT", [NE, T])
        tmin = [scratch(0), scratch(1)]
        eluv = [scratch(2), scratch(3)]
        phi = [scratch(4), scratch(5)]
        vT = scratch(6)
        gT = scratch(7)
        kv = [scratch(8), scratch(9)]
        st = [scratch(10), scratch(11)]
        qs = [scratch(12), scratch(13)]
        ig = flat[0:MH, 8 * T:9 * T]
        fmin = flat[0:MH, 9 * T:10 * T]
        fabs = flat[0:MH, 10 * T:11 * T]
        fexp = flat[0:MH, 11 * T:12 * T]
        fln = flat[0:MH, 12 * T:13 * T]
        fcum = flat[0:MH, 13 * T:14 * T]
        umax = flat[0:MH, 14 * T:15 * T]
        mrow = flat[0:MH, 15 * T:16 * T]
        u36 = sb("u36", [36, T])
        uT = sb("uT", [P, NT, 36])
        efm = sb("efm", [P, NT, MH])
        decay = [scratch(i, 384).rearrange("p (b t) -> p b t", b=3) for i in range(2)]
        cT = [scratch(2 + i, 384).rearrange("p (b t) -> p b t", b=3) for i in range(2)]
        nrm = sb("nrm", [P, NT, MH])
        rn = sb("rn", [P, NT, MH])
        hh = scratch(4).rearrange("p (g d) -> p g d", d=MD)
        hc = scratch(5).rearrange("p (g d) -> p g d", d=MD)
        hsq = scratch(6).rearrange("p (g d) -> p g d", d=MD)
        hn = scratch(7).rearrange("p (g d) -> p g d", d=MD)
        mstat = sb("mstat", [P, 4, NT * MH])

        passed_dve = ctx.enter_context(nc.semaphore("passed_dve"))
        passed_pool = ctx.enter_context(nc.semaphore("passed_pool"))
        weights_in = ctx.enter_context(nc.semaphore("weights_in"))
        setup_done = ctx.enter_context(nc.semaphore("setup_done"))
        x_loaded = sig("x_loaded", 16)
        ctx_loaded = sig("ctx_loaded", 16 * (1 + NT))
        dist_loaded = sig("dist_loaded", 16)
        x_taken = sig("x_taken", 1, base=1)
        dist_taken = sig("dist_taken", 1, base=1)
        ctx_taken = sig("ctx_taken", 1, base=1)
        x_stored = sig("x_stored", 16, base=16)
        var_ready = sig("var_ready", 6)
        rstd_ready = sig("rstd_ready", 6)
        xn_ready = sig("xn_ready", 6)
        xnT_psum = sig("xnT_psum", 6)
        xnT_ready = sig("xnT_ready", 6)
        rnn_proj = sig("rnn_proj", NC0)
        rnn_sig = sig("rnn_sig", NC0)
        rnn_state = sig("rnn_state", 2)
        rnn_y = sig("rnn_y", 1)
        log_dist = sig("log_dist", 1)
        qkv_psum = sig("qkv_psum", 3)
        qk_sb = sig("qk_sb", 2)
        bounced = sig("bounced", 32)
        qr_in = sig("qr_in", 16 * 2 * PAIR)
        v_ready = sig("v_ready", 1)
        s_psum = sig("s_psum", UNITS)
        s_biased = sig("s_biased", UNITS)
        p_ready = sig("p_ready", UNITS)
        p_turned = sig("p_turned", UNITS)
        pT_even = sig("pT_even", UNITS // 2)
        pT_odd = sig("pT_odd", UNITS // 2)
        pT_ready = [pT_even, pT_odd]
        pv_done = sig("pv_done", UNITS)
        attn_ready = sig("attn_ready", NT)
        attnT_psum = sig("attnT_psum", 1)
        attnT_ready = sig("attnT_ready", 1)
        attn_y = sig("attn_y", 1)
        logits_psum = sig("logits_psum", 2)
        route_in = sig("route_in", 2)
        route_exp = sig("route_exp", 2)
        sel_ready = sig("sel_ready", 1)
        rank_psum = sig("rank_psum", 1)
        up_psum = sig("up_psum", 2 * NE * FC)
        hid_ready = sig("hid_ready", 2 * NE * FC)
        down_psum = sig("down_psum", 2 * NE)
        expert_added = sig("expert_added", 2 * NE)
        gate_ready = sig("gate_ready", 1)
        gateT_psum = sig("gateT_psum", 1)
        gateT_ready = sig("gateT_ready", 1)
        bias_psum = sig("bias_psum", 1)
        lin_proj = sig("lin_proj", 4)
        elu_in = sig("elu_in", 2)
        elu_exp = sig("elu_exp", 2)
        phi_ready = sig("phi_ready", 2)
        lin_vg = sig("lin_vg", 2)
        kb_psum = sig("kb_psum", HD)
        qb_psum = sig("qb_psum", HD)
        kv_ready = sig("kv_ready", HD)
        qs_ready = sig("qs_ready", HD)
        lin_fold = sig("lin_fold", HD)
        gates_psum = sig("gates_psum", 1)
        fabs_ready = sig("fabs_ready", 1)
        fexp_ready = sig("fexp_ready", 1)
        fln_ready = sig("fln_ready", 1)
        m_ready = sig("m_ready", 1)
        uT_psum = sig("uT_psum", 1)
        uT_ready = sig("uT_ready", 1)
        efm_ready = sig("efm_ready", 1)
        mb_psum = sig("mb_psum", MH)
        qk_psum = sig("qk_psum", MH * PAIR)
        decay_exp = sig("decay_exp", MH * PAIR)
        decay_cut = sig("decay_cut", MH * PAIR)
        c_ready = sig("c_ready", MH * PAIR)
        h_psum = sig("h_psum", MH * PAIR)
        hvar_ready = sig("hvar_ready", 1)
        hrstd_ready = sig("hrstd_ready", 1)
        DVE_STEPS = 79
        dve_step = sig("dve_step", DVE_STEPS)

        setup_loads = []

        def setup_load(eng, dst, src):
            setup_loads.append(1)
            eng.dma_start(dst, src).then_inc(weights_in, 16)

        SETUP_OPS = 16
        block = ctx.enter_context(nc.Block())

        @block.sync
        def _(sp):
            for dst, name in ((ident, "ident"), (earlier, "earlier"), (ones, "ones"), (lower, "lower"),
                              (pick, "pick"), (row, "row"), (w_rnn, "w_rnn"), (b_rnn, "b_rnn"),
                              (wd_rnn, "wd_rnn"), (w_x, "w_x"), (b_xqk, "b_xqk"), (w_l, "w_l"),
                              (w_route, "w_route"), (b_up, "b_up"), (b_down, "b_down"), (gk_raw, "gk_raw")):
                setup_load(sp, dst[:], a[name])
            setup_load(sp, wg_raw[:], a["wg_l"])
            setup_load(sp, bg_l[:, 0:1], a["bg_l"])
            setup_load(sp, gbias[0:MH, :], a["gate_bias"][0])
            setup_load(sp, gbias[32:32 + MH, :], a["gate_bias"][1])
            for dst, name in ((bv_row, "bv"), (bo_row, "bo"), (dscale, "dscale"), (onw, "onw")):
                setup_load(sp, dst[:], a[name].partition_broadcast(P))
            for l in range(2):
                setup_load(sp, w_up[:, l], a["w_up"][l].rearrange("e d f -> d e f"))
                setup_load(sp, w_down[:, l], a["w_down"][l].rearrange("e (c p) d -> p e c d", p=P))
            for s in (x_taken, dist_taken, ctx_taken, x_stored):
                sp.sem_inc(s.sem, s.base)
            with sp.Fori(0, STEPS) as it:
                sp.wait_ge(x_taken.sem, x_taken.at(it, 0))
                sp.dma_start(x_in[:], a["x"][bass.ds(it, 1)].rearrange("o p n d -> p (o n) d")).then_inc(x_loaded.sem, 16)
                sp.wait_ge(dist_taken.sem, dist_taken.at(it, 0))
                sp.dma_start(dist[:], a["dist"][bass.ds(it, 1)].rearrange("o p n k -> p (o n) k")).then_inc(dist_loaded.sem, 16)
                sp.wait_ge(ctx_taken.sem, ctx_taken.at(it, 0))
                sp.dma_start(ctxT[:], a["ctxT"][bass.ds(it, 1)].rearrange("o p t -> p (o t)")).then_inc(ctx_loaded.sem, 16)
                for n in range(NT):
                    sp.dma_start(ctx_tok[:, n, :, 0:MD], a["ctx"][bass.ds(it, 1), :, n].rearrange("o p (h d) -> p (o h) d", h=MH)
                                 ).then_inc(ctx_loaded.sem, 16)
                for i, dst in ((0, qr), (1, kr)):
                    sp.wait_ge(qk_sb.sem, qk_sb.at(it, i + 1))
                    sp.dma_start(bounce[i], qk_f[i]).then_inc(bounced.sem, 16)
                for i, dst in ((0, qr), (1, kr)):
                    sp.wait_ge(bounced.sem, bounced.at(it, 32))
                    for bb in range(PAIR):
                        sp.dma_start(dst[32 * bb:32 * bb + HD],
                                     bounce[i, :, bb * S:(bb + 1) * S].rearrange("(h d) t -> d h t", d=HD)
                                     ).then_inc(qr_in.sem, 16)
                sp.wait_ge(expert_added.sem, expert_added.at(it, 2 * NE))
                sp.dma_start(out[bass.ds(it, 1)].rearrange("o p n d -> p (o n) d"), x[:]).then_inc(x_stored.sem, 16)
            sp.wait_ge(x_stored.sem, 16 * STEPS + x_stored.base)

        LOADS = len(setup_loads)

        @block.gpsimd
        def _(pool):
            nc.gpsimd.memset(mhalf[:], -0.5).then_inc(setup_done, 1)
            nc.gpsimd.memset(tiny[:], 1e-9).then_inc(setup_done, 1)
            nc.gpsimd.memset(v_aug[:], 1.0).then_inc(setup_done, 1)
            nc.gpsimd.memset(ctx_tok[:, :, :, MD:MD + 1], 1.0).then_inc(setup_done, 1)
            nc.gpsimd.memset(u36[:], 0.0).then_inc(setup_done, 1)
            nc.gpsimd.memset(taken[:], 0.0).then_inc(setup_done, 1)
            pool.wait_ge(setup_done, SETUP_OPS)
            with pool.Fori(0, STEPS) as it:
                def inverse_root(j):
                    pool.wait_ge(var_ready.sem, var_ready.at(it, j + 1))
                    nc.gpsimd.tensor_tensor(rstd[:], ve[:], mhalf[:, 0:NT], ALU.pow).then_inc(rstd_ready.sem, 1)

                for j in range(5):
                    inverse_root(j)
                for k in range(MH * PAIR):
                    pool.wait_ge(decay_exp.sem, decay_exp.at(it, k + 1))
                    pool.sem_inc(passed_pool, 1)
                    d = decay[k % 2][:, 0:3:2, :]
                    nc.gpsimd.affine_select(out=d, in_=d, compare_op=ALU.is_ge, fill=0.0, base=0,
                                            pattern=[[0, 2], [1, P]], channel_multiplier=-1).then_inc(decay_cut.sem, 1)
                pool.wait_ge(hvar_ready.sem, hvar_ready.at(it, 1))
                nc.gpsimd.tensor_tensor(mstat[:, 3], mstat[:, 2], mhalf[:], ALU.pow).then_inc(hrstd_ready.sem, 1)
                inverse_root(5)

        @block.scalar
        def _(act):
            act.wait_ge(setup_done, SETUP_OPS)
            with act.Fori(0, STEPS) as it:
                def turn_out(j):
                    act.wait_ge(xnT_psum.sem, xnT_psum.at(it, j + 1))
                    nc.scalar.copy(xnT[:], bank[7][:]).then_inc(xnT_ready.sem, 1)

                def experts(l, func):
                    act.wait_ge(route_in.sem, route_in.at(it, l + 1))
                    nc.scalar.activation(ex[:], ex[:], ACT.Exp).then_inc(route_exp.sem, 1)
                    for e in range(NE):
                        for c in range(FC):
                            k = (l * NE + e) * FC + c
                            act.wait_ge(up_psum.sem, up_psum.at(it, k + 1))
                            if e >= 2 and c == 0:
                                act.wait_ge(down_psum.sem, down_psum.at(it, l * NE + e - 1))
                            bias = {} if l == 0 else {"bias": b_up[:, e * FC + c:e * FC + c + 1]}
                            nc.scalar.activation(hid[:, e % 2, c], bank[c][:], func, **bias).then_inc(hid_ready.sem, 1)

                act.wait_ge(dist_loaded.sem, dist_loaded.at(it, 16))
                nc.scalar.activation(nb[:], dist[:], ACT.Ln, bias=tiny[:, 0:1]).then_inc(log_dist.sem, 1)

                turn_out(0)
                for c in range(NC0):
                    act.wait_ge(rnn_proj.sem, rnn_proj.at(it, c + 1))
                    k = (c % 3) * 2 + c // 3
                    nc.scalar.activation(sgm[c], bank[c][:], ACT.Sigmoid, bias=b_rnn[:, k:k + 1]).then_inc(rnn_sig.sem, 1)

                turn_out(1)
                act.wait_ge(qkv_psum.sem, qkv_psum.at(it, 1))
                nc.scalar.activation(qk_f[0], bank[0][:], ACT.Identity, bias=bq_scaled[:, 0:1],
                                     scale=-HD ** -0.5).then_inc(qk_sb.sem, 1)
                act.wait_ge(qkv_psum.sem, qkv_psum.at(it, 2))
                nc.scalar.activation(qk_f[1], bank[1][:], ACT.Identity, bias=b_xqk[:, 1:2]).then_inc(qk_sb.sem, 1)

                def turned_copy(u):
                    act.wait_ge(p_turned.sem, p_turned.at(it, u + 1))
                    if u >= 2:
                        act.wait_ge(pv_done.sem, pv_done.at(it, u - 1))
                    nc.scalar.copy(pT[:, u % 2], bank[3 + u % 2][:]).then_inc(pT_odd.sem, 1)

                for u in range(UNITS):
                    act.wait_ge(s_biased.sem, s_biased.at(it, u + 1))
                    if u >= 3:
                        act.wait_ge(p_turned.sem, p_turned.at(it, u - 2))
                    for j in range(2):
                        last = nc.scalar.activation(prob[:, u % 3, j], sc[:, u % 3, j], ACT.Exp, scale=-1.0,
                                                    bias=mneg[:, 2 * u + j:2 * u + j + 1])
                    last.then_inc(p_ready.sem, 1)
                    if u >= 1 and (u - 1) % 2 == 1:
                        turned_copy(u - 1)
                turned_copy(UNITS - 1)
                act.wait_ge(attnT_psum.sem, attnT_psum.at(it, 1))
                nc.scalar.copy(attnT[:], bank[7][:]).then_inc(attnT_ready.sem, 1)

                turn_out(2)
                experts(0, ACT.Silu)

                turn_out(3)
                for i in range(2):
                    act.wait_ge(elu_in.sem, elu_in.at(it, i + 1))
                    nc.scalar.activation(eluv[i], tmin[i], ACT.Exp).then_inc(elu_exp.sem, 1)
                act.wait_ge(lin_proj.sem, lin_proj.at(it, 3))
                nc.scalar.copy(vT, bank[2][:]).then_inc(lin_vg.sem, 1)
                act.wait_ge(lin_proj.sem, lin_proj.at(it, 4))
                nc.scalar.activation(gT, bank[3][:], ACT.Sigmoid, bias=bg_l[:, 0:1]).then_inc(lin_vg.sem, 1)

                turn_out(4)
                act.wait_ge(fabs_ready.sem, fabs_ready.at(it, 1))
                nc.scalar.activation(fexp[:], fabs[:], ACT.Exp, scale=-1.0).then_inc(fexp_ready.sem, 1)
                act.wait_ge(fexp_ready.sem, fexp_ready.at(it, 1))
                nc.scalar.activation(fln[:], fexp[:], ACT.Ln, bias=1.0).then_inc(fln_ready.sem, 1)
                act.wait_ge(uT_ready.sem, uT_ready.at(it, 1))
                nc.scalar.activation(efm[:], uT[:, :, 32:32 + MH], ACT.Exp, scale=-1.0).then_inc(efm_ready.sem, 1)
                for h in range(MH):
                    for bb in range(PAIR):
                        k = h * PAIR + bb
                        act.wait_ge(mb_psum.sem, mb_psum.at(it, h + 1))
                        if k >= 2:
                            act.wait_ge(c_ready.sem, c_ready.at(it, k - 1))
                        mb = bank[2 + h % 2]
                        nc.scalar.activation(decay[k % 2][:, 0:2, :], mb[:, bb * S:(bb + 1) * S].rearrange("p (b t) -> p b t", b=2),
                                             ACT.Exp, bias=uT[:, 2 * bb, h:h + 1])
                        nc.scalar.activation(decay[k % 2][:, 2, :], mb[:, bb * S + P:(bb + 1) * S],
                                             ACT.Exp, bias=uT[:, 2 * bb + 1, h:h + 1]).then_inc(decay_exp.sem, 1)

                turn_out(5)
                experts(1, ACT.Gelu)

        @block.tensor
        def _(pe):
            pe.wait_ge(weights_in, 16 * LOADS)
            pe.wait_ge(setup_done, SETUP_OPS)
            with pe.Fori(0, STEPS) as it:
                def tok(n):
                    return slice(n * P, (n + 1) * P)

                def alone():
                    pe.wait_ge(setup_done, SETUP_OPS)

                def turn(j):
                    pe.wait_ge(xn_ready.sem, xn_ready.at(it, j + 1))
                    for n in range(NT):
                        last = nc.tensor.transpose(bank[7][:, tok(n)], xn[:, n], ident[:])
                    last.then_inc(xnT_psum.sem, 1)
                    pe.wait_ge(xnT_ready.sem, xnT_ready.at(it, j + 1))

                def experts(l):
                    for n in range(NT):
                        last = nc.tensor.matmul(bank[5][:, n * NE:(n + 1) * NE], xnT[:, tok(n)], w_route[:, l],
                                                start=True, stop=True)
                    last.then_inc(logits_psum.sem, 1)

                    def up(e):
                        for c in range(FC):
                            if e >= 1:
                                pe.wait_ge(hid_ready.sem, hid_ready.at(it, (l * NE + e - 1) * FC + c + 1))
                            nc.tensor.matmul(bank[c][:], w_up[:, l, e, c * P:(c + 1) * P], xnT[:],
                                             start=True, stop=True).then_inc(up_psum.sem, 1)

                    def down(e):
                        pe.wait_ge(hid_ready.sem, hid_ready.at(it, (l * NE + e + 1) * FC))
                        if e >= 2:
                            pe.wait_ge(expert_added.sem, expert_added.at(it, l * NE + e - 1))
                        y = bank[6 + e % 2]
                        for n in range(NT):
                            for c in range(FC):
                                last = nc.tensor.matmul(y[:, tok(n)], hid[:, e % 2, c, tok(n)], w_down[:, l, e, c],
                                                        start=(c == 0), stop=(c == FC - 1))
                        last.then_inc(down_psum.sem, 1)

                    up(0)
                    if l == 0:
                        pe.wait_ge(sel_ready.sem, sel_ready.at(it, 1))
                        for n in range(NT):
                            r = bank[4][:, n * NE:(n + 1) * NE]
                            for m in range(n):
                                nc.tensor.matmul(r, ones[:], sel[:, m], start=(m == 0), stop=False)
                            nc.tensor.matmul(r, earlier[:], sel[:, n], start=(n == 0), stop=True)
                        for m in range(NT):
                            last = nc.tensor.matmul(bank[4][:, NT * NE:(NT + 1) * NE], ones[:], sel[:, m],
                                                    start=(m == 0), stop=(m == NT - 1))
                        last.then_inc(rank_psum.sem, 1)
                    else:
                        pe.wait_ge(gate_ready.sem, gate_ready.at(it, 1))
                        for n in range(NT):
                            last = nc.tensor.transpose(bank[4][0:NE, tok(n)], gate[:, n], ident[:])
                        last.then_inc(gateT_psum.sem, 1)
                    up(1)
                    if l == 1:
                        pe.wait_ge(gateT_ready.sem, gateT_ready.at(it, 1))
                        for n in range(NT):
                            last = nc.tensor.matmul(bank[5][:, tok(n)], gateT[:, tok(n)], b_down[:], start=True, stop=True)
                        last.then_inc(bias_psum.sem, 1)
                    for e in range(NE):
                        down(e)
                        if e + 2 < NE:
                            up(e + 2)

                turn(0)
                for c in range(NC0):
                    k = (c % 3) * 2 + c // 3
                    nc.tensor.matmul(bank[c][:], w_rnn[:, k * P:(k + 1) * P], xnT[:], start=True, stop=True).then_inc(rnn_proj.sem, 1)
                pe.wait_ge(rnn_state.sem, rnn_state.at(it, 2))
                for n in range(NT):
                    for e in range(2):
                        last = nc.tensor.matmul(bank[6][:, tok(n)], hT[e][:, tok(n)], wd_rnn[:, e], start=(e == 0), stop=(e == 1))
                last.then_inc(rnn_y.sem, 1)

                turn(1)
                nc.tensor.matmul(bank[0][:], w_x[:, 0], xnT[:], start=True, stop=True).then_inc(qkv_psum.sem, 1)
                pe.wait_ge(ctx_loaded.sem, ctx_loaded.at(it, ctx_loaded.per))
                nc.tensor.matmul(bank[1][:], w_x[:, 1], ctxT[:], start=True, stop=True).then_inc(qkv_psum.sem, 1)
                for n in range(NT):
                    last = nc.tensor.matmul(bank[2][:, tok(n)], ctxT[:, tok(n)], w_x[:, 2], start=True, stop=True)
                last.then_inc(qkv_psum.sem, 1)
                pe.wait_ge(v_ready.sem, v_ready.at(it, 1))
                pe.wait_ge(qr_in.sem, qr_in.at(it, qr_in.per))

                def scores(u):
                    bb, qt, hp = u // 16, u // 8 % 2, u % 8
                    if u >= 3:
                        pe.wait_ge(s_biased.sem, s_biased.at(it, u - 2))
                    for j in range(2):
                        h = 2 * hp + j
                        last = nc.tensor.matmul(bank[u % 3][:, j * S:(j + 1) * S], qr[32 * bb:32 * bb + HD, h, tok(qt)],
                                                kr[32 * bb:32 * bb + HD, h, :], start=True, stop=True)
                    last.then_inc(s_psum.sem, 1)

                def turn_probs(u):
                    pe.wait_ge(p_ready.sem, p_ready.at(it, u + 1))
                    if u >= 2:
                        pe.wait_ge(pT_ready[u % 2].sem, pT_ready[u % 2].at(it, u // 2))
                    for j in range(2):
                        for kt in range(2):
                            last = nc.tensor.transpose(bank[3 + u % 2][:, tok(2 * j + kt)], prob[:, u % 3, j, tok(kt)], ident[:])
                    last.then_inc(p_turned.sem, 1)

                def weigh(u):
                    bb, hp = u // 16, u % 8
                    pe.wait_ge(pT_ready[u % 2].sem, pT_ready[u % 2].at(it, u // 2 + 1))
                    if u >= 8 and hp == 0:
                        pe.wait_ge(attn_ready.sem, attn_ready.at(it, u // 8))
                    for j in range(2):
                        h = 2 * hp + j
                        for kt in range(2):
                            last = nc.tensor.matmul(bank[5][:, h * (HD + 1):(h + 1) * (HD + 1)], pT[:, u % 2, tok(2 * j + kt)],
                                                    v_aug[:, 2 * bb + kt, h], start=(kt == 0), stop=(kt == 1))
                    last.then_inc(pv_done.sem, 1)

                scores(0)
                scores(1)
                for u in range(UNITS):
                    if u + 2 < UNITS:
                        scores(u + 2)
                    turn_probs(u)
                    if u >= 1:
                        weigh(u - 1)
                weigh(UNITS - 1)
                pe.wait_ge(attn_ready.sem, attn_ready.at(it, NT))
                for n in range(NT):
                    last = nc.tensor.transpose(bank[7][:, tok(n)], attn[:, n], ident[:])
                last.then_inc(attnT_psum.sem, 1)
                pe.wait_ge(attnT_ready.sem, attnT_ready.at(it, 1))
                for n in range(NT):
                    last = nc.tensor.matmul(bank[6][:, tok(n)], attnT[:, tok(n)], w_x[:, 3], start=True, stop=True)
                last.then_inc(attn_y.sem, 1)

                turn(2)
                experts(0)

                turn(3)
                for i, w in enumerate((w_l[:, 0], w_l[:, 1], w_l[:, 2], wg_l[:].rearrange("p h j -> p (h j)"))):
                    nc.tensor.matmul(bank[i][:], w, xnT[:], start=True, stop=True).then_inc(lin_proj.sem, 1)
                pe.wait_ge(phi_ready.sem, phi_ready.at(it, 2))
                pe.wait_ge(lin_vg.sem, lin_vg.at(it, 2))

                def spread_k(i):
                    if i >= 2:
                        pe.wait_ge(kv_ready.sem, kv_ready.at(it, i - 1))
                    nc.tensor.matmul(bank[4 + i % 2][:], pick[:, i], phi[1], start=True, stop=True).then_inc(kb_psum.sem, 1)

                def spread_q(i):
                    if i >= 2:
                        pe.wait_ge(qs_ready.sem, qs_ready.at(it, i - 1))
                    nc.tensor.matmul(bank[2 + i % 2][:], pick[:, i], phi[0], start=True, stop=True).then_inc(qb_psum.sem, 1)

                def fold(i):
                    pe.wait_ge(qs_ready.sem, qs_ready.at(it, i + 1))
                    for n in range(NT):
                        last = nc.tensor.matmul(bank[6][:, tok(n)], qs[i % 2][:, tok(n)], w_l[:, 3], start=(i == 0 and n == 0),
                                                stop=(i == HD - 1), skip_group_check=True)
                    last.then_inc(lin_fold.sem, 1)

                spread_k(0)
                spread_q(0)
                for i in range(HD):
                    if i + 1 < HD:
                        spread_k(i + 1)
                        spread_q(i + 1)
                    fold(i)

                turn(4)
                nc.tensor.matmul(bank[0][0:36, :], gk[:, 0], xnT[:], start=True, stop=False)
                nc.tensor.matmul(bank[0][0:36, :], gk[:, 1], ctxT[:], start=False, stop=True).then_inc(gates_psum.sem, 1)
                alone()
                pe.wait_ge(m_ready.sem, m_ready.at(it, 1))
                for n in range(NT):
                    last = nc.tensor.transpose(bank[1][:, n * 36:(n + 1) * 36], u36[:, tok(n)], ident[0:36, 0:36])
                last.then_inc(uT_psum.sem, 1)

                def m_rows(h):
                    if h >= 2:
                        pe.wait_ge(decay_exp.sem, decay_exp.at(it, PAIR * (h - 1)))
                    nc.tensor.matmul(bank[2 + h % 2][:], row[:, h], mrow[:], start=True, stop=True).then_inc(mb_psum.sem, 1)

                def qk(k):
                    h, bb = k // PAIR, k % PAIR
                    hs = slice(h * MD, (h + 1) * MD)
                    if k >= 2:
                        pe.wait_ge(c_ready.sem, c_ready.at(it, k - 1))
                    qkb = bank[4 + k % 2]
                    nc.tensor.matmul(qkb[:, 0:S], ctxT[hs, bb * S:bb * S + P], xnT[hs, bb * S:(bb + 1) * S], start=True, stop=True, tile_position=(h * MD, 0))
                    nc.tensor.matmul(qkb[:, S:S + P], ctxT[hs, bb * S + P:(bb + 1) * S], xnT[hs, bb * S + P:(bb + 1) * S],
                                     start=True, stop=True, tile_position=(h * MD, 0)).then_inc(qk_psum.sem, 1)

                def weigh_m(k):
                    h, bb = k // PAIR, k % PAIR
                    pe.wait_ge(c_ready.sem, c_ready.at(it, k + 1))
                    o = bank[6 + bb]
                    g = MD + 1
                    nc.tensor.matmul(o[:, h * g:(h + 1) * g], cT[k % 2][:, 0], ctx_tok[:, 2 * bb, h], start=True, stop=True)
                    nc.tensor.matmul(o[:, (MH + h) * g:(MH + h + 1) * g], cT[k % 2][:, 1], ctx_tok[:, 2 * bb, h], start=True, stop=False)
                    nc.tensor.matmul(o[:, (MH + h) * g:(MH + h + 1) * g], cT[k % 2][:, 2], ctx_tok[:, 2 * bb + 1, h],
                                     start=False, stop=True).then_inc(h_psum.sem, 1)

                m_rows(0)
                qk(0)
                for k in range(MH * PAIR):
                    if k + 1 < MH * PAIR:
                        if (k + 1) % PAIR == 0:
                            m_rows((k + 1) // PAIR)
                        qk(k + 1)
                    weigh_m(k)

                turn(5)
                experts(1)

        @block.vector
        def _(dve):
            dve.wait_ge(weights_in, 16 * LOADS)
            nc.vector.tensor_scalar(b_rnn_half[:], b_rnn[:], 0.5, None, ALU.add).then_inc(setup_done, 1)
            nc.vector.tensor_scalar(bq_scaled[:], b_xqk[:, 0:1], -HD ** -0.5, None, ALU.mult).then_inc(setup_done, 1)
            nc.vector.scalar_tensor_tensor(dscale_abs[:], dscale[:], -1.0, dscale[:], ALU.mult, ALU.max).then_inc(setup_done, 1)
            nc.vector.tensor_scalar(w_l[:, 0], w_l[:, 0], HD ** -0.5, None, ALU.mult).then_inc(setup_done, 1)
            nc.vector.tensor_copy(wg_l[:], wg_raw[:].unsqueeze(2).to_broadcast([P, H, HD])).then_inc(setup_done, 1)
            nc.vector.memset(gk[:], 0.0).then_inc(setup_done, 1)
            dve.wait_ge(setup_done, 12)
            for i in range(2):
                g = slice(32 * i, 32 * i + MH)
                r = slice(MH * i, MH * i + MH)
                nc.vector.tensor_copy(gk[:, 0, g], gk_raw[:, 0, r]).then_inc(setup_done, 1)
                nc.vector.tensor_tensor(gk[:, 1, g], gk_raw[:, 1, r], gk_raw[:, 2, r], ALU.add).then_inc(setup_done, 1)
            dve.wait_ge(setup_done, SETUP_OPS)
            with dve.Fori(0, STEPS) as it:
                steps = [0]

                def link(ins):
                    steps[0] += 1
                    ins.then_inc(dve_step.sem, 1)
                    dve.wait_ge(dve_step.sem, dve_step.at(it, steps[0]))

                def alone():
                    dve.sem_inc(passed_dve, 1)

                def layer_norm(j):
                    for n in range(NT):
                        last = nc.vector.bn_stats(stats[:, n], x[:, n])
                    link(last)
                    alone()
                    for n in range(NT):
                        last = nc.vector.bn_aggr(mv[:, n], stats[:, n])
                    link(last)
                    nc.vector.tensor_scalar(ve[:], mv[:, :, 1], 1e-5, None, ALU.add).then_inc(var_ready.sem, 1)
                    dve.wait_ge(rstd_ready.sem, rstd_ready.at(it, j + 1))
                    for n in range(NT):
                        last = nc.vector.tensor_scalar(xn[:, n], x[:, n], mv[:, n, 0:1], rstd[:, n:n + 1], ALU.subtract, ALU.mult)
                    last.then_inc(xn_ready.sem, 1)

                def add_to_x(src):
                    link(nc.vector.tensor_tensor(x[:], src, x[:], ALU.add))

                def tiles(b):
                    return b[:].rearrange("p (n d) -> p n d", n=NT)

                def route(l):
                    dve.wait_ge(logits_psum.sem, logits_psum.at(it, l + 1))
                    link(nc.vector.tensor_copy(logit[:], bank[5][:, 0:NT * NE].rearrange("p (n e) -> p n e", n=NT)))
                    mine = logit[:].unsqueeze(3).to_broadcast([P, NT, NE, NE])
                    other = logit[:].unsqueeze(2).to_broadcast([P, NT, NE, NE])
                    link(nc.vector.tensor_reduce(top[:], logit[:], AX_X, ALU.max))
                    nc.vector.tensor_tensor(ex[:], logit[:], top[:].unsqueeze(2).to_broadcast([P, NT, NE]), ALU.subtract
                                            ).then_inc(route_in.sem, 1)
                    link(nc.vector.tensor_tensor(cmp_eq[:], other, mine, ALU.is_equal))
                    link(nc.vector.tensor_tensor(cmp_eq[:], cmp_eq[:], lower[:].unsqueeze(1).to_broadcast([P, NT, NE, NE]), ALU.mult))
                    link(nc.vector.tensor_tensor(cmp_gt[:], other, mine, ALU.is_gt))
                    link(nc.vector.tensor_tensor(cmp_gt[:], cmp_gt[:], cmp_eq[:], ALU.add))
                    link(nc.vector.tensor_reduce(cnt[:], cmp_gt[:], AX_X, ALU.add))
                    r = nc.vector.tensor_scalar(sel[:], cnt[:], TOPK - 0.5, None, ALU.is_lt)
                    if l == 0:
                        r.then_inc(sel_ready.sem, 1)
                        dve.wait_ge(sel_ready.sem, sel_ready.at(it, 1))
                    else:
                        link(r)
                    dve.wait_ge(route_exp.sem, route_exp.at(it, l + 1))
                    link(nc.vector.tensor_tensor(ex[:], ex[:], sel[:], ALU.mult))
                    link(nc.vector.tensor_reduce(top[:], ex[:], AX_X, ALU.add))
                    link(nc.vector.reciprocal(top[:], top[:]))
                    r = nc.vector.tensor_tensor(gate[:], ex[:], top[:].unsqueeze(2).to_broadcast([P, NT, NE]), ALU.mult)
                    if l == 1:
                        r.then_inc(gate_ready.sem, 1)
                        dve.wait_ge(gateT_psum.sem, gateT_psum.at(it, 1))
                        nc.vector.tensor_copy(gateT[:], bank[4][0:NE, :]).then_inc(gateT_ready.sem, 1)
                        dve.wait_ge(bias_psum.sem, bias_psum.at(it, 1))
                        add_to_x(tiles(bank[5]))
                    else:
                        link(r)
                        dve.wait_ge(rank_psum.sem, rank_psum.at(it, 1))
                        ranks = bank[4][:, 0:NT * NE].rearrange("p (n e) -> p n e", n=NT)
                        link(nc.vector.tensor_tensor(cnt[:], ranks, taken[:].unsqueeze(1).to_broadcast([P, NT, NE]), ALU.add))
                        link(nc.vector.tensor_tensor(taken[:], bank[4][:, NT * NE:(NT + 1) * NE], taken[:], ALU.add))
                        link(nc.vector.tensor_scalar(cnt[:], cnt[:], CAPACITY - 0.5, None, ALU.is_lt))
                        link(nc.vector.tensor_tensor(gate[:], gate[:], cnt[:], ALU.mult))

                def experts(l):
                    route(l)
                    for e in range(NE):
                        dve.wait_ge(down_psum.sem, down_psum.at(it, l * NE + e + 1))
                        if e >= 1:
                            dve.wait_ge(expert_added.sem, expert_added.at(it, l * NE + e))
                        for n in range(NT):
                            last = nc.vector.scalar_tensor_tensor(x[:, n], bank[6 + e % 2][:, n * P:(n + 1) * P], gate[:, n, e:e + 1],
                                                                  x[:, n], ALU.mult, ALU.add)
                        last.then_inc(expert_added.sem, 1)
                    dve.wait_ge(expert_added.sem, expert_added.at(it, l * NE + NE))

                dve.wait_ge(x_loaded.sem, x_loaded.at(it, 16))
                dve.wait_ge(x_stored.sem, x_stored.at(it, 0))
                nc.vector.tensor_copy(x[:], x_in[:]).then_inc(x_taken.sem, 1)
                dve.wait_ge(x_taken.sem, x_taken.at(it, 1))

                layer_norm(0)
                dve.wait_ge(log_dist.sem, log_dist.at(it, 1))
                nc.vector.tensor_scalar(nb[:], nb[:], dscale_abs[:, 0:1], None, ALU.mult).then_inc(dist_taken.sem, 1)
                for e in range(2):
                    dve.wait_ge(rnn_sig.sem, rnn_sig.at(it, 3 * e + 3))
                    link(nc.vector.scalar_tensor_tensor(g0[e], bank[3 * e + 2][:], b_rnn_half[:, 4 + e:5 + e], sgm[3 * e + 2], ALU.add, ALU.max))
                    link(nc.vector.tensor_tensor(bi[e], sgm[3 * e + 1], g0[e], ALU.mult))
                    for bb in range(PAIR):
                        t = slice(bb * S, (bb + 1) * S)
                        last = nc.vector.tensor_tensor_scan(hT[e][:, t], sgm[3 * e][:, t], bi[e][:, t], 0.5, ALU.mult, ALU.add)
                    last.then_inc(rnn_state.sem, 1)
                dve.wait_ge(rnn_y.sem, rnn_y.at(it, 1))
                add_to_x(tiles(bank[6]))

                layer_norm(1)
                dve.wait_ge(qkv_psum.sem, qkv_psum.at(it, 3))
                nc.vector.tensor_tensor(v_aug[:, :, :, 0:HD], bank[2][:].rearrange("p (n h d) -> p n h d", n=NT, h=H),
                                        bv_row[:].rearrange("p (h d) -> p h d", h=H).unsqueeze(1).to_broadcast([P, NT, H, HD]),
                                        ALU.add).then_inc(v_ready.sem, 1)
                link(nc.vector.tensor_tensor(x[:], x[:], bo_row[:].unsqueeze(1).to_broadcast([P, NT, D]), ALU.add))

                def turned_copy(u):
                    dve.wait_ge(p_turned.sem, p_turned.at(it, u + 1))
                    if u >= 2:
                        dve.wait_ge(pv_done.sem, pv_done.at(it, u - 1))
                    nc.vector.tensor_copy(pT[:, u % 2], bank[3 + u % 2][:]).then_inc(pT_even.sem, 1)

                def normalise(g):
                    dve.wait_ge(pv_done.sem, pv_done.at(it, 8 * (g + 1)))
                    o = bank[5][:, 0:H * (HD + 1)].rearrange("p (h d) -> p h d", h=H)
                    link(nc.vector.reciprocal(rsum[:], o[:, :, HD]))
                    nc.vector.tensor_tensor(attn[:, g].rearrange("p (h d) -> p h d", h=H), o[:, :, 0:HD],
                                            rsum[:].unsqueeze(2).to_broadcast([P, H, HD]), ALU.mult).then_inc(attn_ready.sem, 1)

                for u in range(UNITS):
                    tile = u // 8
                    dve.wait_ge(s_psum.sem, s_psum.at(it, u + 1))
                    if u >= 3:
                        dve.wait_ge(p_ready.sem, p_ready.at(it, u - 2))
                    alone()
                    for j in range(2):
                        last = nc.vector.tensor_tensor_reduce(sc[:, u % 3, j], bank[u % 3][:, j * S:(j + 1) * S], nb[:, tile], 1.0, BIG,
                                                              ALU.add, ALU.min, mneg[:, 2 * u + j:2 * u + j + 1])
                    last.then_inc(s_biased.sem, 1)
                    if u >= 1 and (u - 1) % 2 == 0:
                        turned_copy(u - 1)
                    if u >= 9 and u % 8 == 1:
                        normalise(u // 8 - 1)
                normalise(NT - 1)
                dve.wait_ge(attn_y.sem, attn_y.at(it, 1))
                add_to_x(tiles(bank[6]))

                layer_norm(2)
                dve.wait_ge(xn_ready.sem, xn_ready.at(it, 3))
                link(nc.vector.tensor_tensor(x[:], x[:], xn[:], ALU.add))
                experts(0)

                layer_norm(3)
                for i in range(2):
                    dve.wait_ge(lin_proj.sem, lin_proj.at(it, i + 1))
                    nc.vector.tensor_scalar(tmin[i], bank[i][:], 0.0, None, ALU.min).then_inc(elu_in.sem, 1)
                for i in range(2):
                    dve.wait_ge(elu_exp.sem, elu_exp.at(it, i + 1))
                    nc.vector.scalar_tensor_tensor(phi[i], bank[i][:], 0.0, eluv[i], ALU.max, ALU.add).then_inc(phi_ready.sem, 1)
                dve.wait_ge(lin_vg.sem, lin_vg.at(it, 2))
                for i in range(HD):
                    dve.wait_ge(kb_psum.sem, kb_psum.at(it, i + 1))
                    nc.vector.tensor_tensor(kv[i % 2], bank[4 + i % 2][:], vT, ALU.mult).then_inc(kv_ready.sem, 1)
                    dve.wait_ge(kv_ready.sem, kv_ready.at(it, i + 1))
                    for bb in range(PAIR):
                        t = slice(bb * S, (bb + 1) * S)
                        last = nc.vector.tensor_tensor_scan(st[i % 2][:, t], gT[:, t], kv[i % 2][:, t], 0.0, ALU.mult, ALU.add)
                    link(last)
                    dve.wait_ge(qb_psum.sem, qb_psum.at(it, i + 1))
                    if i >= 2:
                        dve.wait_ge(lin_fold.sem, lin_fold.at(it, i - 1))
                    nc.vector.tensor_tensor(qs[i % 2], bank[2 + i % 2][:], st[i % 2], ALU.mult).then_inc(qs_ready.sem, 1)
                dve.wait_ge(lin_fold.sem, lin_fold.at(it, HD))
                add_to_x(tiles(bank[6]))

                layer_norm(4)
                dve.wait_ge(gates_psum.sem, gates_psum.at(it, 1))
                link(nc.vector.tensor_scalar(fcum[:], bank[0][32:32 + MH, :], gbias[32:32 + MH, 0:1], None, ALU.add))
                nc.vector.scalar_tensor_tensor(fabs[:], fcum[:], -1.0, fcum[:], ALU.mult, ALU.max).then_inc(fabs_ready.sem, 1)
                link(nc.vector.tensor_scalar(fmin[:], fcum[:], 0.0, None, ALU.min))
                link(nc.vector.tensor_scalar(ig[:], bank[0][0:MH, :], gbias[0:MH, 0:1], None, ALU.add))
                dve.wait_ge(fln_ready.sem, fln_ready.at(it, 1))
                for bb in range(PAIR):
                    t = slice(bb * S, (bb + 1) * S)
                    last = nc.vector.tensor_tensor_scan(fcum[:, t], fmin[:, t], fln[:, t], 0.0, ALU.add, ALU.subtract)
                link(last)
                link(nc.vector.tensor_tensor(u36[0:MH, :], ig[:], fcum[:], ALU.subtract))
                for bb in range(PAIR):
                    t = slice(bb * S, (bb + 1) * S)
                    last = nc.vector.tensor_tensor_scan(umax[:, t], u36[0:MH, t], u36[0:MH, t], -BIG, ALU.max, ALU.max)
                link(last)
                nc.vector.tensor_scalar(mrow[:], umax[:], -1.0, None, ALU.mult)
                nc.vector.tensor_tensor(u36[32:32 + MH, :], fcum[:], umax[:], ALU.add).then_inc(m_ready.sem, 1)
                dve.wait_ge(uT_psum.sem, uT_psum.at(it, 1))
                nc.vector.tensor_copy(uT[:], bank[1][:, 0:NT * 36].rearrange("p (n g) -> p n g", n=NT)).then_inc(uT_ready.sem, 1)
                for k in range(MH * PAIR):
                    dve.wait_ge(qk_psum.sem, qk_psum.at(it, k + 1))
                    dve.wait_ge(decay_cut.sem, decay_cut.at(it, k + 1))
                    if k >= 2:
                        dve.wait_ge(h_psum.sem, h_psum.at(it, k - 1))
                    nc.vector.scalar_tensor_tensor(cT[k % 2], bank[4 + k % 2][:, 0:384].rearrange("p (b t) -> p b t", b=3), MD ** -0.5,
                                                   decay[k % 2], ALU.mult, ALU.mult).then_inc(c_ready.sem, 1)
                dve.wait_ge(h_psum.sem, h_psum.at(it, MH * PAIR))
                dve.wait_ge(efm_ready.sem, efm_ready.at(it, 1))
                g = MD + 1
                hb = [bank[6 + bb][:, 0:2 * MH * g].rearrange("p (g d) -> p g d", d=g) for bb in range(PAIR)]
                nrm_g = nrm[:].rearrange("p n h -> p (n h)")
                rn_g = rn[:].rearrange("p n h -> p (n h)")
                for bb in range(PAIR):
                    last = nc.vector.tensor_copy(nrm_g[:, bb * 2 * MH:(bb + 1) * 2 * MH], hb[bb][:, :, MD])
                link(last)
                link(nc.vector.scalar_tensor_tensor(nrm[:], nrm[:], -1.0, nrm[:], ALU.mult, ALU.max))
                link(nc.vector.tensor_tensor(nrm[:], nrm[:], efm[:], ALU.max))
                link(nc.vector.tensor_scalar(nrm[:], nrm[:], 1e-6, None, ALU.add))
                link(nc.vector.reciprocal(rn[:], nrm[:]))
                for bb in range(PAIR):
                    gs = slice(bb * 2 * MH, (bb + 1) * 2 * MH)
                    last = nc.vector.tensor_tensor(hh[:, gs], hb[bb][:, :, 0:MD], rn_g[:, gs].unsqueeze(2).to_broadcast([P, 2 * MH, MD]), ALU.mult)
                link(last)
                NG = NT * MH

                def per_head(v):
                    return v.unsqueeze(2).to_broadcast([P, NG, MD])

                link(nc.vector.tensor_reduce(mstat[:, 0], hh, AX_X, ALU.add))
                link(nc.vector.tensor_scalar(mstat[:, 0], mstat[:, 0], 1.0 / MD, None, ALU.mult))
                link(nc.vector.tensor_tensor(hc, hh, per_head(mstat[:, 0]), ALU.subtract))
                link(nc.vector.tensor_tensor(hsq, hc, hc, ALU.mult))
                link(nc.vector.tensor_reduce(mstat[:, 1], hsq, AX_X, ALU.add))
                nc.vector.tensor_scalar(mstat[:, 2], mstat[:, 1], 1.0 / MD, 1e-6, ALU.mult, ALU.add).then_inc(hvar_ready.sem, 1)
                dve.wait_ge(hrstd_ready.sem, hrstd_ready.at(it, 1))
                link(nc.vector.tensor_tensor(hn, hc, per_head(mstat[:, 3]), ALU.mult))
                hn_t = hn.rearrange("p (n h) d -> p n (h d)", n=NT)
                link(nc.vector.tensor_tensor(hn_t, hn_t, onw[:].unsqueeze(1).to_broadcast([P, NT, D]), ALU.mult))
                nc.vector.tensor_tensor(x[:], hn_t, x[:], ALU.add).then_inc(ctx_taken.sem, 1)
                dve.wait_ge(ctx_taken.sem, ctx_taken.at(it, 1))

                layer_norm(5)
                experts(1)
                assert steps[0] == DVE_STEPS, f"DVE_STEPS is {steps[0]}"


def _layout(inp):
    def put(v):
        return np.ascontiguousarray(v)

    i = {k: np.asarray(v) for k, v in inp.items()}

    def tokens(v):
        return put(v.reshape(STEPS, NT, P, v.shape[-1]).transpose(0, 2, 1, 3))

    eye = np.eye(P, dtype=np.float32)
    pick = np.zeros((H, HD, HD, H, HD), np.float32)
    for h in range(H):
        for k in range(HD):
            pick[h, k, k, h, :] = 1
    row = np.zeros((MH, MH, P), np.float32)
    for h in range(MH):
        row[h, h] = 1
    r = {
        "x": tokens(i["x"]),
        "dist": tokens(i["fside_BxSxS2_0"]),
        "ctx": tokens(i["ctx_1024"]),
        "ctxT": put(i["ctx_1024"].reshape(STEPS, T, D).transpose(0, 2, 1)),
        "ident": eye,
        "earlier": np.triu(np.ones((P, P), np.float32), 1),
        "ones": np.ones((P, P), np.float32),
        "lower": put(np.broadcast_to(np.tril(np.ones((NE, NE), np.float32), -1), (P, NE, NE))),
        "pick": pick.reshape(P, HD, P),
        "row": row,
        "w_rnn": put(i["L0_attn_W"].T),
        "b_rnn": put(i["L0_attn_b"].reshape(NC0, P).T),
        "wd_rnn": put(i["L0_attn_Wd"].T.reshape(E0 // P, P, D).transpose(1, 0, 2)),
        "w_x": put(np.stack([i[f"L0_xattn_W{k}"].T for k in "qkvo"], 1)),
        "b_xqk": put(np.stack([i["L0_xattn_bq"], i["L0_xattn_bk"]], 1)),
        "bv": i["L0_xattn_bv"], "bo": i["L0_xattn_bo"],
        "dscale": i["L0_xattn_distance_scaling"].reshape(1),
        "w_l": put(np.stack([i[f"L1_attn_W{k}"].T for k in "qkvo"], 1)),
        "wg_l": put(i["L1_attn_Wg"].T),
        "bg_l": put(np.broadcast_to(i["L1_attn_bg"].reshape(H, 1), (H, HD)).reshape(P, 1)),
        "w_route": put(np.stack([i["L0_ffn_router_w"].T, i["L1_ffn_Wg"].T], 1)),
        "w_up": put(np.stack([i["L0_ffn_w1"], i["L1_ffn_W1"]])),
        "w_down": put(np.stack([i["L0_ffn_w2"], i["L1_ffn_W2"]])),
        "b_up": put(i["L1_ffn_b1"].reshape(NE * FC, P).T),
        "b_down": i["L1_ffn_b2"],
        "gk_raw": put(np.concatenate([i["L1_xattn_ig_kernel"].reshape(3, P, MH),
                                      i["L1_xattn_fg_kernel"].reshape(3, P, MH)], 2).transpose(1, 0, 2)),
        "gate_bias": put(np.stack([i["L1_xattn_ig_bias"], i["L1_xattn_fg_bias"]]).reshape(2, MH, 1)),
        "onw": put(i["L1_xattn_outnorm_weight"].reshape(D)),
    }
    return r


def kernel(**inputs):
    import concourse.bacc as _bacc
    from concourse.bass_utils import run_bass_kernel_spmd as _run

    nc = _bacc.Bacc("TRN2", target_bir_lowering=False, num_devices=1)
    arrays = {f"in_{k}": v for k, v in _layout(inputs).items()}
    aps = {k[3:]: nc.dram_tensor(k, v.shape, mybir.dt.from_np(v.dtype), kind="ExternalInput").ap()
           for k, v in arrays.items()}
    out = nc.dram_tensor("out_x", (STEPS, P, NT, D), F32, kind="ExternalOutput").ap()
    decoder(nc, aps, out)
    r = _run(nc, [arrays], core_ids=[0])
    got = r.results[0]["out_x"]
    return np.ascontiguousarray(got.transpose(0, 2, 1, 3)).reshape(B, S, D)
```

```python
from contextlib import ExitStack
from functools import partial

import numpy as np

import concourse.bass as bass
from concourse import mybir

F32 = mybir.dt.float32
BF16 = mybir.dt.bfloat16
ALU = mybir.AluOpType
ACT = mybir.ActivationFunctionType
AX_X = mybir.AxisListType.X

P = 128
B, S, D = 8, 256, 128
NT = S // P
E0 = 256
EH = E0 // P
H, HD = 16, 8
NE, FF = 8, 512
FC = FF // P
TOPK = 2
CAPACITY = int(1.25 * B * S * TOPK / NE) + 1
MH, MD = 4, 32
PARTS = 3
PAIRS = PARTS * PARTS
GROUP = 32
UNITS = NT * (H // 2)
BIG = 3.0e38


def side_by_side(*lanes):
    at = [[next(g, None), n, g] for n, g in enumerate(lanes)]
    while any(x[0] is not None for x in at):
        x = min((x for x in at if x[0] is not None), key=lambda x: (x[0], x[1]))
        x[0] = next(x[2], None)


def one_by_one(*blocks):
    for b in blocks:
        yield from b


def in_order(steps):
    for place, step in sorted(steps, key=lambda x: x[0]):
        yield place
        step()


def within(block, first, last):
    for place in block:
        yield first + (last - first) * place


class Signal:

    def __init__(self, nc, ctx, name, per, base=0):
        self.sem = ctx.enter_context(nc.semaphore(name))
        self.per = per
        self.base = base

    def at(self, k, n):
        assert n > 0 or self.base > 0, "a wait must be against a value above zero"
        return k * self.per + (self.base + n)


def decoder(nc, a, out):
    with ExitStack() as ctx:
        def sb(name, shape, dt=F32):
            return ctx.enter_context(nc.sbuf_tensor(name, shape, dt))

        def sig(name, per, base=0):
            return Signal(nc, ctx, name, per, base)

        bank = [ctx.enter_context(nc.psum_tensor(f"bank{i}", [P, 512], F32)) for i in range(8)]

        ident = sb("ident", [P, P])
        earlier = sb("earlier", [P, P])
        ones = sb("ones", [P, P])
        lower = sb("lower", [P, NE, NE])
        pick = sb("pick", [P, HD, P])
        of_head = sb("of_head", [H, D])
        row = sb("row", [MH, MH, P])
        w_rnn = sb("w_rnn", [P, 3 * E0])
        b_rnn = sb("b_rnn", [P, 3 * EH])
        b_rnn_half = sb("b_rnn_half", [P, 3 * EH])
        wd_rnn = sb("wd_rnn", [P, E0 // P, D])
        w_x = sb("w_x", [P, 4, D])
        b_xqk = sb("b_xqk", [P, 2])
        bq_scaled = sb("bq_scaled", [P, 1])
        bv_row = sb("bv_row", [P, D])
        bo_row = sb("bo_row", [P, D])
        dscale = sb("dscale", [P, 1])
        dscale_abs = sb("dscale_abs", [P, 1])
        tiny = sb("tiny", [P, 1])
        w_l = sb("w_l", [P, 4, D])
        wg_l = sb("wg_l", [P, H, HD])
        wg_raw = sb("wg_raw", [P, H])
        bg_l = sb("bg_l", [P, 1])
        w_route = sb("w_route", [P, 2, NE])
        w_up = sb("w_up", [P, 2, NE, FF])
        w_down = sb("w_down", [P, 2, NE, FC, D])
        b_up = sb("b_up", [P, NE * FC])
        b_down = sb("b_down", [NE, D])
        gk_raw = sb("gk_raw", [P, 3, 2 * MH])
        gk = sb("gk", [P, 2, 36])
        gbias = sb("gbias", [36, 1])
        onw = sb("onw", [P, MH * MD])

        x_in = sb("x_in", [P, NT, D])
        x_e0 = sb("x_e0", [P, NT, D])
        x_mid = sb("x_mid", [P, NT, D])
        x_lin = sb("x_lin", [P, NT, D])
        x_e1 = sb("x_e1", [P, NT, D])

        class Norm:

            def __init__(self, name):
                self.stats = sb(name + "_stats", [P, NT, 6])
                self.mv = sb(name + "_mv", [P, NT, 2])
                self.ve = sb(name + "_ve", [P, NT])
                self.rstd = sb(name + "_rstd", [P, NT])
                self.xn = sb(name + "_xn", [P, NT, D])
                self.xnT = sb(name + "_xnT", [P, S])

        nf, ne, nm = Norm("nf"), Norm("ne"), Norm("nm")
        norms = [nf, nf, ne, nm, nm, ne]
        mix = sb("mix", [P, 20 * S])

        def scratch(first, *shape, rows=P):
            n = int(np.prod(shape))
            v = mix[0:rows, first * S:first * S + n]
            if len(shape) == 2:
                return v.rearrange("p (a b) -> p a b", b=shape[1])
            return v.rearrange("p (a b c) -> p a b c", b=shape[1], c=shape[2]) if len(shape) == 3 else v

        mhalf = sb("mhalf", [P, NT * MH])
        dist = sb("dist", [P, NT, S])
        nb = sb("nb", [P, NT, S])
        ctxT_f = sb("ctxT_f", [P, S])
        qr = sb("qr", [PAIRS * HD, H, S], BF16)
        kr = sb("kr", [PAIRS * HD, H, S], BF16)
        qk_p = sb("qk_p", [P, 2, PARTS, S], BF16)
        v_pad = sb("v_pad", [P, NT, H, 2 * GROUP - HD])
        sc = scratch(14, 3, 2, S)
        mneg = sb("mneg", [P, UNITS * 2])
        prob = sb("prob", [P, 3, 2, S])
        pT = sb("pT", [P, 2, 2 * S])
        esum = sb("esum", [P, UNITS * 2])
        rsum = sb("rsum", [P, UNITS * 2])
        rsumT = sb("rsumT", [H, S])
        attnT = sb("attnT", [P, S])
        sf = scratch(0, EH, S)
        si = scratch(2, EH, S)
        sh = scratch(4, EH, S)
        g0 = scratch(6, EH, S)
        bi = scratch(8, EH, S)
        hT = scratch(10, EH, S)
        qk_f = scratch(12, 2, S)
        hid = sb("hid", [P, NE, FC, S])
        logit = sb("logit", [P, NT, NE])
        cmp_gt = sb("cmp_gt", [P, NT, NE, NE])
        cmp_eq = sb("cmp_eq", [P, NT, NE, NE])
        cnt = sb("cnt", [P, NT, NE])
        sel = sb("sel", [P, NT, NE])
        top = sb("top", [P, NT])
        ex = sb("ex", [P, NT, NE])
        gate = sb("gate", [P, NT, NE])
        taken = sb("taken", [P, NE])
        gateT = sb("gateT", [NE, S])
        tmin = scratch(0, 2, S)
        eluv = scratch(2, 2, S)
        phi = scratch(4, 2, S)
        vT = scratch(6, S)
        gT = scratch(7, S)
        kv = scratch(8, 2, 2, S)
        st = scratch(12, 2, 2, S)
        qs = scratch(16, 2, 2, S)
        ctxT = sb("ctxT", [P, S])
        ctx_tok = sb("ctx_tok", [P, NT, MH, MD + 1])
        rows = scratch(0, 8, S, rows=MH)
        ig, fsum, fmin, fabs, fln, fcum, umax, mrow = (rows[:, i] for i in range(8))
        u36 = sb("u36", [36, S])
        uT = sb("uT", [P, NT, 36])
        efm = sb("efm", [P, NT, MH])
        decay = scratch(8, 2, 3, P)
        cT = scratch(11, 2, 3, P)
        nrm = sb("nrm", [P, NT, MH])
        rn = sb("rn", [P, NT, MH])
        hh = scratch(14, NT * MH, MD)
        hc = scratch(15, NT * MH, MD)
        hsq = scratch(16, NT * MH, MD)
        hn = scratch(17, NT * MH, MD)
        mstat = sb("mstat", [P, 4, NT * MH])

        bounce_q = nc.dram_tensor("bounce_q", (2 * PARTS - 1, P, S), BF16, kind="Internal").ap()
        bounce_k = nc.dram_tensor("bounce_k", (PARTS, P, S), BF16, kind="Internal").ap()

        passed_dve = ctx.enter_context(nc.semaphore("passed_dve"))
        passed_pool = ctx.enter_context(nc.semaphore("passed_pool"))
        weights_in = ctx.enter_context(nc.semaphore("weights_in"))
        setup_done = ctx.enter_context(nc.semaphore("setup_done"))
        dve_step = ctx.enter_context(nc.semaphore("dve_step"))
        experts_loaded = ctx.enter_context(nc.semaphore("experts_loaded"))
        rank_read = sig("rank_read", 1)
        front_loaded = sig("front_loaded", 32)
        ctx_loaded = sig("ctx_loaded", 16 * (1 + NT))
        dist_loaded = sig("dist_loaded", 16)
        front_done = sig("front_done", 1, base=1)
        dist_taken = sig("dist_taken", 1, base=1)
        ctx_taken = sig("ctx_taken", 1, base=1)
        x_stored = sig("x_stored", 16, base=16)
        var_ready = [sig(f"var_ready{j}", 1) for j in range(6)]
        rstd_ready = [sig(f"rstd_ready{j}", 1) for j in range(6)]
        xn_ready = [sig(f"xn_ready{j}", 1) for j in range(6)]
        xnT_psum = [sig(f"xnT_psum{j}", 1) for j in range(6)]
        xnT_ready = [sig(f"xnT_ready{j}", 1) for j in range(6)]
        rnn_proj = sig("rnn_proj", 3 * EH)
        rnn_sig = sig("rnn_sig", 3 * EH)
        rnn_state = sig("rnn_state", EH)
        rnn_y = sig("rnn_y", 1)
        log_dist = sig("log_dist", 1)
        qkv_psum = sig("qkv_psum", 3)
        qk_sb = sig("qk_sb", 2)
        parts_ready = sig("parts_ready", 1)
        bounced = sig("bounced", 48)
        qr_in = sig("qr_in", 32 * PARTS)
        v_ready = sig("v_ready", 1)
        s_psum = sig("s_psum", UNITS)
        s_biased = sig("s_biased", UNITS)
        p_ready = sig("p_ready", UNITS)
        p_turned = sig("p_turned", UNITS)
        pT_even = sig("pT_even", UNITS // 2)
        pT_odd = sig("pT_odd", UNITS // 2)
        pT_ready = [pT_even, pT_odd]
        pv_done = sig("pv_done", UNITS)
        rsum_ready = sig("rsum_ready", 1)
        rsumT_psum = sig("rsumT_psum", 1)
        rsumT_ready = sig("rsumT_ready", 1)
        rspread = sig("rspread", 1)
        oT_ready = sig("oT_ready", 1)
        attnT_ready = sig("attnT_ready", 1)
        attn_y = sig("attn_y", 1)
        logits_psum = [sig(f"logits_psum{l}", 1) for l in range(2)]
        route_in = [sig(f"route_in{l}", 1) for l in range(2)]
        route_exp = [sig(f"route_exp{l}", 1) for l in range(2)]
        sel_ready = sig("sel_ready", 1)
        rank_psum = sig("rank_psum", 1)
        up_psum = [sig(f"up_psum{l}", NE * FC // 2) for l in range(2)]
        hid_ready = [sig(f"hid_ready{l}", NE * FC // 2) for l in range(2)]
        tanh_ready = sig("tanh_ready", NE * FC // 2)
        down_psum = [sig(f"down_psum{l}", NE) for l in range(2)]
        expert_added = [sig(f"expert_added{l}", NE) for l in range(2)]
        gate_ready = sig("gate_ready", 1)
        gateT_psum = sig("gateT_psum", 1)
        gateT_ready = sig("gateT_ready", 1)
        bias_psum = sig("bias_psum", 1)
        bias_added = sig("bias_added", 1)
        lin_proj = sig("lin_proj", 4)
        elu_in = sig("elu_in", 2)
        elu_exp = sig("elu_exp", 2)
        phi_ready = sig("phi_ready", 2)
        lin_vg = sig("lin_vg", 2)
        kb_psum = sig("kb_psum", HD // 2)
        qb_psum = sig("qb_psum", HD // 2)
        kv_ready = sig("kv_ready", HD // 2)
        qs_ready = sig("qs_ready", HD // 2)
        lin_fold = sig("lin_fold", HD // 2)
        gates_psum = sig("gates_psum", 1)
        fabs_ready = sig("fabs_ready", 1)
        fexp_ready = sig("fexp_ready", 1)
        fln_ready = sig("fln_ready", 1)
        m_ready = sig("m_ready", 1)
        uT_psum = sig("uT_psum", 1)
        uT_ready = sig("uT_ready", 1)
        efm_ready = sig("efm_ready", 1)
        mb_psum = sig("mb_psum", MH)
        qk_psum = sig("qk_psum", MH)
        decay_exp = sig("decay_exp", MH)
        decay_cut = sig("decay_cut", MH)
        c_ready = sig("c_ready", MH)
        h_psum = sig("h_psum", MH)
        hvar_ready = sig("hvar_ready", 1)
        hrstd_ready = sig("hrstd_ready", 1)

        def unit_at(u):
            return 0.26 + 0.68 * u / UNITS

        OPEN_DOWNS = [5, 6]
        NORM_AT, TURN_AT = [0.035, 0.11], [0.05, 0.13]
        ROUTE_AT, CHOICE_AT, GATE_AT = [0.07, 0.165], [0.10, 0.27], [0.105, 0.28]
        UP_AT = [[0.08, 0.09, 0.11, 0.22, 0.43, 0.44, 0.50, 0.52],
                 [0.17, 0.175, 0.202, 0.204, 0.206, 0.208, 0.22, 0.23]]
        RANK_AT = [0.53, 0.30]
        DOWN_AT = [[0.54, 0.57, 0.75, 0.85, 0.92, 0.01, 0.08, 0.10],
                   [0.34, 0.42, 0.50, 0.58, 0.66, 0.74, 0.01, 0.03]]

        def lin_at(i):
            return 0.14 + 0.06 * i

        def head_at(h):
            return 0.70 + 0.05 * h

        def course(eng, front, middle, opening, closing):
            side_by_side(front(0))
            side_by_side(front(1), one_by_one(within(opening(0, 0), -1, 0), closing(0, 0)))
            side_by_side(middle(0), opening(0, 1))
            with eng.Fori(0, B - 2) as k:
                side_by_side(front(k + 2), one_by_one(closing(0, k + 1), opening(1, k)))
                side_by_side(middle(k + 1), one_by_one(closing(1, k), opening(0, k + 2)))
            side_by_side(closing(0, B - 1))
            side_by_side(middle(B - 1), one_by_one(within(opening(1, B - 2), -0.1, 0.85), within(closing(1, B - 2), 0.85, 0.9)))
            side_by_side(one_by_one(opening(1, B - 1), closing(1, B - 1)))

        setup_loads = []

        def setup_load(eng, dst, src):
            setup_loads.append(1)
            eng.dma_start(dst, src).then_inc(weights_in, 16)

        SETUP_OPS = 16
        block = ctx.enter_context(nc.Block())

        @block.sync
        def _(sp):
            for s in (front_done, dist_taken, ctx_taken, x_stored):
                sp.sem_inc(s.sem, s.base)

            def load_front(k):
                sp.wait_ge(front_done.sem, front_done.at(k, 0))
                sp.dma_start(x_in[:], a["x"][bass.ds(k, 1)].rearrange("o p n d -> p (o n) d")).then_inc(front_loaded.sem, 16)
                sp.dma_start(ctxT_f[:], a["ctxT"][bass.ds(k, 1)].rearrange("o p t -> p (o t)")).then_inc(front_loaded.sem, 16)
                sp.wait_ge(dist_taken.sem, dist_taken.at(k, 0))
                sp.dma_start(dist[:], a["dist"][bass.ds(k, 1)].rearrange("o p n k -> p (o n) k")).then_inc(dist_loaded.sem, 16)

            load_front(0)
            for dst, name in ((ident, "ident"), (w_rnn, "w_rnn"), (b_rnn, "b_rnn"),
                              (wd_rnn, "wd_rnn"), (w_x, "w_x"), (b_xqk, "b_xqk"),
                              (earlier, "earlier"), (ones, "ones"), (lower, "lower"),
                              (pick, "pick"), (row, "row"), (of_head, "of_head"), (w_l, "w_l"), (wg_raw, "wg_l"), (bg_l, "bg_l"),
                              (w_route, "w_route"), (b_up, "b_up"), (b_down, "b_down"), (gk_raw, "gk_raw")):
                setup_load(sp, dst[:], a[name])
            setup_load(sp, gbias[0:MH, :], a["gate_bias"][0])
            setup_load(sp, gbias[32:32 + MH, :], a["gate_bias"][1])
            for dst, name in ((bv_row, "bv"), (bo_row, "bo"), (dscale, "dscale"), (onw, "onw")):
                setup_load(sp, dst[:], a[name].partition_broadcast(P))

            def experts_in(l):
                sp.dma_start(w_up[:, l], a["w_up"][l].rearrange("e d f -> d e f")).then_inc(experts_loaded, 16)
                sp.dma_start(w_down[:, l], a["w_down"][l].rearrange("e (c p) d -> p e c d", p=P)).then_inc(experts_loaded, 16)

            def bounce_qk(k):
                sp.wait_ge(parts_ready.sem, parts_ready.at(k, 1))
                sp.dma_start(bounce_q[0:PARTS].rearrange("a p t -> p a t"), qk_p[:, 0]).then_inc(bounced.sem, 16)
                sp.dma_start(bounce_q[PARTS:].rearrange("a p t -> p a t"), qk_p[:, 0, 0:PARTS - 1]).then_inc(bounced.sem, 16)
                sp.dma_start(bounce_k.rearrange("a p t -> p a t"), qk_p[:, 1]).then_inc(bounced.sem, 16)
                sp.wait_ge(bounced.sem, bounced.at(k, 48))
                for s in range(PARTS):
                    block_rows = slice(s * PARTS * HD, (s + 1) * PARTS * HD)
                    for dst, src in ((qr, bounce_q[s:s + PARTS]), (kr, bounce_k)):
                        sp.dma_start(dst[block_rows], src.rearrange("a (d h) t -> (a d) h t", h=H)).then_inc(qr_in.sem, 16)

            def load_middle(k):
                sp.wait_ge(ctx_taken.sem, ctx_taken.at(k, 0))
                sp.dma_start(ctxT[:], a["ctxT"][bass.ds(k, 1)].rearrange("o p t -> p (o t)")).then_inc(ctx_loaded.sem, 16)
                for n in range(NT):
                    sp.dma_start(ctx_tok[:, n, :, 0:MD], a["ctx"][bass.ds(k, 1), :, n].rearrange("o p (h d) -> p (o h) d", h=MH)
                                 ).then_inc(ctx_loaded.sem, 16)

            def store(k):
                sp.wait_ge(expert_added[1].sem, expert_added[1].at(k, NE))
                sp.dma_start(out[bass.ds(k, 1)].rearrange("o p n d -> p (o n) d"), x_e1[:]).then_inc(x_stored.sem, 16)

            experts_in(0)
            bounce_qk(0)
            load_front(1)
            experts_in(1)
            bounce_qk(1)
            load_middle(0)
            load_front(2)
            with sp.Fori(0, B - 3) as k:
                load_middle(k + 1)
                bounce_qk(k + 2)
                load_front(k + 3)
                store(k)
            load_middle(B - 2)
            bounce_qk(B - 1)
            store(B - 3)
            load_middle(B - 1)
            store(B - 2)
            store(B - 1)
            sp.wait_ge(x_stored.sem, 16 * B + x_stored.base)

        LOADS = len(setup_loads)

        @block.gpsimd
        def _(pool):
            nc.gpsimd.memset(mhalf[:], -0.5).then_inc(setup_done, 1)
            nc.gpsimd.memset(tiny[:], 1e-9).then_inc(setup_done, 1)
            nc.gpsimd.memset(v_pad[:], 0.0).then_inc(setup_done, 1)
            nc.gpsimd.memset(ctx_tok[:, :, :, MD:MD + 1], 1.0).then_inc(setup_done, 1)
            nc.gpsimd.memset(u36[:], 0.0).then_inc(setup_done, 1)
            nc.gpsimd.memset(taken[:], 0.0).then_inc(setup_done, 1)
            pool.wait_ge(setup_done, SETUP_OPS)

            def inverse_root(j, k):
                pool.wait_ge(var_ready[j].sem, var_ready[j].at(k, 1))
                nc.gpsimd.tensor_tensor(norms[j].rstd[:], norms[j].ve[:], mhalf[:, 0:NT], ALU.pow).then_inc(rstd_ready[j].sem, 1)

            def front(k):
                yield 0.0
                inverse_root(0, k)
                yield 0.18
                inverse_root(1, k)

            def opening(l, k):
                yield NORM_AT[l]
                inverse_root(2 if l == 0 else 5, k)

            def closing(l, k):
                yield from ()

            def middle(k):
                yield 0.0
                inverse_root(3, k)
                yield 0.44
                inverse_root(4, k)
                for h in range(MH):
                    yield head_at(h)
                    pool.wait_ge(decay_exp.sem, decay_exp.at(k, h + 1))
                    pool.sem_inc(passed_pool, 1)
                    d = decay[:, h % 2, 0:3:2, :]
                    nc.gpsimd.affine_select(out=d, in_=d, compare_op=ALU.is_ge, fill=0.0, base=0,
                                            pattern=[[0, 2], [1, P]], channel_multiplier=-1).then_inc(decay_cut.sem, 1)
                yield 0.93
                pool.wait_ge(hvar_ready.sem, hvar_ready.at(k, 1))
                nc.gpsimd.tensor_tensor(mstat[:, 3], mstat[:, 2], mhalf[:], ALU.pow).then_inc(hrstd_ready.sem, 1)

            course(pool, front, middle, opening, closing)

        @block.scalar
        def _(act):
            act.wait_ge(setup_done, SETUP_OPS)

            def turn_out(j, src, k):
                act.wait_ge(xnT_psum[j].sem, xnT_psum[j].at(k, 1))
                nc.scalar.copy(norms[j].xnT[:], src[:, 0:S]).then_inc(xnT_ready[j].sem, 1)

            def front(k):
                yield 0.0
                act.wait_ge(dist_loaded.sem, dist_loaded.at(k, 16))
                nc.scalar.activation(nb[:], dist[:], ACT.Ln, bias=tiny[:, 0:1]).then_inc(log_dist.sem, 1)
                yield 0.03
                turn_out(0, bank[7], k)
                yield 0.06
                for c in range(3 * EH):
                    act.wait_ge(rnn_proj.sem, rnn_proj.at(k, (c // EH + 1) * EH))
                    nc.scalar.activation((sf, si, sh)[c // EH][:, c % EH], bank[3 + c // EH][:, (c % EH) * S:(c % EH + 1) * S],
                                         ACT.Sigmoid, bias=b_rnn[:, c:c + 1]).then_inc(rnn_sig.sem, 1)
                yield 0.20
                turn_out(1, bank[7], k)
                act.wait_ge(qkv_psum.sem, qkv_psum.at(k, 1))
                nc.scalar.activation(qk_f[:, 0], bank[3][:, 0:S], ACT.Identity, bias=bq_scaled[:, 0:1],
                                     scale=-HD ** -0.5).then_inc(qk_sb.sem, 1)
                act.wait_ge(qkv_psum.sem, qkv_psum.at(k, 2))
                nc.scalar.activation(qk_f[:, 1], bank[4][:, 0:S], ACT.Identity, bias=b_xqk[:, 1:2]).then_inc(qk_sb.sem, 1)

                def turned_copy(u):
                    act.wait_ge(p_turned.sem, p_turned.at(k, u + 1))
                    if u >= 2:
                        act.wait_ge(pv_done.sem, pv_done.at(k, u - 1))
                    nc.scalar.copy(pT[:, u % 2], bank[5 + u % 2][:]).then_inc(pT_odd.sem, 1)

                for u in range(UNITS):
                    yield unit_at(u)
                    act.wait_ge(s_biased.sem, s_biased.at(k, u + 1))
                    if u >= 3:
                        act.wait_ge(p_turned.sem, p_turned.at(k, u - 2))
                    for j in range(2):
                        last = nc.scalar.activation(prob[:, u % 3, j], sc[:, u % 3, j], ACT.Exp, scale=-1.0,
                                                    bias=mneg[:, 2 * u + j:2 * u + j + 1],
                                                    accum_out=esum[:, 2 * u + j:2 * u + j + 1])
                    last.then_inc(p_ready.sem, 1)
                    if u >= 1 and (u - 1) % 2 == 1:
                        turned_copy(u - 1)
                yield 0.95
                turned_copy(UNITS - 1)
                yield 0.97
                act.wait_ge(pv_done.sem, pv_done.at(k, UNITS))
                nc.scalar.copy(attnT[:], bank[7][:, 0:S]).then_inc(oT_ready.sem, 1)

            def hidden(l, k, e):
                for c2 in range(FC // 2):
                    up = bank[c2][:].rearrange("p (c t) -> p c t", c=2)
                    act.wait_ge(up_psum[l].sem, up_psum[l].at(k, e * FC // 2 + c2 + 1))
                    if l == 0:
                        nc.scalar.activation(hid[:, e, 2 * c2:2 * c2 + 2], up, ACT.Tanh, scale=0.5).then_inc(tanh_ready.sem, 1)
                    else:
                        for c in range(2):
                            f = e * FC + 2 * c2 + c
                            last = nc.scalar.activation(hid[:, e, 2 * c2 + c], up[:, c], ACT.Gelu, bias=b_up[:, f:f + 1])
                        last.then_inc(hid_ready[l].sem, 1)

            def opening(l, k):
                yield TURN_AT[l] + 0.01
                turn_out(2 if l == 0 else 5, bank[0], k)

                def choice():
                    act.wait_ge(route_in[l].sem, route_in[l].at(k, 1))
                    nc.scalar.activation(ex[:], ex[:], ACT.Exp).then_inc(route_exp[l].sem, 1)

                yield from in_order([(CHOICE_AT[l] + 0.001, choice)] + [(UP_AT[l][e], partial(hidden, l, k, e)) for e in range(NE)])

            def closing(l, k):
                yield from ()

            def middle(k):
                yield 0.03
                turn_out(3, bank[7], k)
                yield 0.08
                for i in range(2):
                    act.wait_ge(elu_in.sem, elu_in.at(k, i + 1))
                    nc.scalar.activation(eluv[:, i], tmin[:, i], ACT.Exp).then_inc(elu_exp.sem, 1)
                act.wait_ge(lin_proj.sem, lin_proj.at(k, 3))
                nc.scalar.copy(vT, bank[5][:, 0:S]).then_inc(lin_vg.sem, 1)
                act.wait_ge(lin_proj.sem, lin_proj.at(k, 4))
                nc.scalar.activation(gT, bank[6][:, 0:S], ACT.Sigmoid, bias=bg_l[:, 0:1]).then_inc(lin_vg.sem, 1)
                yield 0.46
                turn_out(4, bank[7], k)
                yield 0.53
                act.wait_ge(fabs_ready.sem, fabs_ready.at(k, 1))
                nc.scalar.activation(fabs, fabs, ACT.Exp, scale=-1.0).then_inc(fexp_ready.sem, 1)
                act.wait_ge(fexp_ready.sem, fexp_ready.at(k, 1))
                nc.scalar.activation(fln, fabs, ACT.Ln, bias=1.0).then_inc(fln_ready.sem, 1)
                yield 0.66
                act.wait_ge(uT_ready.sem, uT_ready.at(k, 1))
                nc.scalar.activation(efm[:], uT[:, :, 32:32 + MH], ACT.Exp, scale=-1.0).then_inc(efm_ready.sem, 1)
                for h in range(MH):
                    yield head_at(h)
                    act.wait_ge(mb_psum.sem, mb_psum.at(k, 2 * (h // 2) + 2))
                    if h >= 2:
                        act.wait_ge(c_ready.sem, c_ready.at(k, h - 1))
                    mb = bank[5 + h // 2][:, (h % 2) * S:(h % 2 + 1) * S]
                    nc.scalar.activation(decay[:, h % 2, 0:2, :], mb.rearrange("p (b t) -> p b t", b=2), ACT.Exp, bias=uT[:, 0, h:h + 1])
                    nc.scalar.activation(decay[:, h % 2, 2, :], mb[:, P:S], ACT.Exp, bias=uT[:, 1, h:h + 1]).then_inc(decay_exp.sem, 1)

            course(act, front, middle, opening, closing)

        @block.tensor
        def _(pe):
            pe.wait_ge(weights_in, 16 * LOADS)
            pe.wait_ge(setup_done, SETUP_OPS)

            def alone():
                pe.wait_ge(setup_done, SETUP_OPS)

            def tok(n):
                return slice(n * P, (n + 1) * P)

            def half(n):
                return slice(n * S, (n + 1) * S)

            def turn(j, dst, k):
                pe.wait_ge(xn_ready[j].sem, xn_ready[j].at(k, 1))
                for n in range(NT):
                    last = nc.tensor.transpose(dst[:, tok(n)], norms[j].xn[:, n], ident[:])
                last.then_inc(xnT_psum[j].sem, 1)

            def front(k):
                yield 0.02
                turn(0, bank[7], k)
                yield 0.05
                pe.wait_ge(xnT_ready[0].sem, xnT_ready[0].at(k, 1))
                for c in range(3 * EH):
                    nc.tensor.matmul(bank[3 + c // EH][:, half(c % EH)], w_rnn[:, c * P:(c + 1) * P], nf.xnT[:],
                                     start=True, stop=True).then_inc(rnn_proj.sem, 1)
                yield 0.14
                pe.wait_ge(rnn_state.sem, rnn_state.at(k, EH))
                for n in range(NT):
                    for e in range(EH):
                        last = nc.tensor.matmul(bank[6][:, tok(n)], hT[:, e, tok(n)], wd_rnn[:, e], start=(e == 0), stop=(e == EH - 1))
                last.then_inc(rnn_y.sem, 1)
                yield 0.19
                turn(1, bank[7], k)
                pe.wait_ge(front_loaded.sem, front_loaded.at(k, 32))
                nc.tensor.matmul(bank[4][:, 0:S], w_x[:, 1], ctxT_f[:], start=True, stop=True)
                for n in range(NT):
                    nc.tensor.matmul(bank[5][:, tok(n)], ctxT_f[:, tok(n)], w_x[:, 2], start=True, stop=True)
                pe.wait_ge(xnT_ready[1].sem, xnT_ready[1].at(k, 1))
                nc.tensor.matmul(bank[3][:, 0:S], w_x[:, 0], nf.xnT[:], start=True, stop=True).then_inc(qkv_psum.sem, 3)

                def scores(u):
                    qt, hp = u // (H // 2), u % (H // 2)
                    if u >= 2:
                        pe.wait_ge(s_biased.sem, s_biased.at(k, u - 1))
                    for j in range(2):
                        h = 2 * hp + j
                        last = nc.tensor.matmul(bank[3 + u % 2][:, half(j)], qr[:, h, tok(qt)], kr[:, h, :], start=True, stop=True)
                    last.then_inc(s_psum.sem, 1)

                def turn_probs(u):
                    pe.wait_ge(p_ready.sem, p_ready.at(k, u + 1))
                    if u >= 2:
                        pe.wait_ge(pT_ready[u % 2].sem, pT_ready[u % 2].at(k, u // 2))
                    for j in range(2):
                        for kt in range(NT):
                            last = nc.tensor.transpose(bank[5 + u % 2][:, tok(NT * j + kt)], prob[:, u % 3, j, tok(kt)], ident[:])
                    last.then_inc(p_turned.sem, 1)

                def weigh(u):
                    qt, hp = u // (H // 2), u % (H // 2)
                    pe.wait_ge(pT_ready[u % 2].sem, pT_ready[u % 2].at(k, u // 2 + 1))
                    for j in range(2):
                        g, m = divmod(2 * hp + j, GROUP // HD)
                        for kt in range(NT):
                            last = nc.tensor.matmul(bank[7][g * GROUP:(g + 1) * GROUP, tok(qt)],
                                                    v_pad[:, kt, 2 * hp + j, GROUP - (m + 1) * HD:2 * GROUP - (m + 1) * HD],
                                                    pT[:, u % 2, tok(NT * j + kt)], start=(m == 0 and kt == 0),
                                                    stop=(m == GROUP // HD - 1 and kt == NT - 1), tile_position=(0, g * GROUP))
                    last.then_inc(pv_done.sem, 1)

                yield 0.25
                pe.wait_ge(v_ready.sem, v_ready.at(k, 1))
                pe.wait_ge(qr_in.sem, qr_in.at(k, 32 * PARTS))
                scores(0)
                for u in range(UNITS):
                    yield unit_at(u)
                    if u + 1 < UNITS:
                        scores(u + 1)
                    if u >= 1:
                        turn_probs(u - 1)
                    if u >= 2:
                        weigh(u - 2)
                yield 0.945
                turn_probs(UNITS - 1)
                weigh(UNITS - 2)
                yield 0.96
                weigh(UNITS - 1)
                yield 0.962
                pe.wait_ge(rsum_ready.sem, rsum_ready.at(k, 1))
                for n in range(NT):
                    last = nc.tensor.transpose(bank[3][0:H, tok(n)], rsum[:, n * H:(n + 1) * H], ident[:])
                last.then_inc(rsumT_psum.sem, 1)
                yield 0.966
                pe.wait_ge(rsumT_ready.sem, rsumT_ready.at(k, 1))
                nc.tensor.matmul(bank[4][:, 0:S], of_head[:], rsumT[:], start=True, stop=True).then_inc(rspread.sem, 1)
                yield 0.985
                pe.wait_ge(attnT_ready.sem, attnT_ready.at(k, 1))
                for n in range(NT):
                    last = nc.tensor.matmul(bank[3][:, tok(n)], attnT[:, tok(n)], w_x[:, 3], start=True, stop=True)
                last.then_inc(attn_y.sem, 1)

            def up(l, k, e):
                for c in range(FC):
                    if e >= 1 and c % 2 == 0:
                        pe.wait_ge(hid_ready[l].sem, hid_ready[l].at(k, (e - 1) * FC // 2 + c // 2 + 1))
                    last = nc.tensor.matmul(bank[c // 2][:, half(c % 2)], w_up[:, l, e, c * P:(c + 1) * P], ne.xnT[:],
                                            start=True, stop=True)
                    if c % 2 == 1:
                        last.then_inc(up_psum[l].sem, 1)

            def down(l, k, e):
                if e >= 1:
                    pe.wait_ge(expert_added[l].sem, expert_added[l].at(k, e))
                elif l == 0:
                    pe.wait_ge(rank_read.sem, rank_read.at(k, 1))
                else:
                    pe.wait_ge(bias_added.sem, bias_added.at(k, 1))
                pe.wait_ge(hid_ready[l].sem, hid_ready[l].at(k, (e + 1) * FC // 2))
                for n in range(NT):
                    for c in range(FC):
                        last = nc.tensor.matmul(bank[2][:, tok(n)], hid[:, e, c, tok(n)],
                                                w_down[:, l, e, c], start=(c == 0), stop=(c == FC - 1))
                last.then_inc(down_psum[l].sem, 1)

            def opening(l, k):
                j = 2 if l == 0 else 5
                yield TURN_AT[l]
                turn(j, bank[0], k)
                yield ROUTE_AT[l]
                pe.wait_ge(xnT_ready[j].sem, xnT_ready[j].at(k, 1))
                for n in range(NT):
                    last = nc.tensor.matmul(bank[2][:, n * NE:(n + 1) * NE], ne.xnT[:, tok(n)], w_route[:, l], start=True, stop=True)
                last.then_inc(logits_psum[l].sem, 1)
                pe.wait_ge(experts_loaded, 32 * (l + 1))

                def rank():
                    pe.wait_ge(sel_ready.sem, sel_ready.at(k, 1))
                    for n in range(NT):
                        r = bank[2][:, n * NE:(n + 1) * NE]
                        for m in range(n):
                            nc.tensor.matmul(r, ones[:], sel[:, m], start=(m == 0), stop=False)
                        nc.tensor.matmul(r, earlier[:], sel[:, n], start=(n == 0), stop=True)
                    for m in range(NT):
                        last = nc.tensor.matmul(bank[2][:, NT * NE:(NT + 1) * NE], ones[:], sel[:, m],
                                                start=(m == 0), stop=(m == NT - 1))
                    last.then_inc(rank_psum.sem, 1)

                def turn_gates():
                    pe.wait_ge(gate_ready.sem, gate_ready.at(k, 1))
                    for n in range(NT):
                        last = nc.tensor.transpose(bank[2][0:NE, tok(n)], gate[:, n], ident[:])
                    last.then_inc(gateT_psum.sem, 1)

                def bias_of_down():
                    pe.wait_ge(gateT_ready.sem, gateT_ready.at(k, 1))
                    for n in range(NT):
                        last = nc.tensor.matmul(bank[2][:, S + n * P:S + (n + 1) * P], gateT[:, tok(n)], b_down[:], start=True, stop=True)
                    last.then_inc(bias_psum.sem, 1)

                others = [(RANK_AT[l], rank)] if l == 0 else [(RANK_AT[l], turn_gates), (RANK_AT[l] + 0.03, bias_of_down)]
                yield from in_order(others + [(UP_AT[l][e], partial(up, l, k, e)) for e in range(NE)]
                                    + [(DOWN_AT[l][e], partial(down, l, k, e)) for e in range(OPEN_DOWNS[l])])

            def closing(l, k):
                yield from in_order([(DOWN_AT[l][e], partial(down, l, k, e)) for e in range(OPEN_DOWNS[l], NE)])

            def middle(k):
                yield 0.02
                turn(3, bank[7], k)
                yield 0.05
                pe.wait_ge(xnT_ready[3].sem, xnT_ready[3].at(k, 1))
                for i, w in enumerate((w_l[:, 0], w_l[:, 1], w_l[:, 2], wg_l[:].rearrange("p h j -> p (h j)"))):
                    nc.tensor.matmul(bank[3 + i][:, 0:S], w, nm.xnT[:], start=True, stop=True).then_inc(lin_proj.sem, 1)

                def spread_k(i):
                    if i >= 2:
                        pe.wait_ge(kv_ready.sem, kv_ready.at(k, i - 1))
                    for r in range(2):
                        last = nc.tensor.matmul(bank[3 + i % 2][:, half(r)], pick[:, 2 * i + r], phi[:, 1], start=True, stop=True)
                    last.then_inc(kb_psum.sem, 1)

                def spread_q(i):
                    if i >= 2:
                        pe.wait_ge(qs_ready.sem, qs_ready.at(k, i - 1))
                    for r in range(2):
                        last = nc.tensor.matmul(bank[5 + i % 2][:, half(r)], pick[:, 2 * i + r], phi[:, 0], start=True, stop=True)
                    last.then_inc(qb_psum.sem, 1)

                def fold(i):
                    pe.wait_ge(qs_ready.sem, qs_ready.at(k, i + 1))
                    for r in range(2):
                        for n in range(NT):
                            last = nc.tensor.matmul(bank[7][:, tok(n)], qs[:, i % 2, r, tok(n)], w_l[:, 3],
                                                    start=(i == 0 and r == 0 and n == 0), stop=(i == HD // 2 - 1 and r == 1),
                                                    skip_group_check=True)
                    last.then_inc(lin_fold.sem, 1)

                yield 0.12
                pe.wait_ge(phi_ready.sem, phi_ready.at(k, 2))
                pe.wait_ge(lin_vg.sem, lin_vg.at(k, 2))
                spread_k(0)
                spread_q(0)
                for i in range(HD // 2):
                    yield lin_at(i)
                    if i + 1 < HD // 2:
                        spread_k(i + 1)
                        spread_q(i + 1)
                    if i >= 1:
                        fold(i - 1)
                yield 0.40
                fold(HD // 2 - 1)

                yield 0.45
                turn(4, bank[7], k)
                yield 0.48
                pe.wait_ge(ctx_loaded.sem, ctx_loaded.at(k, ctx_loaded.per))
                pe.wait_ge(xnT_ready[4].sem, xnT_ready[4].at(k, 1))
                nc.tensor.matmul(bank[3][0:36, 0:S], gk[:, 0], nm.xnT[:], start=True, stop=False)
                nc.tensor.matmul(bank[3][0:36, 0:S], gk[:, 1], ctxT[:], start=False, stop=True).then_inc(gates_psum.sem, 1)
                yield 0.60
                alone()
                pe.wait_ge(m_ready.sem, m_ready.at(k, 1))
                for n in range(NT):
                    last = nc.tensor.transpose(bank[7][:, n * 36:(n + 1) * 36], u36[:, tok(n)], ident[0:36, 0:36])
                last.then_inc(uT_psum.sem, 1)
                for h in range(MH):
                    nc.tensor.matmul(bank[5 + h // 2][:, half(h % 2)], row[:, h], mrow, start=True, stop=True).then_inc(mb_psum.sem, 1)

                def qk(h):
                    hs = slice(h * MD, (h + 1) * MD)
                    if h >= 2:
                        pe.wait_ge(c_ready.sem, c_ready.at(k, h - 1))
                    qkb = bank[3 + h % 2]
                    nc.tensor.matmul(qkb[:, 0:S], ctxT[hs, 0:P], nm.xnT[hs, :], start=True, stop=True, tile_position=(h * MD, 0))
                    nc.tensor.matmul(qkb[:, S:S + P], ctxT[hs, P:S], nm.xnT[hs, P:S],
                                     start=True, stop=True, tile_position=(h * MD, 0)).then_inc(qk_psum.sem, 1)

                def weigh_m(h):
                    pe.wait_ge(c_ready.sem, c_ready.at(k, h + 1))
                    g = MD + 1
                    nc.tensor.matmul(bank[7][:, h * g:(h + 1) * g], cT[:, h % 2, 0], ctx_tok[:, 0, h], start=True, stop=True)
                    nc.tensor.matmul(bank[7][:, (MH + h) * g:(MH + h + 1) * g], cT[:, h % 2, 1], ctx_tok[:, 0, h], start=True, stop=False)
                    nc.tensor.matmul(bank[7][:, (MH + h) * g:(MH + h + 1) * g], cT[:, h % 2, 2], ctx_tok[:, 1, h],
                                     start=False, stop=True).then_inc(h_psum.sem, 1)

                qk(0)
                for h in range(MH):
                    yield head_at(h)
                    if h + 1 < MH:
                        qk(h + 1)
                    if h >= 1:
                        weigh_m(h - 1)
                yield 0.90
                weigh_m(MH - 1)

            course(pe, front, middle, opening, closing)

        @block.vector
        def _(dve):
            dve.wait_ge(weights_in, 16 * LOADS)
            nc.vector.tensor_scalar(b_rnn_half[:], b_rnn[:], 0.5, None, ALU.add).then_inc(setup_done, 1)
            nc.vector.tensor_scalar(bq_scaled[:], b_xqk[:, 0:1], -HD ** -0.5, None, ALU.mult).then_inc(setup_done, 1)
            nc.vector.scalar_tensor_tensor(dscale_abs[:], dscale[:], -1.0, dscale[:], ALU.mult, ALU.max).then_inc(setup_done, 1)
            nc.vector.tensor_scalar(w_l[:, 0], w_l[:, 0], HD ** -0.5, None, ALU.mult).then_inc(setup_done, 1)
            nc.vector.tensor_copy(wg_l[:], wg_raw[:].unsqueeze(2).to_broadcast([P, H, HD])).then_inc(setup_done, 1)
            nc.vector.memset(gk[:], 0.0).then_inc(setup_done, 1)
            dve.wait_ge(setup_done, 12)
            for i in range(2):
                g = slice(32 * i, 32 * i + MH)
                r = slice(MH * i, MH * i + MH)
                nc.vector.tensor_copy(gk[:, 0, g], gk_raw[:, 0, r]).then_inc(setup_done, 1)
                nc.vector.tensor_tensor(gk[:, 1, g], gk_raw[:, 1, r], gk_raw[:, 2, r], ALU.add).then_inc(setup_done, 1)
            dve.wait_ge(setup_done, SETUP_OPS)

            class Chain:

                before, here = 0, 0

            LOOP_LINKS = 66

            def link(ins):
                Chain.here += 1
                ins.then_inc(dve_step, 1)
                dve.wait_ge(dve_step, Chain.before + Chain.here)

            def alone():
                dve.sem_inc(passed_dve, 1)

            def layer_norm(j, x, k):
                b = norms[j]
                for n in range(NT):
                    last = nc.vector.bn_stats(b.stats[:, n], x[:, n])
                link(last)
                alone()
                for n in range(NT):
                    last = nc.vector.bn_aggr(b.mv[:, n], b.stats[:, n])
                link(last)
                nc.vector.tensor_scalar(b.ve[:], b.mv[:, :, 1], 1e-5, None, ALU.add).then_inc(var_ready[j].sem, 1)

            def normalised(j, x, k):
                b = norms[j]
                dve.wait_ge(rstd_ready[j].sem, rstd_ready[j].at(k, 1))
                for n in range(NT):
                    last = nc.vector.tensor_scalar(b.xn[:, n], x[:, n], b.mv[:, n, 0:1], b.rstd[:, n:n + 1], ALU.subtract, ALU.mult)
                last.then_inc(xn_ready[j].sem, 1)

            def tiles(b):
                return b[:, 0:S].rearrange("p (n d) -> p n d", n=NT)

            def front(k):
                yield 0.0
                dve.wait_ge(front_loaded.sem, front_loaded.at(k, 32))
                layer_norm(0, x_in, k)
                yield 0.015
                normalised(0, x_in, k)
                yield 0.07
                dve.wait_ge(log_dist.sem, log_dist.at(k, 1))
                nc.vector.tensor_scalar(nb[:], nb[:], dscale_abs[:, 0:1], None, ALU.mult).then_inc(dist_taken.sem, 1)
                yield 0.09
                dve.wait_ge(rnn_sig.sem, rnn_sig.at(k, 3 * EH))
                for e in range(EH):
                    last = nc.vector.scalar_tensor_tensor(g0[:, e], bank[5][:, e * S:(e + 1) * S], b_rnn_half[:, 2 * EH + e:2 * EH + e + 1],
                                                          sh[:, e], ALU.add, ALU.max)
                link(last)
                link(nc.vector.tensor_tensor(bi, si, g0, ALU.mult))
                for e in range(EH):
                    nc.vector.tensor_tensor_scan(hT[:, e], sf[:, e], bi[:, e], 0.5, ALU.mult, ALU.add).then_inc(rnn_state.sem, 1)
                yield 0.16
                dve.wait_ge(rnn_y.sem, rnn_y.at(k, 1))
                link(nc.vector.tensor_tensor(x_in[:], tiles(bank[6]), x_in[:], ALU.add))

                layer_norm(1, x_in, k)
                yield 0.185
                normalised(1, x_in, k)
                yield 0.21
                dve.wait_ge(qk_sb.sem, qk_sb.at(k, 2))
                link(nc.vector.tensor_copy(qk_p[:, :, 0], qk_f[:]))
                link(nc.vector.tensor_tensor(qk_f[:], qk_f[:], qk_p[:, :, 0], ALU.subtract))
                link(nc.vector.tensor_copy(qk_p[:, :, 1], qk_f[:]))
                nc.vector.tensor_tensor(qk_p[:, :, 2], qk_f[:], qk_p[:, :, 1], ALU.subtract).then_inc(parts_ready.sem, 1)
                dve.wait_ge(qkv_psum.sem, qkv_psum.at(k, 3))
                nc.vector.tensor_tensor(v_pad[:, :, :, GROUP - HD:GROUP], bank[5][:, 0:S].rearrange("p (n h d) -> p n h d", n=NT, h=H),
                                        bv_row[:].rearrange("p (h d) -> p h d", h=H).unsqueeze(1).to_broadcast([P, NT, H, HD]),
                                        ALU.add).then_inc(v_ready.sem, 1)
                link(nc.vector.tensor_tensor(x_in[:], x_in[:], bo_row[:].unsqueeze(1).to_broadcast([P, NT, D]), ALU.add))

                def turned_copy(u):
                    dve.wait_ge(p_turned.sem, p_turned.at(k, u + 1))
                    if u >= 2:
                        dve.wait_ge(pv_done.sem, pv_done.at(k, u - 1))
                    nc.vector.tensor_copy(pT[:, u % 2], bank[5 + u % 2][:]).then_inc(pT_even.sem, 1)

                for u in range(UNITS):
                    yield unit_at(u)
                    dve.wait_ge(s_psum.sem, s_psum.at(k, u + 1))
                    if u >= 3:
                        dve.wait_ge(p_ready.sem, p_ready.at(k, u - 2))
                    alone()
                    for j in range(2):
                        last = nc.vector.tensor_tensor_reduce(sc[:, u % 3, j], bank[3 + u % 2][:, j * S:(j + 1) * S],
                                                              nb[:, u // (H // 2)], 1.0, BIG,
                                                              ALU.add, ALU.min, mneg[:, 2 * u + j:2 * u + j + 1])
                    last.then_inc(s_biased.sem, 1)
                    if u >= 1 and (u - 1) % 2 == 0:
                        turned_copy(u - 1)
                yield 0.961
                dve.wait_ge(p_ready.sem, p_ready.at(k, UNITS))
                nc.vector.reciprocal(rsum[:], esum[:]).then_inc(rsum_ready.sem, 1)
                yield 0.963
                dve.wait_ge(rsumT_psum.sem, rsumT_psum.at(k, 1))
                nc.vector.tensor_copy(rsumT[:], bank[3][0:H, 0:S]).then_inc(rsumT_ready.sem, 1)
                yield 0.98
                dve.wait_ge(rspread.sem, rspread.at(k, 1))
                dve.wait_ge(oT_ready.sem, oT_ready.at(k, 1))
                nc.vector.tensor_tensor(attnT[:], attnT[:], bank[4][:, 0:S], ALU.mult).then_inc(attnT_ready.sem, 1)
                yield 0.99
                dve.wait_ge(attn_y.sem, attn_y.at(k, 1))
                nc.vector.tensor_tensor(x_e0[:], tiles(bank[3]), x_in[:], ALU.add).then_inc(front_done.sem, 1)

            def opening(l, k):
                j = 2 if l == 0 else 5
                x = x_e0 if l == 0 else x_e1
                yield NORM_AT[l]
                if l == 0:
                    dve.wait_ge(front_done.sem, front_done.at(k, 1))
                else:
                    dve.wait_ge(ctx_taken.sem, ctx_taken.at(k, 1))
                layer_norm(j, x, k)
                yield NORM_AT[l] + 0.02
                normalised(j, x, k)
                if l == 0:
                    dve.wait_ge(xn_ready[2].sem, xn_ready[2].at(k, 1))
                    link(nc.vector.tensor_tensor(x[:], x[:], ne.xn[:], ALU.add))

                def choose():
                    dve.wait_ge(logits_psum[l].sem, logits_psum[l].at(k, 1))
                    link(nc.vector.tensor_copy(logit[:], bank[2][:, 0:NT * NE].rearrange("p (n e) -> p n e", n=NT)))
                    mine = logit[:].unsqueeze(3).to_broadcast([P, NT, NE, NE])
                    other = logit[:].unsqueeze(2).to_broadcast([P, NT, NE, NE])
                    link(nc.vector.tensor_reduce(top[:], logit[:], AX_X, ALU.max))
                    nc.vector.tensor_tensor(ex[:], logit[:], top[:].unsqueeze(2).to_broadcast([P, NT, NE]), ALU.subtract
                                            ).then_inc(route_in[l].sem, 1)
                    link(nc.vector.tensor_tensor(cmp_eq[:], other, mine, ALU.is_equal))
                    nc.vector.tensor_tensor(cmp_gt[:], other, mine, ALU.is_gt)
                    link(nc.vector.tensor_tensor(cmp_eq[:], cmp_eq[:], lower[:].unsqueeze(1).to_broadcast([P, NT, NE, NE]), ALU.mult))
                    link(nc.vector.tensor_tensor(cmp_gt[:], cmp_gt[:], cmp_eq[:], ALU.add))
                    link(nc.vector.tensor_reduce(cnt[:], cmp_gt[:], AX_X, ALU.add))
                    r = nc.vector.tensor_scalar(sel[:], cnt[:], TOPK - 0.5, None, ALU.is_lt)
                    if l == 0:
                        r.then_inc(sel_ready.sem, 1)
                        dve.wait_ge(sel_ready.sem, sel_ready.at(k, 1))
                    else:
                        link(r)

                def gates():
                    dve.wait_ge(route_exp[l].sem, route_exp[l].at(k, 1))
                    link(nc.vector.tensor_tensor(ex[:], ex[:], sel[:], ALU.mult))
                    link(nc.vector.tensor_reduce(top[:], ex[:], AX_X, ALU.add))
                    link(nc.vector.reciprocal(top[:], top[:]))
                    r = nc.vector.tensor_tensor(gate[:], ex[:], top[:].unsqueeze(2).to_broadcast([P, NT, NE]), ALU.mult)
                    if l == 1:
                        r.then_inc(gate_ready.sem, 1)
                    else:
                        link(r)

                def gates_out():
                    dve.wait_ge(gateT_psum.sem, gateT_psum.at(k, 1))
                    nc.vector.tensor_copy(gateT[:], bank[2][0:NE, 0:S]).then_inc(gateT_ready.sem, 1)

                def add_bias():
                    dve.wait_ge(bias_psum.sem, bias_psum.at(k, 1))
                    nc.vector.tensor_tensor(x[:], bank[2][:, S:2 * S].rearrange("p (n d) -> p n d", n=NT), x[:], ALU.add
                                            ).then_inc(bias_added.sem, 1)
                    dve.wait_ge(bias_added.sem, bias_added.at(k, 1))

                def keep():
                    dve.wait_ge(rank_psum.sem, rank_psum.at(k, 1))
                    ranks = bank[2][:, 0:NT * NE].rearrange("p (n e) -> p n e", n=NT)
                    link(nc.vector.tensor_tensor(cnt[:], ranks, taken[:].unsqueeze(1).to_broadcast([P, NT, NE]), ALU.add))
                    nc.vector.tensor_tensor(taken[:], bank[2][:, NT * NE:(NT + 1) * NE], taken[:], ALU.add).then_inc(rank_read.sem, 1)
                    link(nc.vector.tensor_scalar(cnt[:], cnt[:], CAPACITY - 0.5, 0.5, ALU.is_lt, ALU.mult))
                    link(nc.vector.tensor_tensor(gate[:], gate[:], cnt[:], ALU.mult))

                def silu(e):
                    for c2 in range(FC // 2):
                        dve.wait_ge(tanh_ready.sem, tanh_ready.at(k, e * FC // 2 + c2 + 1))
                        h = hid[:, e, 2 * c2:2 * c2 + 2]
                        nc.vector.scalar_tensor_tensor(h, h, 1.0, bank[c2][:].rearrange("p (c t) -> p c t", c=2),
                                                       ALU.add, ALU.mult).then_inc(hid_ready[0].sem, 1)

                steps = [(CHOICE_AT[l], choose), (GATE_AT[l], gates)]
                if l == 0:
                    steps += [(RANK_AT[l] + 0.01, keep)] + [(UP_AT[l][e] + 0.004, partial(silu, e)) for e in range(NE)]
                else:
                    steps += [(RANK_AT[l] + 0.01, gates_out), (RANK_AT[l] + 0.035, add_bias)]
                yield from in_order(steps + [(DOWN_AT[l][e] + 0.003, partial(add_expert, l, k, e)) for e in range(OPEN_DOWNS[l])])

            def add_expert(l, k, e):
                x = x_e0 if l == 0 else x_e1
                dve.wait_ge(down_psum[l].sem, down_psum[l].at(k, e + 1))
                if e >= 1:
                    dve.wait_ge(expert_added[l].sem, expert_added[l].at(k, e))
                to = x_mid if l == 0 and e == NE - 1 else x
                for n in range(NT):
                    last = nc.vector.scalar_tensor_tensor(to[:, n], bank[2][:, n * P:(n + 1) * P],
                                                          gate[:, n, e:e + 1], x[:, n], ALU.mult, ALU.add)
                last.then_inc(expert_added[l].sem, 1)

            def closing(l, k):
                yield from in_order([(DOWN_AT[l][e] + 0.003, partial(add_expert, l, k, e)) for e in range(OPEN_DOWNS[l], NE)])

            def middle(k):
                yield 0.0
                dve.wait_ge(expert_added[0].sem, expert_added[0].at(k, NE))
                layer_norm(3, x_mid, k)
                yield 0.015
                normalised(3, x_mid, k)
                yield 0.07
                for i in range(2):
                    dve.wait_ge(lin_proj.sem, lin_proj.at(k, i + 1))
                    nc.vector.tensor_scalar(tmin[:, i], bank[3 + i][:, 0:S], 0.0, None, ALU.min).then_inc(elu_in.sem, 1)
                yield 0.09
                for i in range(2):
                    dve.wait_ge(elu_exp.sem, elu_exp.at(k, i + 1))
                    nc.vector.scalar_tensor_tensor(phi[:, i], bank[3 + i][:, 0:S], 0.0, eluv[:, i], ALU.max, ALU.add).then_inc(phi_ready.sem, 1)
                dve.wait_ge(lin_vg.sem, lin_vg.at(k, 2))
                for i in range(HD // 2):
                    yield lin_at(i)
                    dve.wait_ge(kb_psum.sem, kb_psum.at(k, i + 1))
                    nc.vector.tensor_tensor(kv[:, i % 2], bank[3 + i % 2][:].rearrange("p (r t) -> p r t", r=2),
                                            vT.unsqueeze(1).to_broadcast([P, 2, S]), ALU.mult).then_inc(kv_ready.sem, 1)
                    dve.wait_ge(kv_ready.sem, kv_ready.at(k, i + 1))
                    for r in range(2):
                        last = nc.vector.tensor_tensor_scan(st[:, i % 2, r], gT, kv[:, i % 2, r], 0.0, ALU.mult, ALU.add)
                    link(last)
                    dve.wait_ge(qb_psum.sem, qb_psum.at(k, i + 1))
                    if i >= 2:
                        dve.wait_ge(lin_fold.sem, lin_fold.at(k, i - 1))
                    nc.vector.tensor_tensor(qs[:, i % 2], bank[5 + i % 2][:].rearrange("p (r t) -> p r t", r=2), st[:, i % 2],
                                            ALU.mult).then_inc(qs_ready.sem, 1)
                yield 0.42
                dve.wait_ge(lin_fold.sem, lin_fold.at(k, HD // 2))
                link(nc.vector.tensor_tensor(x_lin[:], tiles(bank[7]), x_mid[:], ALU.add))

                layer_norm(4, x_lin, k)
                yield 0.445
                normalised(4, x_lin, k)
                yield 0.50
                dve.wait_ge(gates_psum.sem, gates_psum.at(k, 1))
                link(nc.vector.tensor_scalar(fsum, bank[3][32:32 + MH, 0:S], gbias[32:32 + MH, 0:1], None, ALU.add))
                nc.vector.scalar_tensor_tensor(fabs, fsum, -1.0, fsum, ALU.mult, ALU.max).then_inc(fabs_ready.sem, 1)
                nc.vector.tensor_scalar(fmin, fsum, 0.0, None, ALU.min)
                link(nc.vector.tensor_scalar(ig, bank[3][0:MH, 0:S], gbias[0:MH, 0:1], None, ALU.add))
                yield 0.55
                dve.wait_ge(fln_ready.sem, fln_ready.at(k, 1))
                link(nc.vector.tensor_tensor_scan(fcum, fmin, fln, 0.0, ALU.add, ALU.subtract))
                link(nc.vector.tensor_tensor(u36[0:MH, :], ig, fcum, ALU.subtract))
                link(nc.vector.tensor_tensor_scan(umax, u36[0:MH, :], u36[0:MH, :], -BIG, ALU.max, ALU.max))
                nc.vector.tensor_scalar(mrow, umax, -1.0, None, ALU.mult)
                nc.vector.tensor_tensor(u36[32:32 + MH, :], fcum, umax, ALU.add).then_inc(m_ready.sem, 1)
                yield 0.63
                dve.wait_ge(uT_psum.sem, uT_psum.at(k, 1))
                nc.vector.tensor_copy(uT[:], bank[7][:, 0:NT * 36].rearrange("p (n g) -> p n g", n=NT)).then_inc(uT_ready.sem, 1)
                for h in range(MH):
                    yield head_at(h)
                    dve.wait_ge(qk_psum.sem, qk_psum.at(k, h + 1))
                    dve.wait_ge(decay_cut.sem, decay_cut.at(k, h + 1))
                    if h >= 2:
                        dve.wait_ge(h_psum.sem, h_psum.at(k, h - 1))
                    nc.vector.scalar_tensor_tensor(cT[:, h % 2], bank[3 + h % 2][:, 0:3 * P].rearrange("p (b t) -> p b t", b=3), MD ** -0.5,
                                                   decay[:, h % 2], ALU.mult, ALU.mult).then_inc(c_ready.sem, 1)
                yield 0.91
                dve.wait_ge(h_psum.sem, h_psum.at(k, MH))
                dve.wait_ge(efm_ready.sem, efm_ready.at(k, 1))
                NG = NT * MH
                hb = bank[7][:, 0:NG * (MD + 1)].rearrange("p (g d) -> p g d", d=MD + 1)
                nrm_g = nrm[:].rearrange("p n h -> p (n h)")
                rn_g = rn[:].rearrange("p n h -> p (n h)")

                def per_head(v):
                    return v.unsqueeze(2).to_broadcast([P, NG, MD])

                link(nc.vector.tensor_copy(nrm_g, hb[:, :, MD]))
                link(nc.vector.scalar_tensor_tensor(nrm[:], nrm[:], -1.0, nrm[:], ALU.mult, ALU.max))
                link(nc.vector.tensor_tensor(nrm[:], nrm[:], efm[:], ALU.max))
                link(nc.vector.tensor_scalar(nrm[:], nrm[:], 1e-6, None, ALU.add))
                link(nc.vector.reciprocal(rn[:], nrm[:]))
                link(nc.vector.tensor_tensor(hh, hb[:, :, 0:MD], per_head(rn_g), ALU.mult))
                link(nc.vector.tensor_reduce(mstat[:, 0], hh, AX_X, ALU.add))
                link(nc.vector.tensor_scalar(mstat[:, 0], mstat[:, 0], 1.0 / MD, None, ALU.mult))
                link(nc.vector.tensor_tensor(hc, hh, per_head(mstat[:, 0]), ALU.subtract))
                link(nc.vector.tensor_tensor(hsq, hc, hc, ALU.mult))
                link(nc.vector.tensor_reduce(mstat[:, 1], hsq, AX_X, ALU.add))
                nc.vector.tensor_scalar(mstat[:, 2], mstat[:, 1], 1.0 / MD, 1e-6, ALU.mult, ALU.add).then_inc(hvar_ready.sem, 1)
                yield 0.95
                dve.wait_ge(hrstd_ready.sem, hrstd_ready.at(k, 1))
                link(nc.vector.tensor_tensor(hn, hc, per_head(mstat[:, 3]), ALU.mult))
                hn_t = hn.rearrange("p (n h) d -> p n (h d)", n=NT)
                link(nc.vector.tensor_tensor(hn_t, hn_t, onw[:].unsqueeze(1).to_broadcast([P, NT, D]), ALU.mult))
                yield 0.96
                dve.wait_ge(x_stored.sem, x_stored.at(k, 0))
                nc.vector.tensor_tensor(x_e1[:], hn_t, x_lin[:], ALU.add).then_inc(ctx_taken.sem, 1)

            side_by_side(front(0))
            side_by_side(front(1), one_by_one(within(opening(0, 0), -1, 0), closing(0, 0)))
            side_by_side(middle(0), opening(0, 1))
            first = Chain.here
            with dve.Fori(0, B - 2) as k:
                Chain.before, Chain.here = k * LOOP_LINKS + first, 0
                side_by_side(front(k + 2), one_by_one(closing(0, k + 1), opening(1, k)))
                side_by_side(middle(k + 1), one_by_one(closing(1, k), opening(0, k + 2)))
                assert Chain.here == LOOP_LINKS, f"LOOP_LINKS is {Chain.here}"
            Chain.before, Chain.here = first + (B - 2) * LOOP_LINKS, 0
            side_by_side(closing(0, B - 1))
            side_by_side(middle(B - 1), one_by_one(within(opening(1, B - 2), -0.1, 0.85), within(closing(1, B - 2), 0.85, 0.9)))
            side_by_side(one_by_one(opening(1, B - 1), closing(1, B - 1)))


def _layout(inp):
    def put(v):
        return np.ascontiguousarray(v)

    i = {k: np.asarray(v) for k, v in inp.items()}

    def tokens(v):
        return put(v.reshape(B, NT, P, v.shape[-1]).transpose(0, 2, 1, 3))

    def by_feature(v):
        return v.reshape(H, HD, -1).swapaxes(0, 1).reshape(v.shape)

    eye = np.eye(P, dtype=np.float32)
    pick = np.zeros((H, HD, HD, H, HD), np.float32)
    for h in range(H):
        for k in range(HD):
            pick[h, k, k, h, :] = 1
    of_head = np.repeat(np.eye(H, dtype=np.float32), HD, axis=1)
    row = np.zeros((MH, MH, P), np.float32)
    for h in range(MH):
        row[h, h] = 1
    r = {
        "x": tokens(i["x"]),
        "dist": tokens(i["fside_BxSxS2_0"]),
        "ctx": tokens(i["ctx_1024"]),
        "ctxT": put(i["ctx_1024"].transpose(0, 2, 1)),
        "ident": eye,
        "earlier": np.triu(np.ones((P, P), np.float32), 1),
        "ones": np.ones((P, P), np.float32),
        "lower": put(np.broadcast_to(np.tril(np.ones((NE, NE), np.float32), -1), (P, NE, NE))),
        "pick": pick.reshape(P, HD, P),
        "row": row,
        "of_head": of_head,
        "w_rnn": put(i["L0_attn_W"].T),
        "b_rnn": put(i["L0_attn_b"].reshape(3 * EH, P).T),
        "wd_rnn": put(i["L0_attn_Wd"].T.reshape(E0 // P, P, D).transpose(1, 0, 2)),
        "w_x": put(np.stack([(by_feature(i[f"L0_xattn_W{k}"]) if k in "qk" else i[f"L0_xattn_W{k}"]).T for k in "qkvo"], 1)),
        "b_xqk": put(np.stack([by_feature(i["L0_xattn_bq"]), by_feature(i["L0_xattn_bk"])], 1)),
        "bv": i["L0_xattn_bv"], "bo": i["L0_xattn_bo"],
        "dscale": i["L0_xattn_distance_scaling"].reshape(1),
        "w_l": put(np.stack([i[f"L1_attn_W{k}"].T for k in "qkvo"], 1)),
        "wg_l": put(i["L1_attn_Wg"].T),
        "bg_l": put(np.broadcast_to(i["L1_attn_bg"].reshape(H, 1), (H, HD)).reshape(P, 1)),
        "w_route": put(np.stack([i["L0_ffn_router_w"].T, i["L1_ffn_Wg"].T], 1)),
        "w_up": put(np.stack([i["L0_ffn_w1"], i["L1_ffn_W1"]])),
        "w_down": put(np.stack([i["L0_ffn_w2"], i["L1_ffn_W2"]])),
        "b_up": put(i["L1_ffn_b1"].reshape(NE * FC, P).T),
        "b_down": i["L1_ffn_b2"],
        "gk_raw": put(np.concatenate([i["L1_xattn_ig_kernel"].reshape(3, P, MH),
                                      i["L1_xattn_fg_kernel"].reshape(3, P, MH)], 2).transpose(1, 0, 2)),
        "gate_bias": put(np.stack([i["L1_xattn_ig_bias"], i["L1_xattn_fg_bias"]]).reshape(2, MH, 1)),
        "onw": put(i["L1_xattn_outnorm_weight"].reshape(D)),
    }
    return r


def kernel(**inputs):
    import concourse.bacc as _bacc
    from concourse.bass_utils import run_bass_kernel_spmd as _run

    nc = _bacc.Bacc("TRN2", target_bir_lowering=False, num_devices=1)
    arrays = {f"in_{k}": v for k, v in _layout(inputs).items()}
    aps = {k[3:]: nc.dram_tensor(k, v.shape, mybir.dt.from_np(v.dtype), kind="ExternalInput").ap()
           for k, v in arrays.items()}
    out = nc.dram_tensor("out_x", (B, P, NT, D), F32, kind="ExternalOutput").ap()
    decoder(nc, aps, out)
    r = _run(nc, [arrays], core_ids=[0])
    got = r.results[0]["out_x"]
    return np.ascontiguousarray(got.transpose(0, 2, 1, 3)).reshape(B, S, D)
```

```python
from contextlib import ExitStack

import numpy as np

import concourse.bass as bass
from concourse import mybir

F32 = mybir.dt.float32
BF16 = mybir.dt.bfloat16
ALU = mybir.AluOpType
ACT = mybir.ActivationFunctionType
AX_X = mybir.AxisListType.X

P = 128
B, S, D = 8, 256, 128
NT = S // P
E0 = 256
EH = E0 // P
H, HD = 16, 8
NE, FF = 8, 512
FC = FF // P
TOPK = 2
CAPACITY = int(1.25 * B * S * TOPK / NE) + 1
MH, MD = 4, 32
PARTS = 3
PAIRS = PARTS * PARTS
GROUP = 32
UNITS = NT * (H // 2)
BIG = 3.0e38


def together(*lanes):
    at = [[next(g, None), n, g] for n, g in enumerate(lanes)]
    while any(x[0] is not None for x in at):
        x = min((x for x in at if x[0] is not None), key=lambda x: (x[0], x[1]))
        yield x[0]
        x[0] = next(x[2], None)


def side_by_side(*lanes):
    for _ in together(*lanes):
        pass


def one_by_one(*blocks):
    for b in blocks:
        yield from b


def within(block, first, last):
    for place in block:
        yield first + (last - first) * place


class Signal:

    def __init__(self, nc, ctx, name, per, base=0):
        self.sem = ctx.enter_context(nc.semaphore(name))
        self.per = per
        self.base = base

    def at(self, k, n):
        assert n > 0 or self.base > 0, "a wait must be against a value above zero"
        return k * self.per + (self.base + n)


def decoder(nc, a, out):
    with ExitStack() as ctx:
        def sb(name, shape, dt=F32):
            return ctx.enter_context(nc.sbuf_tensor(name, shape, dt))

        def sig(name, per, base=0):
            return Signal(nc, ctx, name, per, base)

        bank = [ctx.enter_context(nc.psum_tensor(f"bank{i}", [P, 512], F32)) for i in range(8)]

        ident = sb("ident", [P, P])
        earlier = sb("earlier", [P, P])
        ones = sb("ones", [P, P])
        lower = sb("lower", [P, NE, NE])
        pick = sb("pick", [P, HD, P])
        of_head = sb("of_head", [H, D])
        row = sb("row", [MH, MH, P])
        w_rnn = sb("w_rnn", [P, 3 * E0])
        b_rnn = sb("b_rnn", [P, 3 * EH])
        b_rnn_half = sb("b_rnn_half", [P, 3 * EH])
        wd_rnn = sb("wd_rnn", [P, E0 // P, D])
        w_x = sb("w_x", [P, 4, D])
        b_xqk = sb("b_xqk", [P, 2])
        bq_scaled = sb("bq_scaled", [P, 1])
        bv_row = sb("bv_row", [P, D])
        bo_row = sb("bo_row", [P, D])
        dscale = sb("dscale", [P, 1])
        dscale_abs = sb("dscale_abs", [P, 1])
        tiny = sb("tiny", [P, 1])
        w_l = sb("w_l", [P, 4, D])
        wg_l = sb("wg_l", [P, H, HD])
        wg_raw = sb("wg_raw", [P, H])
        bg_l = sb("bg_l", [P, 1])
        bg_half = sb("bg_half", [P, 1])
        w_route = sb("w_route", [P, 2, NE])
        w_up = sb("w_up", [P, 2, NE, FF])
        w_down = sb("w_down", [P, 2, NE, FC, D])
        b_up = sb("b_up", [P, NE * FC])
        b_down = sb("b_down", [NE, D])
        gk_raw = sb("gk_raw", [P, 3, 2 * MH])
        gk = sb("gk", [P, 2, 36])
        gbias = sb("gbias", [36, 1])
        onw = sb("onw", [P, MH * MD])

        x_in = sb("x_in", [P, NT, D])
        x_e0 = sb("x_e0", [P, NT, D])
        x_mid = sb("x_mid", [P, NT, D])
        x_lin = sb("x_lin", [P, NT, D])
        x_e1 = sb("x_e1", [P, NT, D])

        class Norm:

            def __init__(self, name):
                self.stats = sb(name + "_stats", [P, NT, 6])
                self.mv = sb(name + "_mv", [P, NT, 2])
                self.ve = sb(name + "_ve", [P, NT])
                self.rstd = sb(name + "_rstd", [P, NT])
                self.xn = sb(name + "_xn", [P, NT, D])
                self.xnT = sb(name + "_xnT", [P, S])

        nf, ne, nm = Norm("nf"), Norm("ne"), Norm("nm")
        norms = [nf, nf, ne, nm, nm, ne]
        mix = sb("mix", [P, 20 * S])

        def scratch(first, *shape, rows=P):
            n = int(np.prod(shape))
            v = mix[0:rows, first * S:first * S + n]
            if len(shape) == 2:
                return v.rearrange("p (a b) -> p a b", b=shape[1])
            return v.rearrange("p (a b c) -> p a b c", b=shape[1], c=shape[2]) if len(shape) == 3 else v

        mhalf = sb("mhalf", [P, NT * MH])
        dist = sb("dist", [P, NT, S])
        nb = sb("nb", [P, NT, S])
        ctxT_f = sb("ctxT_f", [P, S])
        qr = sb("qr", [PAIRS * HD, H, S], BF16)
        kr = sb("kr", [PAIRS * HD, H, S], BF16)
        qk_p = sb("qk_p", [P, 2, PARTS, S], BF16)
        v_pad = sb("v_pad", [P, NT, H, 2 * GROUP - HD])
        sc = scratch(14, 3, 2, S)
        mneg = sb("mneg", [P, UNITS * 2])
        prob = sb("prob", [P, 3, 2, S])
        pT = sb("pT", [P, 2, 2 * S])
        esum = sb("esum", [P, UNITS * 2])
        rsum = sb("rsum", [P, UNITS * 2])
        rsumT = sb("rsumT", [H, S])
        attnT = sb("attnT", [P, S])
        sf = scratch(0, EH, S)
        si = scratch(2, EH, S)
        sh = scratch(4, EH, S)
        g0 = scratch(6, EH, S)
        bi = scratch(8, EH, S)
        hT = scratch(10, EH, S)
        qk_f = scratch(12, 2, S)
        hid = sb("hid", [P, NE, FC, S])
        logit = sb("logit", [P, NT, NE])
        cmp_gt = sb("cmp_gt", [P, NT, NE, NE])
        cmp_eq = sb("cmp_eq", [P, NT, NE, NE])
        cnt = sb("cnt", [P, NT, NE])
        sel = sb("sel", [P, NT, NE])
        top = sb("top", [P, NT])
        ex = sb("ex", [P, NT, NE])
        gate = sb("gate", [P, NT, NE])
        taken = sb("taken", [P, NE])
        gateT = sb("gateT", [NE, S])
        tmin = scratch(0, 2, S)
        eluv = scratch(2, 2, S)
        phi = scratch(4, 2, S)
        vT = scratch(6, S)
        gT = scratch(7, S)
        kv = scratch(8, 2, 2, S)
        st = scratch(12, 2, 2, S)
        qs = scratch(16, 2, 2, S)
        ctxT = sb("ctxT", [P, S])
        ctx_tok = sb("ctx_tok", [P, NT, MH, MD + 1])
        rows = scratch(0, 8, S, rows=MH)
        ig, fsum, fmin, fabs, fln, fcum, umax, mrow = (rows[:, i] for i in range(8))
        u36 = sb("u36", [36, S])
        uT = sb("uT", [P, NT, 36])
        efm = sb("efm", [P, NT, MH])
        decay = scratch(8, 2, 3, P)
        cT = scratch(11, 2, 3, P)
        nrm = sb("nrm", [P, NT, MH])
        rn = sb("rn", [P, NT, MH])
        hh = scratch(14, NT * MH, MD)
        hc = scratch(15, NT * MH, MD)
        hsq = scratch(16, NT * MH, MD)
        hn = scratch(17, NT * MH, MD)
        mstat = sb("mstat", [P, 4, NT * MH])

        bounce_q = nc.dram_tensor("bounce_q", (2 * PARTS - 1, P, S), BF16, kind="Internal").ap()
        bounce_k = nc.dram_tensor("bounce_k", (PARTS, P, S), BF16, kind="Internal").ap()

        passed_dve = ctx.enter_context(nc.semaphore("passed_dve"))
        passed_pool = ctx.enter_context(nc.semaphore("passed_pool"))
        weights_in = ctx.enter_context(nc.semaphore("weights_in"))
        later_in = ctx.enter_context(nc.semaphore("later_in"))
        setup_done = ctx.enter_context(nc.semaphore("setup_done"))
        later_done = ctx.enter_context(nc.semaphore("later_done"))
        dve_step = ctx.enter_context(nc.semaphore("dve_step"))
        experts_loaded = ctx.enter_context(nc.semaphore("experts_loaded"))
        rank_read = sig("rank_read", 1)
        front_loaded = sig("front_loaded", 32)
        ctx_loaded = sig("ctx_loaded", 16 * (1 + NT))
        dist_loaded = sig("dist_loaded", 16)
        front_done = sig("front_done", 1, base=1)
        dist_taken = sig("dist_taken", 1, base=1)
        ctx_taken = sig("ctx_taken", 1, base=1)
        x_stored = sig("x_stored", 16, base=16)
        var_ready = [sig(f"var_ready{j}", 1) for j in range(6)]
        rstd_ready = [sig(f"rstd_ready{j}", 1) for j in range(6)]
        xn_ready = [sig(f"xn_ready{j}", 1) for j in range(6)]
        xnT_psum = [sig(f"xnT_psum{j}", 1) for j in range(6)]
        xnT_ready = [sig(f"xnT_ready{j}", 1) for j in range(6)]
        rnn_proj = sig("rnn_proj", 3 * EH)
        rnn_sig = sig("rnn_sig", 3 * EH)
        rnn_state = sig("rnn_state", EH)
        rnn_y = sig("rnn_y", 1)
        log_dist = sig("log_dist", 1)
        qkv_psum = sig("qkv_psum", 3)
        qk_sb = sig("qk_sb", 2)
        parts_ready = sig("parts_ready", 1)
        bounced = sig("bounced", 48)
        qr_in = sig("qr_in", 32 * PARTS)
        v_ready = sig("v_ready", 1)
        s_psum = sig("s_psum", UNITS)
        s_biased = sig("s_biased", UNITS)
        p_ready = sig("p_ready", UNITS)
        p_turned = sig("p_turned", UNITS)
        pT_even = sig("pT_even", UNITS // 2)
        pT_odd = sig("pT_odd", UNITS // 2)
        pT_ready = [pT_even, pT_odd]
        pv_done = sig("pv_done", UNITS)
        rsum_ready = sig("rsum_ready", 1)
        rsumT_psum = sig("rsumT_psum", 1)
        rsumT_ready = sig("rsumT_ready", 1)
        rspread = sig("rspread", 1)
        oT_ready = sig("oT_ready", 1)
        attnT_ready = sig("attnT_ready", 1)
        attn_y = sig("attn_y", 1)
        logits_psum = [sig(f"logits_psum{l}", 1) for l in range(2)]
        route_in = [sig(f"route_in{l}", 1) for l in range(2)]
        route_exp = [sig(f"route_exp{l}", 1) for l in range(2)]
        sel_ready = sig("sel_ready", 1)
        rank_psum = sig("rank_psum", 1)
        up_psum = [sig(f"up_psum{l}", NE * FC // 2) for l in range(2)]
        hid_ready = [sig(f"hid_ready{l}", NE * FC // 2) for l in range(2)]
        tanh_ready = sig("tanh_ready", NE * FC // 2)
        down_psum = [sig(f"down_psum{l}", NE) for l in range(2)]
        expert_added = [sig(f"expert_added{l}", NE) for l in range(2)]
        gate_ready = sig("gate_ready", 1)
        gateT_psum = sig("gateT_psum", 1)
        gateT_ready = sig("gateT_ready", 1)
        bias_psum = sig("bias_psum", 1)
        bias_added = sig("bias_added", 1)
        lin_proj = sig("lin_proj", 4)
        elu_in = sig("elu_in", 2)
        elu_exp = sig("elu_exp", 2)
        phi_ready = sig("phi_ready", 2)
        lin_vg = sig("lin_vg", 2)
        kb_psum = sig("kb_psum", HD // 2)
        qb_psum = sig("qb_psum", HD // 2)
        kv_ready = sig("kv_ready", HD // 2)
        qs_ready = sig("qs_ready", HD // 2)
        lin_fold = sig("lin_fold", HD // 2)
        gates_psum = sig("gates_psum", 1)
        fabs_ready = sig("fabs_ready", 1)
        fexp_ready = sig("fexp_ready", 1)
        fln_ready = sig("fln_ready", 1)
        m_ready = sig("m_ready", 1)
        uT_psum = sig("uT_psum", 1)
        uT_ready = sig("uT_ready", 1)
        efm_ready = sig("efm_ready", 1)
        mb_psum = sig("mb_psum", MH)
        qk_psum = sig("qk_psum", MH)
        decay_exp = sig("decay_exp", MH)
        decay_cut = sig("decay_cut", MH)
        c_ready = sig("c_ready", MH)
        h_psum = sig("h_psum", MH)
        hvar_ready = sig("hvar_ready", 1)
        hrstd_ready = sig("hrstd_ready", 1)

        def unit_at(u):
            return 0.26 + 0.68 * u / UNITS

        BIAS_LAG = 0.042
        SUM_BANK = [2, 1]
        OPEN_DOWNS = [4, 7, 8, 8]
        TAIL_AT = [0.016, 0.0885]
        UP_AT = [[0.08, 0.09, 0.11, 0.14, 0.443, 0.444, 0.497, 0.517],
                 [0.17, 0.175, 0.202, 0.204, 0.206, 0.208, 0.22, 0.24],
                 [0.2, 0.22, 0.3, 0.4, 0.5, 0.64, 0.7, 0.8],
                 [0.14, 0.17, 0.175, 0.202, 0.204, 0.206, 0.208, 0.23]]
        RANK_AT = [0.53, 0.303, 0.22, 0.303]
        DOWN_AT = [[0.54, 0.57, 0.75, 0.846, 0.01, 0.0275, 0.086, 0.1],
                   [0.378, 0.463, 0.548, 0.6755, 0.718, 0.903, 0.92, 0.003],
                   [0.33, 0.43, 0.53, 0.63, 0.73, 0.83, 0.88, 0.93],
                   [0.388, 0.431, 0.473, 0.558, 0.643, 0.728, 0.813, 0.8985]]
        ADD_AT = [[0.543, 0.573, 0.75, 0.889, 0.014, 0.0305, 0.089, 0.103],
                  [0.421, 0.506, 0.571, 0.7185, 0.761, 0.918, 0.9325, 0.018],
                  [0.35, 0.45, 0.55, 0.65, 0.75, 0.85, 0.9, 0.95],
                  [0.4305, 0.4727, 0.515, 0.601, 0.686, 0.771, 0.856, 0.941]]
        NORM_AT = [0.025, 0.11, 0.0, 0.11]
        TURN_AT = [0.052, 0.147, 0.05, 0.147]
        ROUTE_AT = [0.07, 0.165, 0.1, 0.165]
        CHOICE_AT = [0.1, 0.225, 0.15, 0.225]
        GATE_AT = [0.105, 0.2605, 0.18, 0.2605]

        def lin_at(i):
            return 0.14 + 0.06 * i

        def head_at(h):
            return 0.70 + 0.05 * h

        def course(eng, later_setup, front, middle, tail, opening, closing):
            side_by_side(front(0))
            later_setup()
            side_by_side(front(1), opening(0, 0, 3))
            side_by_side(middle(0), opening(0, 1))
            with eng.Fori(0, B - 2) as k:
                side_by_side(front(k + 2), tail(k), one_by_one(closing(0, k + 1), opening(1, k)))
                side_by_side(middle(k + 1), one_by_one(closing(1, k), opening(0, k + 2)))
            side_by_side(tail(B - 2), closing(0, B - 1))
            side_by_side(middle(B - 1), within(opening(1, B - 2, 2), -0.1, 0.85))
            side_by_side(one_by_one(tail(B - 1), opening(1, B - 1, 2)))

        LOADS, LATER_LOADS = 10, 15

        def setup_load(eng, dst, src, arrived):
            eng.dma_start(dst, src).then_inc(arrived, 16)

        SETUP_OPS, LATER_OPS = 9, 8
        block = ctx.enter_context(nc.Block())

        @block.sync
        def _(sp):
            for s in (front_done, dist_taken, ctx_taken, x_stored):
                sp.sem_inc(s.sem, s.base)

            def load_front(k):
                sp.wait_ge(front_done.sem, front_done.at(k, 0))
                sp.dma_start(x_in[:], a["x"][bass.ds(k, 1)].rearrange("o p n d -> p (o n) d")).then_inc(front_loaded.sem, 16)
                sp.dma_start(ctxT_f[:], a["ctxT"][bass.ds(k, 1)].rearrange("o p t -> p (o t)")).then_inc(front_loaded.sem, 16)
                sp.wait_ge(dist_taken.sem, dist_taken.at(k, 0))
                sp.dma_start(dist[:], a["dist"][bass.ds(k, 1)].rearrange("o p n k -> p (o n) k")).then_inc(dist_loaded.sem, 16)

            load_front(0)
            for dst, name in ((w_rnn, "w_rnn"), (ident, "ident"), (b_rnn, "b_rnn"), (wd_rnn, "wd_rnn"),
                              (w_x, "w_x"), (b_xqk, "b_xqk"), (of_head, "of_head")):
                setup_load(sp, dst[:], a[name], weights_in)
            for dst, name in ((dscale, "dscale"), (bv_row, "bv"), (bo_row, "bo")):
                setup_load(sp, dst[:], a[name].partition_broadcast(P), weights_in)
            for dst, name in ((earlier, "earlier"), (ones, "ones"), (lower, "lower"),
                              (pick, "pick"), (row, "row"), (w_l, "w_l"), (wg_raw, "wg_l"), (bg_l, "bg_l"),
                              (w_route, "w_route"), (b_up, "b_up"), (b_down, "b_down"), (gk_raw, "gk_raw")):
                setup_load(sp, dst[:], a[name], later_in)
            setup_load(sp, gbias[0:MH, :], a["gate_bias"][0], later_in)
            setup_load(sp, gbias[32:32 + MH, :], a["gate_bias"][1], later_in)
            setup_load(sp, onw[:], a["onw"].partition_broadcast(P), later_in)

            def experts_in(l):
                sp.dma_start(w_up[:, l], a["w_up"][l].rearrange("e d f -> d e f")).then_inc(experts_loaded, 16)
                sp.dma_start(w_down[:, l], a["w_down"][l].rearrange("e (c p) d -> p e c d", p=P)).then_inc(experts_loaded, 16)

            def bounce_qk(k):
                sp.wait_ge(parts_ready.sem, parts_ready.at(k, 1))
                sp.dma_start(bounce_q[0:PARTS].rearrange("a p t -> p a t"), qk_p[:, 0]).then_inc(bounced.sem, 16)
                sp.dma_start(bounce_q[PARTS:].rearrange("a p t -> p a t"), qk_p[:, 0, 0:PARTS - 1]).then_inc(bounced.sem, 16)
                sp.dma_start(bounce_k.rearrange("a p t -> p a t"), qk_p[:, 1]).then_inc(bounced.sem, 16)
                sp.wait_ge(bounced.sem, bounced.at(k, 48))
                for s in range(PARTS):
                    block_rows = slice(s * PARTS * HD, (s + 1) * PARTS * HD)
                    for dst, src in ((qr, bounce_q[s:s + PARTS]), (kr, bounce_k)):
                        sp.dma_start(dst[block_rows], src.rearrange("a (d h) t -> (a d) h t", h=H)).then_inc(qr_in.sem, 16)

            def load_middle(k):
                sp.wait_ge(ctx_taken.sem, ctx_taken.at(k, 0))
                sp.dma_start(ctxT[:], a["ctxT"][bass.ds(k, 1)].rearrange("o p t -> p (o t)")).then_inc(ctx_loaded.sem, 16)
                for n in range(NT):
                    sp.dma_start(ctx_tok[:, n, :, 0:MD], a["ctx"][bass.ds(k, 1), :, n].rearrange("o p (h d) -> p (o h) d", h=MH)
                                 ).then_inc(ctx_loaded.sem, 16)

            def store(k):
                sp.wait_ge(expert_added[1].sem, expert_added[1].at(k, NE))
                sp.dma_start(out[bass.ds(k, 1)].rearrange("o p n d -> p (o n) d"), x_e1[:]).then_inc(x_stored.sem, 16)

            experts_in(0)
            bounce_qk(0)
            load_front(1)
            experts_in(1)
            bounce_qk(1)
            load_middle(0)
            load_front(2)
            with sp.Fori(0, B - 3) as k:
                load_middle(k + 1)
                bounce_qk(k + 2)
                load_front(k + 3)
                store(k)
            load_middle(B - 2)
            bounce_qk(B - 1)
            store(B - 3)
            load_middle(B - 1)
            store(B - 2)
            store(B - 1)
            sp.wait_ge(x_stored.sem, 16 * B + x_stored.base)

        @block.gpsimd
        def _(pool):
            nc.gpsimd.memset(mhalf[:], -0.5).then_inc(setup_done, 1)
            nc.gpsimd.memset(tiny[:], 1e-9).then_inc(setup_done, 1)
            nc.gpsimd.memset(v_pad[:], 0.0).then_inc(setup_done, 1)
            nc.gpsimd.memset(ctx_tok[:, :, :, MD:MD + 1], 1.0).then_inc(setup_done, 1)
            nc.gpsimd.memset(u36[:], 0.0).then_inc(setup_done, 1)
            nc.gpsimd.memset(taken[:], 0.0).then_inc(setup_done, 1)
            pool.wait_ge(setup_done, SETUP_OPS)

            def inverse_root(j, k):
                pool.wait_ge(var_ready[j].sem, var_ready[j].at(k, 1))
                nc.gpsimd.tensor_tensor(norms[j].rstd[:], norms[j].ve[:], mhalf[:, 0:NT], ALU.pow).then_inc(rstd_ready[j].sem, 1)

            def front(k):
                yield 0.0
                inverse_root(0, k)
                yield 0.18
                inverse_root(1, k)

            def opening(l, k, t=None):
                t = l if t is None else t
                yield NORM_AT[t]
                inverse_root(2 if l == 0 else 5, k)

            def closing(l, k, t=None):
                t = l if t is None else t
                yield from ()

            def middle(k):
                yield 0.0
                inverse_root(3, k)
                yield 0.44
                inverse_root(4, k)
                for h in range(MH):
                    yield head_at(h)
                    pool.wait_ge(decay_exp.sem, decay_exp.at(k, h + 1))
                    pool.sem_inc(passed_pool, 1)
                    d = decay[:, h % 2, 0:3:2, :]
                    nc.gpsimd.affine_select(out=d, in_=d, compare_op=ALU.is_ge, fill=0.0, base=0,
                                            pattern=[[0, 2], [1, P]], channel_multiplier=-1).then_inc(decay_cut.sem, 1)

            def tail(k):
                yield TAIL_AT[0] + 0.01
                pool.wait_ge(hvar_ready.sem, hvar_ready.at(k, 1))
                nc.gpsimd.tensor_tensor(mstat[:, 3], mstat[:, 2], mhalf[:], ALU.pow).then_inc(hrstd_ready.sem, 1)

            def later_setup():
                pool.wait_ge(later_in, 16 * LATER_LOADS)
                pool.wait_ge(later_done, LATER_OPS)

            course(pool, later_setup, front, middle, tail, opening, closing)

        @block.scalar
        def _(act):
            act.wait_ge(setup_done, SETUP_OPS)

            def turn_out(j, src, k):
                act.wait_ge(xnT_psum[j].sem, xnT_psum[j].at(k, 1))
                nc.scalar.copy(norms[j].xnT[:], src[:, 0:S]).then_inc(xnT_ready[j].sem, 1)

            def front(k):
                yield 0.0
                act.wait_ge(dist_loaded.sem, dist_loaded.at(k, 16))
                nc.scalar.activation(nb[:], dist[:], ACT.Ln, bias=tiny[:, 0:1]).then_inc(log_dist.sem, 1)
                yield 0.03
                turn_out(0, bank[6], k)
                yield 0.06
                for c in range(3 * EH):
                    act.wait_ge(rnn_proj.sem, rnn_proj.at(k, (c // EH + 1) * EH))
                    nc.scalar.activation((sf, si, sh)[c // EH][:, c % EH], bank[3 + c // EH][:, (c % EH) * S:(c % EH + 1) * S],
                                         ACT.Sigmoid, bias=b_rnn[:, c:c + 1]).then_inc(rnn_sig.sem, 1)
                yield 0.20
                turn_out(1, bank[7], k)
                act.wait_ge(qkv_psum.sem, qkv_psum.at(k, 1))
                nc.scalar.activation(qk_f[:, 0], bank[3][:, 0:S], ACT.Identity, bias=bq_scaled[:, 0:1],
                                     scale=-HD ** -0.5).then_inc(qk_sb.sem, 1)
                act.wait_ge(qkv_psum.sem, qkv_psum.at(k, 2))
                nc.scalar.activation(qk_f[:, 1], bank[4][:, 0:S], ACT.Identity, bias=b_xqk[:, 1:2]).then_inc(qk_sb.sem, 1)

                def turned_copy(u):
                    act.wait_ge(p_turned.sem, p_turned.at(k, u + 1))
                    if u >= 2:
                        act.wait_ge(pv_done.sem, pv_done.at(k, u - 1))
                    nc.scalar.copy(pT[:, u % 2], bank[5 + u % 2][:]).then_inc(pT_odd.sem, 1)

                for u in range(UNITS):
                    yield unit_at(u)
                    act.wait_ge(s_biased.sem, s_biased.at(k, u + 1))
                    if u >= 3:
                        act.wait_ge(p_turned.sem, p_turned.at(k, u - 2))
                    for j in range(2):
                        last = nc.scalar.activation(prob[:, u % 3, j], sc[:, u % 3, j], ACT.Exp, scale=-1.0,
                                                    bias=mneg[:, 2 * u + j:2 * u + j + 1],
                                                    accum_out=esum[:, 2 * u + j:2 * u + j + 1])
                    last.then_inc(p_ready.sem, 1)
                    if u >= 2 and u % 2 == 1:
                        turned_copy(u - 2)
                yield 0.957
                turned_copy(UNITS - 1)
                yield 0.97
                act.wait_ge(pv_done.sem, pv_done.at(k, UNITS))
                nc.scalar.copy(attnT[:], bank[7][:, 0:S]).then_inc(oT_ready.sem, 1)

            def hidden(l, k, e):
                for c2 in range(FC // 2):
                    up = bank[c2][:].rearrange("p (c t) -> p c t", c=2)
                    act.wait_ge(up_psum[l].sem, up_psum[l].at(k, e * FC // 2 + c2 + 1))
                    if l == 0:
                        nc.scalar.activation(hid[:, e, 2 * c2:2 * c2 + 2], up, ACT.Tanh, scale=0.5).then_inc(tanh_ready.sem, 1)
                    else:
                        for c in range(2):
                            f = e * FC + 2 * c2 + c
                            last = nc.scalar.activation(hid[:, e, 2 * c2 + c], up[:, c], ACT.Gelu, bias=b_up[:, f:f + 1])
                        last.then_inc(hid_ready[l].sem, 1)

            def opening(l, k, t=None):
                t = l if t is None else t
                yield TURN_AT[t] + 0.01
                turn_out(2 if l == 0 else 5, bank[0], k)

                def choice():
                    yield GATE_AT[t] - 0.001
                    act.wait_ge(route_in[l].sem, route_in[l].at(k, 1))
                    nc.scalar.activation(ex[:], ex[:], ACT.Exp).then_inc(route_exp[l].sem, 1)

                def all_hidden():
                    for e in range(NE):
                        yield UP_AT[t][e]
                        hidden(l, k, e)

                yield from together(choice(), all_hidden())

            def closing(l, k, t=None):
                t = l if t is None else t
                yield from ()

            def middle(k):
                yield 0.03
                turn_out(3, bank[7], k)
                yield 0.08
                for i in range(2):
                    act.wait_ge(elu_in.sem, elu_in.at(k, i + 1))
                    nc.scalar.activation(eluv[:, i], tmin[:, i], ACT.Exp).then_inc(elu_exp.sem, 1)
                act.wait_ge(lin_proj.sem, lin_proj.at(k, 3))
                nc.scalar.copy(vT, bank[5][:, 0:S]).then_inc(lin_vg.sem, 1)
                act.wait_ge(lin_proj.sem, lin_proj.at(k, 4))
                nc.scalar.activation(gT, bank[6][:, 0:S], ACT.Tanh, bias=bg_half[:, 0:1], scale=0.5).then_inc(lin_vg.sem, 1)
                yield 0.46
                turn_out(4, bank[7], k)
                yield 0.505
                act.wait_ge(fabs_ready.sem, fabs_ready.at(k, 1))
                nc.scalar.activation(fabs, fabs, ACT.Exp, scale=-1.0).then_inc(fexp_ready.sem, 1)
                act.wait_ge(fexp_ready.sem, fexp_ready.at(k, 1))
                nc.scalar.activation(fln, fabs, ACT.Ln, bias=1.0).then_inc(fln_ready.sem, 1)
                yield 0.55
                act.wait_ge(uT_ready.sem, uT_ready.at(k, 1))
                nc.scalar.activation(efm[:], uT[:, :, 32:32 + MH], ACT.Exp, scale=-1.0).then_inc(efm_ready.sem, 1)
                for h in range(MH):
                    yield head_at(h)
                    act.wait_ge(mb_psum.sem, mb_psum.at(k, 2 * (h // 2) + 2))
                    if h >= 2:
                        act.wait_ge(c_ready.sem, c_ready.at(k, h - 1))
                    mb = bank[5 + h // 2][:, (h % 2) * S:(h % 2 + 1) * S]
                    nc.scalar.activation(decay[:, h % 2, 0:2, :], mb.rearrange("p (b t) -> p b t", b=2), ACT.Exp, bias=uT[:, 0, h:h + 1])
                    nc.scalar.activation(decay[:, h % 2, 2, :], mb[:, P:S], ACT.Exp, bias=uT[:, 1, h:h + 1]).then_inc(decay_exp.sem, 1)

            def tail(k):
                yield from ()

            def later_setup():
                act.wait_ge(later_in, 16 * LATER_LOADS)
                act.wait_ge(later_done, LATER_OPS)

            course(act, later_setup, front, middle, tail, opening, closing)

        @block.tensor
        def _(pe):
            pe.wait_ge(weights_in, 16 * LOADS)
            pe.wait_ge(setup_done, SETUP_OPS)

            def alone():
                pe.wait_ge(setup_done, SETUP_OPS)

            def tok(n):
                return slice(n * P, (n + 1) * P)

            def half(n):
                return slice(n * S, (n + 1) * S)

            def turn(j, dst, k):
                pe.wait_ge(xn_ready[j].sem, xn_ready[j].at(k, 1))
                for n in range(NT):
                    last = nc.tensor.transpose(dst[:, tok(n)], norms[j].xn[:, n], ident[:])
                last.then_inc(xnT_psum[j].sem, 1)

            def front(k):
                yield 0.02
                turn(0, bank[6], k)
                yield 0.05
                pe.wait_ge(xnT_ready[0].sem, xnT_ready[0].at(k, 1))
                for c in range(3 * EH):
                    nc.tensor.matmul(bank[3 + c // EH][:, half(c % EH)], w_rnn[:, c * P:(c + 1) * P], nf.xnT[:],
                                     start=True, stop=True).then_inc(rnn_proj.sem, 1)
                yield 0.14
                pe.wait_ge(rnn_state.sem, rnn_state.at(k, EH))
                for n in range(NT):
                    for e in range(EH):
                        last = nc.tensor.matmul(bank[6][:, tok(n)], hT[:, e, tok(n)], wd_rnn[:, e], start=(e == 0), stop=(e == EH - 1))
                last.then_inc(rnn_y.sem, 1)
                yield 0.145
                pe.wait_ge(front_loaded.sem, front_loaded.at(k, 32))
                nc.tensor.matmul(bank[4][:, 0:S], w_x[:, 1], ctxT_f[:], start=True, stop=True)
                for n in range(NT):
                    nc.tensor.matmul(bank[5][:, tok(n)], ctxT_f[:, tok(n)], w_x[:, 2], start=True, stop=True)
                yield 0.19
                turn(1, bank[7], k)
                pe.wait_ge(xnT_ready[1].sem, xnT_ready[1].at(k, 1))
                nc.tensor.matmul(bank[3][:, 0:S], w_x[:, 0], nf.xnT[:], start=True, stop=True).then_inc(qkv_psum.sem, 3)

                def scores(u):
                    qt, hp = u // (H // 2), u % (H // 2)
                    if u >= 2:
                        pe.wait_ge(s_biased.sem, s_biased.at(k, u - 1))
                    for j in range(2):
                        h = 2 * hp + j
                        last = nc.tensor.matmul(bank[3 + u % 2][:, half(j)], qr[:, h, tok(qt)], kr[:, h, :], start=True, stop=True)
                    last.then_inc(s_psum.sem, 1)

                def turn_probs(u):
                    pe.wait_ge(p_ready.sem, p_ready.at(k, u + 1))
                    if u >= 2:
                        pe.wait_ge(pT_ready[u % 2].sem, pT_ready[u % 2].at(k, u // 2))
                    for j in range(2):
                        for kt in range(NT):
                            last = nc.tensor.transpose(bank[5 + u % 2][:, tok(NT * j + kt)], prob[:, u % 3, j, tok(kt)], ident[:])
                    last.then_inc(p_turned.sem, 1)

                def weigh(u):
                    qt, hp = u // (H // 2), u % (H // 2)
                    pe.wait_ge(pT_ready[u % 2].sem, pT_ready[u % 2].at(k, u // 2 + 1))
                    for j in range(2):
                        g, m = divmod(2 * hp + j, GROUP // HD)
                        for kt in range(NT):
                            last = nc.tensor.matmul(bank[7][g * GROUP:(g + 1) * GROUP, tok(qt)],
                                                    v_pad[:, kt, 2 * hp + j, GROUP - (m + 1) * HD:2 * GROUP - (m + 1) * HD],
                                                    pT[:, u % 2, tok(NT * j + kt)], start=(m == 0 and kt == 0),
                                                    stop=(m == GROUP // HD - 1 and kt == NT - 1), tile_position=(0, g * GROUP))
                    last.then_inc(pv_done.sem, 1)

                yield 0.25
                pe.wait_ge(v_ready.sem, v_ready.at(k, 1))
                pe.wait_ge(qr_in.sem, qr_in.at(k, 32 * PARTS))
                scores(0)
                scores(1)
                for u in range(UNITS):
                    yield unit_at(u)
                    if u >= 2:
                        turn_probs(u - 2)
                    if u >= 3:
                        weigh(u - 3)
                    if u + 2 < UNITS:
                        scores(u + 2)
                yield 0.945
                turn_probs(UNITS - 2)
                weigh(UNITS - 3)
                yield 0.955
                turn_probs(UNITS - 1)
                weigh(UNITS - 2)
                yield 0.96
                weigh(UNITS - 1)
                yield 0.962
                pe.wait_ge(rsum_ready.sem, rsum_ready.at(k, 1))
                for n in range(NT):
                    last = nc.tensor.transpose(bank[3][0:H, tok(n)], rsum[:, n * H:(n + 1) * H], ident[:])
                last.then_inc(rsumT_psum.sem, 1)
                yield 0.966
                pe.wait_ge(rsumT_ready.sem, rsumT_ready.at(k, 1))
                nc.tensor.matmul(bank[4][:, 0:S], of_head[:], rsumT[:], start=True, stop=True).then_inc(rspread.sem, 1)
                yield 0.985
                pe.wait_ge(attnT_ready.sem, attnT_ready.at(k, 1))
                for n in range(NT):
                    last = nc.tensor.matmul(bank[3][:, tok(n)], attnT[:, tok(n)], w_x[:, 3], start=True, stop=True)
                last.then_inc(attn_y.sem, 1)

            in_bank1 = {"ups": 0, "down": 0}

            def up(l, k, e):
                in_bank1["ups"] = e + 1
                for c in range(FC):
                    if e >= 1 and c % 2 == 0:
                        pe.wait_ge(hid_ready[l].sem, hid_ready[l].at(k, (e - 1) * FC // 2 + c // 2 + 1))
                    if c == FC // 2 and in_bank1["down"]:
                        pe.wait_ge(expert_added[l].sem, expert_added[l].at(k, in_bank1["down"]))
                        in_bank1["down"] = 0
                    last = nc.tensor.matmul(bank[c // 2][:, half(c % 2)], w_up[:, l, e, c * P:(c + 1) * P], ne.xnT[:],
                                            start=True, stop=True)
                    if c % 2 == 1:
                        last.then_inc(up_psum[l].sem, 1)

            def down(l, k, e):
                if e >= 2:
                    pe.wait_ge(expert_added[l].sem, expert_added[l].at(k, e - 1))
                elif e == 0 and l == 0:
                    pe.wait_ge(rank_read.sem, rank_read.at(k, 1))
                elif e == 0:
                    pe.wait_ge(bias_added.sem, bias_added.at(k, 1))
                if e % 2 == 1:
                    in_bank1["down"] = e + 1
                    pe.wait_ge(hid_ready[l].sem, hid_ready[l].at(k, in_bank1["ups"] * FC // 2))
                else:
                    pe.wait_ge(hid_ready[l].sem, hid_ready[l].at(k, (e + 1) * FC // 2))
                to = bank[SUM_BANK[e % 2]]
                for n in range(NT):
                    for c in range(FC):
                        last = nc.tensor.matmul(to[:, tok(n)], hid[:, e, c, tok(n)],
                                                w_down[:, l, e, c], start=(c == 0), stop=(c == FC - 1))
                last.then_inc(down_psum[l].sem, 1)

            def opening(l, k, t=None):
                t = l if t is None else t
                j = 2 if l == 0 else 5
                in_bank1["down"] = 0
                yield TURN_AT[t]
                turn(j, bank[0], k)
                yield ROUTE_AT[t]
                pe.wait_ge(xnT_ready[j].sem, xnT_ready[j].at(k, 1))
                for n in range(NT):
                    last = nc.tensor.matmul(bank[2][:, n * NE:(n + 1) * NE], ne.xnT[:, tok(n)], w_route[:, l], start=True, stop=True)
                last.then_inc(logits_psum[l].sem, 1)
                pe.wait_ge(experts_loaded, 32 * (l + 1))

                def rank():
                    yield RANK_AT[t]
                    pe.wait_ge(sel_ready.sem, sel_ready.at(k, 1))
                    for n in range(NT):
                        r = bank[2][:, n * NE:(n + 1) * NE]
                        for m in range(n):
                            nc.tensor.matmul(r, ones[:], sel[:, m], start=(m == 0), stop=False)
                        nc.tensor.matmul(r, earlier[:], sel[:, n], start=(n == 0), stop=True)
                    for m in range(NT):
                        last = nc.tensor.matmul(bank[2][:, NT * NE:(NT + 1) * NE], ones[:], sel[:, m],
                                                start=(m == 0), stop=(m == NT - 1))
                    last.then_inc(rank_psum.sem, 1)

                def bias_of_down():
                    yield RANK_AT[t]
                    pe.wait_ge(gate_ready.sem, gate_ready.at(k, 1))
                    for n in range(NT):
                        last = nc.tensor.transpose(bank[2][0:NE, tok(n)], gate[:, n], ident[:])
                    last.then_inc(gateT_psum.sem, 1)
                    yield RANK_AT[t] + BIAS_LAG
                    pe.wait_ge(gateT_ready.sem, gateT_ready.at(k, 1))
                    for n in range(NT):
                        last = nc.tensor.matmul(bank[2][:, S + n * P:S + (n + 1) * P], gateT[:, tok(n)], b_down[:], start=True, stop=True)
                    last.then_inc(bias_psum.sem, 1)

                def ups():
                    for e in range(NE):
                        yield UP_AT[t][e]
                        up(l, k, e)

                yield from together(rank() if l == 0 else bias_of_down(), ups(), downs(l, k, t, range(OPEN_DOWNS[t])))

            def downs(l, k, t, experts):
                for e in experts:
                    yield DOWN_AT[t][e]
                    down(l, k, e)

            def closing(l, k, t=None):
                t = l if t is None else t
                yield from downs(l, k, t, range(OPEN_DOWNS[t], NE))

            def middle(k):
                yield 0.02
                turn(3, bank[7], k)
                yield 0.05
                pe.wait_ge(xnT_ready[3].sem, xnT_ready[3].at(k, 1))
                for i, w in enumerate((w_l[:, 0], w_l[:, 1], w_l[:, 2], wg_l[:].rearrange("p h j -> p (h j)"))):
                    nc.tensor.matmul(bank[3 + i][:, 0:S], w, nm.xnT[:], start=True, stop=True).then_inc(lin_proj.sem, 1)

                def spread_k(i):
                    if i >= 2:
                        pe.wait_ge(kv_ready.sem, kv_ready.at(k, i - 1))
                    for r in range(2):
                        last = nc.tensor.matmul(bank[3 + i % 2][:, half(r)], pick[:, 2 * i + r], phi[:, 1], start=True, stop=True)
                    last.then_inc(kb_psum.sem, 1)

                def spread_q(i):
                    if i >= 2:
                        pe.wait_ge(qs_ready.sem, qs_ready.at(k, i - 1))
                    for r in range(2):
                        last = nc.tensor.matmul(bank[5 + i % 2][:, half(r)], pick[:, 2 * i + r], phi[:, 0], start=True, stop=True)
                    last.then_inc(qb_psum.sem, 1)

                def fold(i):
                    pe.wait_ge(qs_ready.sem, qs_ready.at(k, i + 1))
                    for r in range(2):
                        for n in range(NT):
                            last = nc.tensor.matmul(bank[7][:, tok(n)], qs[:, i % 2, r, tok(n)], w_l[:, 3],
                                                    start=(i == 0 and r == 0 and n == 0), stop=(i == HD // 2 - 1 and r == 1),
                                                    skip_group_check=True)
                    last.then_inc(lin_fold.sem, 1)

                yield 0.12
                pe.wait_ge(phi_ready.sem, phi_ready.at(k, 2))
                pe.wait_ge(lin_vg.sem, lin_vg.at(k, 2))
                spread_k(0)
                spread_q(0)
                for i in range(HD // 2):
                    yield lin_at(i)
                    if i + 1 < HD // 2:
                        spread_k(i + 1)
                        spread_q(i + 1)
                    if i >= 1:
                        fold(i - 1)
                yield 0.40
                fold(HD // 2 - 1)

                yield 0.45
                turn(4, bank[7], k)
                yield 0.48
                pe.wait_ge(ctx_loaded.sem, ctx_loaded.at(k, ctx_loaded.per))
                pe.wait_ge(xnT_ready[4].sem, xnT_ready[4].at(k, 1))
                nc.tensor.matmul(bank[3][0:36, 0:S], gk[:, 0], nm.xnT[:], start=True, stop=False)
                nc.tensor.matmul(bank[3][0:36, 0:S], gk[:, 1], ctxT[:], start=False, stop=True).then_inc(gates_psum.sem, 1)
                yield 0.535
                alone()
                pe.wait_ge(m_ready.sem, m_ready.at(k, 1))
                for n in range(NT):
                    last = nc.tensor.transpose(bank[7][:, n * 36:(n + 1) * 36], u36[:, tok(n)], ident[0:36, 0:36])
                last.then_inc(uT_psum.sem, 1)
                for h in range(MH):
                    nc.tensor.matmul(bank[5 + h // 2][:, half(h % 2)], row[:, h], mrow, start=True, stop=True).then_inc(mb_psum.sem, 1)

                def qk(h):
                    hs = slice(h * MD, (h + 1) * MD)
                    if h >= 2:
                        pe.wait_ge(c_ready.sem, c_ready.at(k, h - 1))
                    qkb = bank[3 + h % 2]
                    nc.tensor.matmul(qkb[:, 0:S], ctxT[hs, 0:P], nm.xnT[hs, :], start=True, stop=True, tile_position=(h * MD, 0))
                    nc.tensor.matmul(qkb[:, S:S + P], ctxT[hs, P:S], nm.xnT[hs, P:S],
                                     start=True, stop=True, tile_position=(h * MD, 0)).then_inc(qk_psum.sem, 1)

                def weigh_m(h):
                    pe.wait_ge(c_ready.sem, c_ready.at(k, h + 1))
                    g = MD + 1
                    nc.tensor.matmul(bank[7][:, h * g:(h + 1) * g], cT[:, h % 2, 0], ctx_tok[:, 0, h], start=True, stop=True)
                    nc.tensor.matmul(bank[7][:, (MH + h) * g:(MH + h + 1) * g], cT[:, h % 2, 1], ctx_tok[:, 0, h], start=True, stop=False)
                    nc.tensor.matmul(bank[7][:, (MH + h) * g:(MH + h + 1) * g], cT[:, h % 2, 2], ctx_tok[:, 1, h],
                                     start=False, stop=True).then_inc(h_psum.sem, 1)

                qk(0)
                for h in range(MH):
                    yield head_at(h)
                    if h + 1 < MH:
                        qk(h + 1)
                    if h >= 1:
                        weigh_m(h - 1)
                yield 0.90
                weigh_m(MH - 1)

            def tail(k):
                yield from ()

            def later_setup():
                pe.wait_ge(later_in, 16 * LATER_LOADS)
                pe.wait_ge(later_done, LATER_OPS)

            course(pe, later_setup, front, middle, tail, opening, closing)

        @block.vector
        def _(dve):
            dve.wait_ge(weights_in, 16 * LOADS)
            nc.vector.tensor_scalar(b_rnn_half[:], b_rnn[:], 0.5, None, ALU.add).then_inc(setup_done, 1)
            nc.vector.tensor_scalar(bq_scaled[:], b_xqk[:, 0:1], -HD ** -0.5, None, ALU.mult).then_inc(setup_done, 1)
            nc.vector.scalar_tensor_tensor(dscale_abs[:], dscale[:], -1.0, dscale[:], ALU.mult, ALU.max).then_inc(setup_done, 1)
            dve.wait_ge(setup_done, SETUP_OPS)

            def later_setup():
                dve.wait_ge(later_in, 16 * LATER_LOADS)
                nc.vector.tensor_scalar(w_l[:, 0], w_l[:, 0], HD ** -0.5, None, ALU.mult).then_inc(later_done, 1)
                nc.vector.tensor_copy(wg_l[:], wg_raw[:].unsqueeze(2).to_broadcast([P, H, HD])).then_inc(later_done, 1)
                nc.vector.tensor_scalar(bg_half[:], bg_l[:], 0.5, None, ALU.mult).then_inc(later_done, 1)
                nc.vector.memset(gk[:], 0.0).then_inc(later_done, 1)
                dve.wait_ge(later_done, 4)
                for i in range(2):
                    g = slice(32 * i, 32 * i + MH)
                    r = slice(MH * i, MH * i + MH)
                    nc.vector.tensor_copy(gk[:, 0, g], gk_raw[:, 0, r]).then_inc(later_done, 1)
                    nc.vector.tensor_tensor(gk[:, 1, g], gk_raw[:, 1, r], gk_raw[:, 2, r], ALU.add).then_inc(later_done, 1)
                dve.wait_ge(later_done, LATER_OPS)

            class Chain:

                before, here = 0, 0

            LOOP_LINKS = 67

            def link(ins):
                Chain.here += 1
                ins.then_inc(dve_step, 1)
                dve.wait_ge(dve_step, Chain.before + Chain.here)

            def alone():
                dve.sem_inc(passed_dve, 1)

            def layer_norm(j, x, k):
                b = norms[j]
                for n in range(NT):
                    last = nc.vector.bn_stats(b.stats[:, n], x[:, n])
                link(last)
                alone()
                for n in range(NT):
                    last = nc.vector.bn_aggr(b.mv[:, n], b.stats[:, n])
                link(last)
                nc.vector.tensor_scalar(b.ve[:], b.mv[:, :, 1], 1e-5, None, ALU.add).then_inc(var_ready[j].sem, 1)

            def normalised(j, x, k):
                b = norms[j]
                dve.wait_ge(rstd_ready[j].sem, rstd_ready[j].at(k, 1))
                for n in range(NT):
                    last = nc.vector.tensor_scalar(b.xn[:, n], x[:, n], b.mv[:, n, 0:1], b.rstd[:, n:n + 1], ALU.subtract, ALU.mult)
                last.then_inc(xn_ready[j].sem, 1)

            def tiles(b):
                return b[:, 0:S].rearrange("p (n d) -> p n d", n=NT)

            def front(k):
                yield 0.0
                dve.wait_ge(front_loaded.sem, front_loaded.at(k, 32))
                layer_norm(0, x_in, k)
                yield 0.015
                normalised(0, x_in, k)
                yield 0.07
                dve.wait_ge(log_dist.sem, log_dist.at(k, 1))
                nc.vector.tensor_scalar(nb[:], nb[:], dscale_abs[:, 0:1], None, ALU.mult).then_inc(dist_taken.sem, 1)
                yield 0.09
                dve.wait_ge(rnn_sig.sem, rnn_sig.at(k, 3 * EH))
                for e in range(EH):
                    last = nc.vector.scalar_tensor_tensor(g0[:, e], bank[5][:, e * S:(e + 1) * S], b_rnn_half[:, 2 * EH + e:2 * EH + e + 1],
                                                          sh[:, e], ALU.add, ALU.max)
                link(last)
                link(nc.vector.tensor_tensor(bi, si, g0, ALU.mult))
                for e in range(EH):
                    nc.vector.tensor_tensor_scan(hT[:, e], sf[:, e], bi[:, e], 0.5, ALU.mult, ALU.add).then_inc(rnn_state.sem, 1)
                yield 0.16
                dve.wait_ge(rnn_y.sem, rnn_y.at(k, 1))
                link(nc.vector.tensor_tensor(x_in[:], tiles(bank[6]), x_in[:], ALU.add))

                layer_norm(1, x_in, k)
                yield 0.185
                normalised(1, x_in, k)
                yield 0.21
                dve.wait_ge(qk_sb.sem, qk_sb.at(k, 2))
                link(nc.vector.tensor_copy(qk_p[:, :, 0], qk_f[:]))
                link(nc.vector.tensor_tensor(qk_f[:], qk_f[:], qk_p[:, :, 0], ALU.subtract))
                link(nc.vector.tensor_copy(qk_p[:, :, 1], qk_f[:]))
                nc.vector.tensor_tensor(qk_p[:, :, 2], qk_f[:], qk_p[:, :, 1], ALU.subtract).then_inc(parts_ready.sem, 1)
                dve.wait_ge(qkv_psum.sem, qkv_psum.at(k, 3))
                nc.vector.tensor_tensor(v_pad[:, :, :, GROUP - HD:GROUP], bank[5][:, 0:S].rearrange("p (n h d) -> p n h d", n=NT, h=H),
                                        bv_row[:].rearrange("p (h d) -> p h d", h=H).unsqueeze(1).to_broadcast([P, NT, H, HD]),
                                        ALU.add).then_inc(v_ready.sem, 1)
                link(nc.vector.tensor_tensor(x_in[:], x_in[:], bo_row[:].unsqueeze(1).to_broadcast([P, NT, D]), ALU.add))

                def turned_copy(u):
                    dve.wait_ge(p_turned.sem, p_turned.at(k, u + 1))
                    if u >= 2:
                        dve.wait_ge(pv_done.sem, pv_done.at(k, u - 1))
                    nc.vector.tensor_copy(pT[:, u % 2], bank[5 + u % 2][:]).then_inc(pT_even.sem, 1)

                for u in range(UNITS):
                    yield unit_at(u)
                    dve.wait_ge(s_psum.sem, s_psum.at(k, u + 1))
                    if u >= 3:
                        dve.wait_ge(p_ready.sem, p_ready.at(k, u - 2))
                    alone()
                    for j in range(2):
                        last = nc.vector.tensor_tensor_reduce(sc[:, u % 3, j], bank[3 + u % 2][:, j * S:(j + 1) * S],
                                                              nb[:, u // (H // 2)], 1.0, BIG,
                                                              ALU.add, ALU.min, mneg[:, 2 * u + j:2 * u + j + 1])
                    last.then_inc(s_biased.sem, 1)
                    if u >= 2 and u % 2 == 0:
                        turned_copy(u - 2)
                yield 0.947
                turned_copy(UNITS - 2)
                yield 0.961
                dve.wait_ge(p_ready.sem, p_ready.at(k, UNITS))
                nc.vector.reciprocal(rsum[:], esum[:]).then_inc(rsum_ready.sem, 1)
                yield 0.963
                dve.wait_ge(rsumT_psum.sem, rsumT_psum.at(k, 1))
                nc.vector.tensor_copy(rsumT[:], bank[3][0:H, 0:S]).then_inc(rsumT_ready.sem, 1)
                yield 0.98
                dve.wait_ge(rspread.sem, rspread.at(k, 1))
                dve.wait_ge(oT_ready.sem, oT_ready.at(k, 1))
                nc.vector.tensor_tensor(attnT[:], attnT[:], bank[4][:, 0:S], ALU.mult).then_inc(attnT_ready.sem, 1)
                yield 0.99
                dve.wait_ge(attn_y.sem, attn_y.at(k, 1))
                nc.vector.tensor_tensor(x_e0[:], tiles(bank[3]), x_in[:], ALU.add).then_inc(front_done.sem, 1)

            def opening(l, k, t=None):
                t = l if t is None else t
                j = 2 if l == 0 else 5
                x = x_e0 if l == 0 else x_e1
                yield NORM_AT[t]
                if l == 0:
                    dve.wait_ge(front_done.sem, front_done.at(k, 1))
                else:
                    dve.wait_ge(ctx_taken.sem, ctx_taken.at(k, 1))
                layer_norm(j, x, k)
                yield NORM_AT[t] + 0.02
                normalised(j, x, k)
                if l == 0:
                    dve.wait_ge(xn_ready[2].sem, xn_ready[2].at(k, 1))
                    link(nc.vector.tensor_tensor(x[:], x[:], ne.xn[:], ALU.add))

                def choose():
                    yield CHOICE_AT[t]
                    dve.wait_ge(logits_psum[l].sem, logits_psum[l].at(k, 1))
                    link(nc.vector.tensor_copy(logit[:], bank[2][:, 0:NT * NE].rearrange("p (n e) -> p n e", n=NT)))
                    mine = logit[:].unsqueeze(3).to_broadcast([P, NT, NE, NE])
                    other = logit[:].unsqueeze(2).to_broadcast([P, NT, NE, NE])
                    link(nc.vector.tensor_reduce(top[:], logit[:], AX_X, ALU.max))
                    nc.vector.tensor_tensor(ex[:], logit[:], top[:].unsqueeze(2).to_broadcast([P, NT, NE]), ALU.subtract
                                            ).then_inc(route_in[l].sem, 1)
                    link(nc.vector.tensor_tensor(cmp_eq[:], other, mine, ALU.is_equal))
                    nc.vector.tensor_tensor(cmp_gt[:], other, mine, ALU.is_gt)
                    link(nc.vector.tensor_tensor(cmp_eq[:], cmp_eq[:], lower[:].unsqueeze(1).to_broadcast([P, NT, NE, NE]), ALU.mult))
                    link(nc.vector.tensor_tensor(cmp_gt[:], cmp_gt[:], cmp_eq[:], ALU.add))
                    link(nc.vector.tensor_reduce(cnt[:], cmp_gt[:], AX_X, ALU.add))
                    r = nc.vector.tensor_scalar(sel[:], cnt[:], TOPK - 0.5, None, ALU.is_lt)
                    if l == 0:
                        r.then_inc(sel_ready.sem, 1)
                        dve.wait_ge(sel_ready.sem, sel_ready.at(k, 1))
                    else:
                        link(r)

                def gates():
                    yield GATE_AT[t]
                    dve.wait_ge(route_exp[l].sem, route_exp[l].at(k, 1))
                    link(nc.vector.tensor_tensor(ex[:], ex[:], sel[:], ALU.mult))
                    link(nc.vector.tensor_reduce(top[:], ex[:], AX_X, ALU.add))
                    link(nc.vector.reciprocal(top[:], top[:]))
                    r = nc.vector.tensor_tensor(gate[:], ex[:], top[:].unsqueeze(2).to_broadcast([P, NT, NE]), ALU.mult)
                    if l == 1:
                        r.then_inc(gate_ready.sem, 1)
                    else:
                        link(r)

                def add_bias():
                    yield RANK_AT[t] + 0.01
                    dve.wait_ge(gateT_psum.sem, gateT_psum.at(k, 1))
                    nc.vector.tensor_copy(gateT[:], bank[2][0:NE, 0:S]).then_inc(gateT_ready.sem, 1)
                    yield RANK_AT[t] + BIAS_LAG + 0.005
                    dve.wait_ge(bias_psum.sem, bias_psum.at(k, 1))
                    nc.vector.tensor_tensor(x[:], bank[2][:, S:2 * S].rearrange("p (n d) -> p n d", n=NT), x[:], ALU.add
                                            ).then_inc(bias_added.sem, 1)
                    dve.wait_ge(bias_added.sem, bias_added.at(k, 1))

                def keep():
                    yield RANK_AT[t] + 0.01
                    dve.wait_ge(rank_psum.sem, rank_psum.at(k, 1))
                    ranks = bank[2][:, 0:NT * NE].rearrange("p (n e) -> p n e", n=NT)
                    link(nc.vector.tensor_tensor(cnt[:], ranks, taken[:].unsqueeze(1).to_broadcast([P, NT, NE]), ALU.add))
                    nc.vector.tensor_tensor(taken[:], bank[2][:, NT * NE:(NT + 1) * NE], taken[:], ALU.add).then_inc(rank_read.sem, 1)
                    link(nc.vector.tensor_scalar(cnt[:], cnt[:], CAPACITY - 0.5, 0.5, ALU.is_lt, ALU.mult))
                    link(nc.vector.tensor_tensor(gate[:], gate[:], cnt[:], ALU.mult))

                def silus():
                    for e in range(NE):
                        yield UP_AT[t][e] + 0.004
                        for c2 in range(FC // 2):
                            dve.wait_ge(tanh_ready.sem, tanh_ready.at(k, e * FC // 2 + c2 + 1))
                            h = hid[:, e, 2 * c2:2 * c2 + 2]
                            nc.vector.scalar_tensor_tensor(h, h, 1.0, bank[c2][:].rearrange("p (c t) -> p c t", c=2),
                                                           ALU.add, ALU.mult).then_inc(hid_ready[0].sem, 1)

                adds = add_experts(l, k, t, range(OPEN_DOWNS[t]))
                if l == 0:
                    yield from together(choose(), gates(), keep(), silus(), adds)
                else:
                    yield from together(choose(), gates(), add_bias(), adds)

            def add_experts(l, k, t, experts):
                for e in experts:
                    yield ADD_AT[t][e]
                    add_expert(l, k, e)

            def add_expert(l, k, e):
                x = x_e0 if l == 0 else x_e1
                dve.wait_ge(down_psum[l].sem, down_psum[l].at(k, e + 1))
                if e >= 1:
                    dve.wait_ge(expert_added[l].sem, expert_added[l].at(k, e))
                to = x_mid if l == 0 and e == NE - 1 else x
                for n in range(NT):
                    last = nc.vector.scalar_tensor_tensor(to[:, n], bank[SUM_BANK[e % 2]][:, n * P:(n + 1) * P],
                                                          gate[:, n, e:e + 1], x[:, n], ALU.mult, ALU.add)
                last.then_inc(expert_added[l].sem, 1)

            def closing(l, k, t=None):
                t = l if t is None else t
                yield from add_experts(l, k, t, range(OPEN_DOWNS[t], NE))

            def middle(k):
                yield 0.0
                dve.wait_ge(expert_added[0].sem, expert_added[0].at(k, NE))
                layer_norm(3, x_mid, k)
                yield 0.015
                normalised(3, x_mid, k)
                yield 0.07
                for i in range(2):
                    dve.wait_ge(lin_proj.sem, lin_proj.at(k, i + 1))
                    nc.vector.tensor_scalar(tmin[:, i], bank[3 + i][:, 0:S], 0.0, None, ALU.min).then_inc(elu_in.sem, 1)
                yield 0.09
                for i in range(2):
                    dve.wait_ge(elu_exp.sem, elu_exp.at(k, i + 1))
                    nc.vector.scalar_tensor_tensor(phi[:, i], bank[3 + i][:, 0:S], 0.0, eluv[:, i], ALU.max, ALU.add).then_inc(phi_ready.sem, 1)
                dve.wait_ge(lin_vg.sem, lin_vg.at(k, 2))
                link(nc.vector.tensor_scalar(gT, gT, 0.5, 0.5, ALU.mult, ALU.add))
                for i in range(HD // 2):
                    yield lin_at(i)
                    dve.wait_ge(kb_psum.sem, kb_psum.at(k, i + 1))
                    nc.vector.tensor_tensor(kv[:, i % 2], bank[3 + i % 2][:].rearrange("p (r t) -> p r t", r=2),
                                            vT.unsqueeze(1).to_broadcast([P, 2, S]), ALU.mult).then_inc(kv_ready.sem, 1)
                    dve.wait_ge(kv_ready.sem, kv_ready.at(k, i + 1))
                    for r in range(2):
                        last = nc.vector.tensor_tensor_scan(st[:, i % 2, r], gT, kv[:, i % 2, r], 0.0, ALU.mult, ALU.add)
                    link(last)
                    dve.wait_ge(qb_psum.sem, qb_psum.at(k, i + 1))
                    if i >= 2:
                        dve.wait_ge(lin_fold.sem, lin_fold.at(k, i - 1))
                    nc.vector.tensor_tensor(qs[:, i % 2], bank[5 + i % 2][:].rearrange("p (r t) -> p r t", r=2), st[:, i % 2],
                                            ALU.mult).then_inc(qs_ready.sem, 1)
                yield 0.42
                dve.wait_ge(lin_fold.sem, lin_fold.at(k, HD // 2))
                link(nc.vector.tensor_tensor(x_lin[:], tiles(bank[7]), x_mid[:], ALU.add))

                layer_norm(4, x_lin, k)
                yield 0.445
                normalised(4, x_lin, k)
                yield 0.50
                dve.wait_ge(gates_psum.sem, gates_psum.at(k, 1))
                link(nc.vector.tensor_scalar(fsum, bank[3][32:32 + MH, 0:S], gbias[32:32 + MH, 0:1], None, ALU.add))
                nc.vector.scalar_tensor_tensor(fabs, fsum, -1.0, fsum, ALU.mult, ALU.max).then_inc(fabs_ready.sem, 1)
                nc.vector.tensor_scalar(fmin, fsum, 0.0, None, ALU.min)
                link(nc.vector.tensor_scalar(ig, bank[3][0:MH, 0:S], gbias[0:MH, 0:1], None, ALU.add))
                yield 0.512
                dve.wait_ge(fln_ready.sem, fln_ready.at(k, 1))
                link(nc.vector.tensor_tensor_scan(fcum, fmin, fln, 0.0, ALU.add, ALU.subtract))
                link(nc.vector.tensor_tensor(u36[0:MH, :], ig, fcum, ALU.subtract))
                link(nc.vector.tensor_tensor_scan(umax, u36[0:MH, :], u36[0:MH, :], -BIG, ALU.max, ALU.max))
                nc.vector.tensor_scalar(mrow, umax, -1.0, None, ALU.mult)
                nc.vector.tensor_tensor(u36[32:32 + MH, :], fcum, umax, ALU.add).then_inc(m_ready.sem, 1)
                yield 0.545
                dve.wait_ge(uT_psum.sem, uT_psum.at(k, 1))
                nc.vector.tensor_copy(uT[:], bank[7][:, 0:NT * 36].rearrange("p (n g) -> p n g", n=NT)).then_inc(uT_ready.sem, 1)
                for h in range(MH):
                    yield head_at(h)
                    dve.wait_ge(qk_psum.sem, qk_psum.at(k, h + 1))
                    dve.wait_ge(decay_cut.sem, decay_cut.at(k, h + 1))
                    if h >= 2:
                        dve.wait_ge(h_psum.sem, h_psum.at(k, h - 1))
                    nc.vector.scalar_tensor_tensor(cT[:, h % 2], bank[3 + h % 2][:, 0:3 * P].rearrange("p (b t) -> p b t", b=3), MD ** -0.5,
                                                   decay[:, h % 2], ALU.mult, ALU.mult).then_inc(c_ready.sem, 1)

            def tail(k):
                yield TAIL_AT[0]
                dve.wait_ge(h_psum.sem, h_psum.at(k, MH))
                dve.wait_ge(efm_ready.sem, efm_ready.at(k, 1))
                NG = NT * MH
                hb = bank[7][:, 0:NG * (MD + 1)].rearrange("p (g d) -> p g d", d=MD + 1)
                nrm_g = nrm[:].rearrange("p n h -> p (n h)")
                rn_g = rn[:].rearrange("p n h -> p (n h)")

                def per_head(v):
                    return v.unsqueeze(2).to_broadcast([P, NG, MD])

                link(nc.vector.tensor_copy(nrm_g, hb[:, :, MD]))
                link(nc.vector.scalar_tensor_tensor(nrm[:], nrm[:], -1.0, nrm[:], ALU.mult, ALU.max))
                link(nc.vector.tensor_tensor(nrm[:], nrm[:], efm[:], ALU.max))
                link(nc.vector.tensor_scalar(nrm[:], nrm[:], 1e-6, None, ALU.add))
                link(nc.vector.reciprocal(rn[:], nrm[:]))
                link(nc.vector.tensor_tensor(hh, hb[:, :, 0:MD], per_head(rn_g), ALU.mult))
                link(nc.vector.tensor_reduce(mstat[:, 0], hh, AX_X, ALU.add))
                link(nc.vector.tensor_scalar(mstat[:, 0], mstat[:, 0], 1.0 / MD, None, ALU.mult))
                link(nc.vector.tensor_tensor(hc, hh, per_head(mstat[:, 0]), ALU.subtract))
                link(nc.vector.tensor_tensor(hsq, hc, hc, ALU.mult))
                link(nc.vector.tensor_reduce(mstat[:, 1], hsq, AX_X, ALU.add))
                nc.vector.tensor_scalar(mstat[:, 2], mstat[:, 1], 1.0 / MD, 1e-6, ALU.mult, ALU.add).then_inc(hvar_ready.sem, 1)
                yield TAIL_AT[1]
                dve.wait_ge(hrstd_ready.sem, hrstd_ready.at(k, 1))
                link(nc.vector.tensor_tensor(hn, hc, per_head(mstat[:, 3]), ALU.mult))
                hn_t = hn.rearrange("p (n h) d -> p n (h d)", n=NT)
                link(nc.vector.tensor_tensor(hn_t, hn_t, onw[:].unsqueeze(1).to_broadcast([P, NT, D]), ALU.mult))
                dve.wait_ge(x_stored.sem, x_stored.at(k, 0))
                nc.vector.tensor_tensor(x_e1[:], hn_t, x_lin[:], ALU.add).then_inc(ctx_taken.sem, 1)

            side_by_side(front(0))
            later_setup()
            side_by_side(front(1), opening(0, 0, 3))
            side_by_side(middle(0), opening(0, 1))
            first = Chain.here
            with dve.Fori(0, B - 2) as k:
                Chain.before, Chain.here = k * LOOP_LINKS + first, 0
                side_by_side(front(k + 2), tail(k), one_by_one(closing(0, k + 1), opening(1, k)))
                side_by_side(middle(k + 1), one_by_one(closing(1, k), opening(0, k + 2)))
                assert Chain.here == LOOP_LINKS, f"LOOP_LINKS is {Chain.here}"
            Chain.before, Chain.here = first + (B - 2) * LOOP_LINKS, 0
            side_by_side(tail(B - 2), closing(0, B - 1))
            side_by_side(middle(B - 1), within(opening(1, B - 2, 2), -0.1, 0.85))
            side_by_side(one_by_one(tail(B - 1), opening(1, B - 1, 2)))


def _layout(inp):
    def put(v):
        return np.ascontiguousarray(v)

    i = {k: np.asarray(v) for k, v in inp.items()}

    def tokens(v):
        return put(v.reshape(B, NT, P, v.shape[-1]).transpose(0, 2, 1, 3))

    def by_feature(v):
        return v.reshape(H, HD, -1).swapaxes(0, 1).reshape(v.shape)

    eye = np.eye(P, dtype=np.float32)
    pick = np.zeros((H, HD, HD, H, HD), np.float32)
    for h in range(H):
        for k in range(HD):
            pick[h, k, k, h, :] = 1
    of_head = np.repeat(np.eye(H, dtype=np.float32), HD, axis=1)
    row = np.zeros((MH, MH, P), np.float32)
    for h in range(MH):
        row[h, h] = 1
    r = {
        "x": tokens(i["x"]),
        "dist": tokens(i["fside_BxSxS2_0"]),
        "ctx": tokens(i["ctx_1024"]),
        "ctxT": put(i["ctx_1024"].transpose(0, 2, 1)),
        "ident": eye,
        "earlier": np.triu(np.ones((P, P), np.float32), 1),
        "ones": np.ones((P, P), np.float32),
        "lower": put(np.broadcast_to(np.tril(np.ones((NE, NE), np.float32), -1), (P, NE, NE))),
        "pick": pick.reshape(P, HD, P),
        "row": row,
        "of_head": of_head,
        "w_rnn": put(i["L0_attn_W"].T),
        "b_rnn": put(i["L0_attn_b"].reshape(3 * EH, P).T),
        "wd_rnn": put(i["L0_attn_Wd"].T.reshape(E0 // P, P, D).transpose(1, 0, 2)),
        "w_x": put(np.stack([(by_feature(i[f"L0_xattn_W{k}"]) if k in "qk" else i[f"L0_xattn_W{k}"]).T for k in "qkvo"], 1)),
        "b_xqk": put(np.stack([by_feature(i["L0_xattn_bq"]), by_feature(i["L0_xattn_bk"])], 1)),
        "bv": i["L0_xattn_bv"], "bo": i["L0_xattn_bo"],
        "dscale": i["L0_xattn_distance_scaling"].reshape(1),
        "w_l": put(np.stack([i[f"L1_attn_W{k}"].T for k in "qkvo"], 1)),
        "wg_l": put(i["L1_attn_Wg"].T),
        "bg_l": put(np.broadcast_to(i["L1_attn_bg"].reshape(H, 1), (H, HD)).reshape(P, 1)),
        "w_route": put(np.stack([i["L0_ffn_router_w"].T, i["L1_ffn_Wg"].T], 1)),
        "w_up": put(np.stack([i["L0_ffn_w1"], i["L1_ffn_W1"]])),
        "w_down": put(np.stack([i["L0_ffn_w2"], i["L1_ffn_W2"]])),
        "b_up": put(i["L1_ffn_b1"].reshape(NE * FC, P).T),
        "b_down": i["L1_ffn_b2"],
        "gk_raw": put(np.concatenate([i["L1_xattn_ig_kernel"].reshape(3, P, MH),
                                      i["L1_xattn_fg_kernel"].reshape(3, P, MH)], 2).transpose(1, 0, 2)),
        "gate_bias": put(np.stack([i["L1_xattn_ig_bias"], i["L1_xattn_fg_bias"]]).reshape(2, MH, 1)),
        "onw": put(i["L1_xattn_outnorm_weight"].reshape(D)),
    }
    return r


def kernel(**inputs):
    import concourse.bacc as _bacc
    from concourse.bass_utils import run_bass_kernel_spmd as _run

    nc = _bacc.Bacc("TRN2", target_bir_lowering=False, num_devices=1)
    arrays = {f"in_{k}": v for k, v in _layout(inputs).items()}
    aps = {k[3:]: nc.dram_tensor(k, v.shape, mybir.dt.from_np(v.dtype), kind="ExternalInput").ap()
           for k, v in arrays.items()}
    out = nc.dram_tensor("out_x", (B, P, NT, D), F32, kind="ExternalOutput").ap()
    decoder(nc, aps, out)
    r = _run(nc, [arrays], core_ids=[0])
    got = r.results[0]["out_x"]
    return np.ascontiguousarray(got.transpose(0, 2, 1, 3)).reshape(B, S, D)
```
